# Optimizing a Trainium2 kernel written in Bass

```python
import numpy as np
import jax
import jax.numpy as jnp

def _softmax(x, axis=-1):
    return jax.nn.softmax(x, axis=axis)

def _gelu(x):
    return jax.nn.gelu(x, approximate=True)

def _silu(x):
    return jax.nn.silu(x)

def _sigmoid(x):
    return jax.nn.sigmoid(x)

def _layernorm(x, axis=-1, eps=1e-05):
    m = jnp.mean(x, axis=axis, keepdims=True)
    v = jnp.var(x, axis=axis, keepdims=True)
    return (x - m) / jnp.sqrt(v + eps)

def _scatter_add(tgt, idx, src, axis=0):
    return tgt.at[idx].add(src)

def _segment_sum(src, seg, n):
    return jax.ops.segment_sum(src, seg, n)
kernel_name = 'mk_vit_tower_d2_tok_img1024_r4_205bd2'

def setup_inputs(seed: int=0):
    np.random.seed(seed)
    _w = jnp.asarray

    def _rec_inputs():
        import jax
        import jax.numpy as jnp
        _rk = jax.random.key(seed)
        x = -0.00016672 + 0.999947 * jax.random.normal(jax.random.fold_in(_rk, 1), (16, 3, 96, 96), jnp.float32)
        return x
    x = _rec_inputs()

    def _L0_tok_setup():
        import jax, jax.numpy as jnp
        import numpy as np
        B, C, H, W = (64, 3, 96, 96)
        P = 16
        HP, WP = (H // P, W // P)
        N = HP * WP
        F = C * P * P
        D = 256
        key = jax.random.key(seed)
        k1, k2, k3, k4, k5 = jax.random.split(key, 5)
        data = jax.random.normal(k1, (B, C, H, W), dtype=jnp.float32)
        lim = 1.0 / np.sqrt(F)
        W_lin = jax.random.uniform(k2, (D, F), minval=-lim, maxval=lim, dtype=jnp.float32)
        b_lin = jax.random.uniform(k3, (D,), minval=-lim, maxval=lim, dtype=jnp.float32)
        class_token = jax.random.normal(k4, (1, 1, D), dtype=jnp.float32)
        position_embeddings = jax.random.normal(k5, (1, N + 1, D), dtype=jnp.float32)
        return {'data': data, 'W_lin': W_lin, 'b_lin': b_lin, 'class_token': class_token, 'position_embeddings': position_embeddings}
    _L0_tok_all = _L0_tok_setup()
    _L0_tok_in = {k: v for k, v in _L0_tok_all.items() if k in ('W_lin', 'b_lin', 'class_token', 'position_embeddings')}
    del _L0_tok_all

    def _L0_attn_setup():
        import jax, jax.numpy as jnp
        import numpy as np
        B, S, DIM, NH = (2, 512, 256, 16)
        HD = DIM // NH
        ROPE_THETA = 10000.0

        def _rope_cos_sin(seq_len, head_dim, dtype):
            inv_freq = 1.0 / ROPE_THETA ** (jnp.arange(0, head_dim, 2, dtype=jnp.float32) / head_dim)
            t = jnp.arange(seq_len, dtype=jnp.float32)
            freqs = jnp.einsum('s,d->sd', t, inv_freq)
            emb = jnp.concatenate([freqs, freqs], axis=-1)
            return (jnp.cos(emb).astype(dtype), jnp.sin(emb).astype(dtype))

        def _rotate_half(x):
            h = x.shape[-1] // 2
            return jnp.concatenate([-x[..., h:], x[..., :h]], axis=-1)
        key = jax.random.key(seed)
        kx, kq, kk, kv, ko = jax.random.split(key, 5)
        w_scale = 0.02
        return {'x': jax.random.normal(kx, (B, S, DIM), jnp.float32), 'Wq': jax.random.normal(kq, (DIM, DIM), jnp.float32) * w_scale, 'Wk': jax.random.normal(kk, (DIM, DIM), jnp.float32) * w_scale, 'Wv': jax.random.normal(kv, (DIM, DIM), jnp.float32) * w_scale, 'Wo': jax.random.normal(ko, (DIM, DIM), jnp.float32) * w_scale}
    _L0_attn_all = _L0_attn_setup()
    _L0_attn_in = {k: v for k, v in _L0_attn_all.items() if k in ('Wq', 'Wk', 'Wv', 'Wo')}
    del _L0_attn_all

    def _L0_ffn_setup():
        import jax, jax.numpy as jnp
        import numpy as np
        B, N, D = (4, 512, 256)
        SPARSITY = 0.01
        key = jax.random.key(seed)
        k1, k2, k3 = jax.random.split(key, 3)
        x = jax.random.normal(k1, (B, N, D), dtype=jnp.float32)
        spatial = jax.random.normal(k2, (D, D), dtype=jnp.float32) * 0.02
        freq = jnp.fft.fft(spatial, axis=-1)
        k = int(D * SPARSITY)
        mag = jnp.abs(freq)
        kth = jax.lax.top_k(mag, k)[0][:, -1:]
        w_sparse = jnp.where(mag >= kth, freq, 0.0 + 0j)
        bias = jax.random.normal(k3, (D,), dtype=jnp.float32) * 0.01
        return {'x': x, 'w_freq_real': jnp.real(w_sparse).astype(jnp.float32), 'w_freq_imag': jnp.imag(w_sparse).astype(jnp.float32), 'bias': bias}
    _L0_ffn_all = _L0_ffn_setup()
    _L0_ffn_in = {k: v for k, v in _L0_ffn_all.items() if k in ('w_freq_real', 'w_freq_imag', 'bias')}
    del _L0_ffn_all

    def _L1_attn_setup():
        import jax, jax.numpy as jnp
        import numpy as np
        B, L, H, I, K, G = (2, 1024, 256, 512, 4, 8)
        EPS = 1e-05

        def _layernorm(x, g, b):
            m = x.mean(-1, keepdims=True)
            v = jnp.var(x, axis=-1, keepdims=True)
            return (x - m) * jax.lax.rsqrt(v + EPS) * g + b
        key = jax.random.key(seed)
        ks = jax.random.split(key, 8)
        s = 0.02
        return {'hidden_states': jax.random.normal(ks[0], (B, L, H), jnp.float32), 'in_proj_w': jax.random.normal(ks[1], (2 * I, H), jnp.float32) * s, 'conv_w': jax.random.normal(ks[2], (I, I // G, K), jnp.float32) * s, 'conv_b': jax.random.normal(ks[3], (I,), jnp.float32) * s, 'ln_g': jnp.ones((I,), jnp.float32), 'ln_b': jnp.zeros((I,), jnp.float32), 'fc_w': jax.random.normal(ks[4], (H, I), jnp.float32) * s, 'fc_b': jnp.zeros((H,), jnp.float32), 'cproj_w': jax.random.normal(ks[5], (I, H), jnp.float32) * s, 'cproj_b': jnp.zeros((I,), jnp.float32), 'out_w': jax.random.normal(ks[6], (H, I), jnp.float32) * s}
    _L1_attn_all = _L1_attn_setup()
    _L1_attn_in = {k: v for k, v in _L1_attn_all.items() if k in ('in_proj_w', 'conv_w', 'conv_b', 'ln_g', 'ln_b', 'fc_w', 'fc_b', 'cproj_w', 'cproj_b', 'out_w')}
    del _L1_attn_all

    def _L1_ffn_setup():
        import jax, jax.numpy as jnp
        import numpy as np
        D_MODEL = 256
        D_HIDDEN = 1024
        NUM_BANKS = 16
        NUM_SELECTED = 2
        key = jax.random.key(seed)
        ks = jax.random.split(key, 7)
        s = 0.02
        return {'tensor': jax.random.normal(ks[0], (4, 256, D_MODEL), dtype=jnp.float32), 'Wr': jax.random.normal(ks[1], (D_MODEL, NUM_BANKS), dtype=jnp.float32) * s, 'br': jnp.zeros((NUM_BANKS,), dtype=jnp.float32), 'W1': jax.random.normal(ks[2], (NUM_BANKS, D_MODEL, D_HIDDEN), dtype=jnp.float32) * s, 'b1': jnp.zeros((NUM_BANKS, D_HIDDEN), dtype=jnp.float32), 'W2': jax.random.normal(ks[3], (NUM_BANKS, D_HIDDEN, D_MODEL), dtype=jnp.float32) * s, 'b2': jnp.zeros((NUM_BANKS, D_MODEL), dtype=jnp.float32)}
    _L1_ffn_all = _L1_ffn_setup()
    _L1_ffn_in = {k: v for k, v in _L1_ffn_all.items() if k in ('Wr', 'br', 'W1', 'b1', 'W2', 'b2')}
    del _L1_ffn_all
    return {'x': x, 'L0_tok_W_lin': _L0_tok_in['W_lin'], 'L0_tok_b_lin': _L0_tok_in['b_lin'], 'L0_tok_class_token': _L0_tok_in['class_token'], 'L0_tok_position_embeddings': _L0_tok_in['position_embeddings'], 'L0_attn_Wq': _L0_attn_in['Wq'], 'L0_attn_Wk': _L0_attn_in['Wk'], 'L0_attn_Wv': _L0_attn_in['Wv'], 'L0_attn_Wo': _L0_attn_in['Wo'], 'L0_ffn_w_freq_real': _L0_ffn_in['w_freq_real'], 'L0_ffn_w_freq_imag': _L0_ffn_in['w_freq_imag'], 'L0_ffn_bias': _L0_ffn_in['bias'], 'L1_attn_in_proj_w': _L1_attn_in['in_proj_w'], 'L1_attn_conv_w': _L1_attn_in['conv_w'], 'L1_attn_conv_b': _L1_attn_in['conv_b'], 'L1_attn_ln_g': _L1_attn_in['ln_g'], 'L1_attn_ln_b': _L1_attn_in['ln_b'], 'L1_attn_fc_w': _L1_attn_in['fc_w'], 'L1_attn_fc_b': _L1_attn_in['fc_b'], 'L1_attn_cproj_w': _L1_attn_in['cproj_w'], 'L1_attn_cproj_b': _L1_attn_in['cproj_b'], 'L1_attn_out_w': _L1_attn_in['out_w'], 'L1_ffn_Wr': _L1_ffn_in['Wr'], 'L1_ffn_br': _L1_ffn_in['br'], 'L1_ffn_W1': _L1_ffn_in['W1'], 'L1_ffn_b1': _L1_ffn_in['b1'], 'L1_ffn_W2': _L1_ffn_in['W2'], 'L1_ffn_b2': _L1_ffn_in['b2']}

def reference(x, L0_tok_W_lin, L0_tok_b_lin, L0_tok_class_token, L0_tok_position_embeddings, L0_attn_Wq, L0_attn_Wk, L0_attn_Wv, L0_attn_Wo, L0_ffn_w_freq_real, L0_ffn_w_freq_imag, L0_ffn_bias, L1_attn_in_proj_w, L1_attn_conv_w, L1_attn_conv_b, L1_attn_ln_g, L1_attn_ln_b, L1_attn_fc_w, L1_attn_fc_b, L1_attn_cproj_w, L1_attn_cproj_b, L1_attn_out_w, L1_ffn_Wr, L1_ffn_br, L1_ffn_W1, L1_ffn_b1, L1_ffn_W2, L1_ffn_b2):
    import jax
    import jax.numpy as jnp

    def _L0_tok_ref(data, W_lin, b_lin, class_token, position_embeddings):
        import jax, jax.numpy as jnp
        import numpy as np
        B, C, H, W = (64, 3, 96, 96)
        P = 16
        HP, WP = (H // P, W // P)
        N = HP * WP
        F = C * P * P
        D = 256
        b = data.shape[0]
        x = data.reshape(b, C, HP, P, WP, P)
        x = x.transpose(0, 2, 4, 1, 3, 5).reshape(b, N, F)
        x = jnp.einsum('bnf,df->bnd', x, W_lin) + b_lin
        cls = jnp.broadcast_to(class_token, (b, 1, D))
        out = jnp.concatenate([cls, x], axis=1) + position_embeddings
        return out

    def _L0_attn_ref(x, Wq, Wk, Wv, Wo):
        import jax, jax.numpy as jnp
        import numpy as np
        B, S, DIM, NH = (2, 512, 256, 16)
        HD = DIM // NH
        ROPE_THETA = 10000.0

        def _rope_cos_sin(seq_len, head_dim, dtype):
            inv_freq = 1.0 / ROPE_THETA ** (jnp.arange(0, head_dim, 2, dtype=jnp.float32) / head_dim)
            t = jnp.arange(seq_len, dtype=jnp.float32)
            freqs = jnp.einsum('s,d->sd', t, inv_freq)
            emb = jnp.concatenate([freqs, freqs], axis=-1)
            return (jnp.cos(emb).astype(dtype), jnp.sin(emb).astype(dtype))

        def _rotate_half(x):
            h = x.shape[-1] // 2
            return jnp.concatenate([-x[..., h:], x[..., :h]], axis=-1)
        Bb, Ss, D = x.shape
        nh, hd = (NH, D // NH)
        scale = hd ** (-0.5)

        def proj(W):
            return (x @ W.T).reshape(Bb, Ss, nh, hd).transpose(0, 2, 1, 3)
        q, k, v = (proj(Wq), proj(Wk), proj(Wv))
        cos, sin = _rope_cos_sin(Ss, hd, x.dtype)
        cos, sin = (cos[None, None], sin[None, None])
        q = q * cos + _rotate_half(q) * sin
        k = k * cos + _rotate_half(k) * sin
        scores = jnp.einsum('bhqd,bhkd->bhqk', q, k) * scale
        causal = jnp.triu(jnp.ones((Ss, Ss), dtype=bool), k=1)
        scores = jnp.where(causal[None, None], -jnp.inf, scores)
        attn = jax.nn.softmax(scores.astype(jnp.float32), axis=-1).astype(x.dtype)
        out = jnp.einsum('bhqk,bhkd->bhqd', attn, v)
        out = out.transpose(0, 2, 1, 3).reshape(Bb, Ss, D)
        return out @ Wo.T

    def _L0_ffn_ref(x, w_freq_real, w_freq_imag, bias):
        import jax, jax.numpy as jnp
        import numpy as np
        B, N, D = (4, 512, 256)
        SPARSITY = 0.01
        w = jax.lax.complex(w_freq_real, w_freq_imag)
        x_freq = jnp.fft.fft(x, axis=-1)
        y_freq = jnp.einsum('bnd,do->bno', x_freq, w)
        y = jnp.real(jnp.fft.ifft(y_freq, axis=-1))
        return y + bias

    def _L1_attn_ref(hidden_states, in_proj_w, conv_w, conv_b, ln_g, ln_b, fc_w, fc_b, cproj_w, cproj_b, out_w):
        import jax, jax.numpy as jnp
        import numpy as np
        B, L, H, I, K, G = (2, 1024, 256, 512, 4, 8)
        EPS = 1e-05

        def _layernorm(x, g, b):
            m = x.mean(-1, keepdims=True)
            v = jnp.var(x, axis=-1, keepdims=True)
            return (x - m) * jax.lax.rsqrt(v + EPS) * g + b
        p = hidden_states @ in_proj_w.T
        h, gate = (p[..., :I], p[..., I:])
        gate = jax.nn.silu(gate)
        hc = jnp.transpose(h, (0, 2, 1))
        conv = jax.lax.conv_general_dilated(hc, conv_w, window_strides=(1,), padding=[(K - 1, 0)], feature_group_count=G, dimension_numbers=('NCH', 'OIH', 'NCH'))
        conv = conv + conv_b[None, :, None]
        h = jnp.transpose(conv, (0, 2, 1)) * gate
        residual = h
        hn = _layernorm(h, ln_g, ln_b)
        m = jax.nn.silu(hn @ fc_w.T + fc_b) @ cproj_w.T + cproj_b
        h = m + residual
        return h @ out_w.T

    def _L1_ffn_ref(tensor, Wr, br, W1, b1, W2, b2):
        import jax, jax.numpy as jnp
        import numpy as np
        D_MODEL = 256
        D_HIDDEN = 1024
        NUM_BANKS = 16
        NUM_SELECTED = 2
        logits = jnp.einsum('bsd,de->bse', tensor, Wr) + br
        probs = jax.nn.softmax(logits, axis=-1)
        topv, topi = jax.lax.top_k(probs, NUM_SELECTED)
        gate = jnp.sum(jax.nn.one_hot(topi, NUM_BANKS, dtype=tensor.dtype) * topv[..., None], axis=-2)
        h = jax.nn.relu(jnp.einsum('bsd,edh->bseh', tensor, W1) + b1)
        y = jnp.einsum('bseh,ehm->bsem', h, W2) + b2
        out = jnp.einsum('bse,bsem->bsm', gate, y)
        return out
    h = _L0_tok_ref(x, L0_tok_W_lin, L0_tok_b_lin, L0_tok_class_token, L0_tok_position_embeddings)
    h = h + _L0_attn_ref(_layernorm(h, axis=-1), L0_attn_Wq, L0_attn_Wk, L0_attn_Wv, L0_attn_Wo)
    h = h + _L0_ffn_ref(_layernorm(h, axis=-1), L0_ffn_w_freq_real, L0_ffn_w_freq_imag, L0_ffn_bias)
    h = h + _L1_attn_ref(_layernorm(h, axis=-1), L1_attn_in_proj_w, L1_attn_conv_w, L1_attn_conv_b, L1_attn_ln_g, L1_attn_ln_b, L1_attn_fc_w, L1_attn_fc_b, L1_attn_cproj_w, L1_attn_cproj_b, L1_attn_out_w)
    h = h + _L1_ffn_ref(_layernorm(h, axis=-1), L1_ffn_Wr, L1_ffn_br, L1_ffn_W1, L1_ffn_b1, L1_ffn_W2, L1_ffn_b2)
    return h

_drawn_inputs = setup_inputs


def setup_inputs(seed=0):
    import zlib

    import numpy as np

    out = dict(_drawn_inputs(seed))
    spreads = {'L1_attn_ln_g': (1.0, 0.6),
     'L1_attn_ln_b': (0.0, 0.8),
     'L1_attn_fc_b': (0.0, 0.8),
     'L1_attn_cproj_b': (0.0, 0.27),
     'L1_ffn_br': (0.0, 0.757),
     'L1_ffn_b1': (0.0, 0.8),
     'L1_ffn_b2': (0.0, 0.789)}
    factors = {'L0_tok_b_lin': 3.079,
     'L0_attn_Wq': 8.0,
     'L0_attn_Wk': 8.0,
     'L0_ffn_bias': 7.513,
     'L1_attn_conv_b': 8.0,
     'L1_ffn_Wr': 3.273,
     'L1_ffn_W1': 4.559,
     'L1_ffn_W2': 3.631}
    for name, (base, spread) in spreads.items():
        noise = np.random.default_rng([zlib.crc32(name.encode()), seed]).standard_normal(out[name].shape)
        drawn = base * np.exp(spread * noise) if base else spread * noise
        out[name] = jnp.asarray(drawn.astype(out[name].dtype))
    for name, factor in factors.items():
        out[name] = (out[name] * factor).astype(out[name].dtype)
    return out
```

```python
import numpy as np
import concourse.bass as bass
from concourse import mybir
from contextlib import ExitStack

F32 = mybir.dt.float32
BF16 = mybir.dt.bfloat16
I32 = mybir.dt.int32
ALU = mybir.AluOpType
ACT = mybir.ActivationFunctionType
AX = mybir.AxisListType

P = 128
IMAGES = 16
SEQ = 37
TOKENS = IMAGES * SEQ
HALF = TOKENS // 2
D = 256
DB = D // P
PATCH = 768
PB = PATCH // P
HEADS = 16
HD = D // HEADS
INNER = 512
IB = INNER // P
TAPS = 4
PADSEQ = SEQ + TAPS - 1
EPS = 1e-5

EXPERTS = 16
HIDDEN = 1024
HB = HIDDEN // P
PAIRS = 2 * TOKENS
OVERFLOW = (PAIRS - EXPERTS) // P
TILES = EXPERTS + OVERFLOW
SLOTS = TILES * P
ROWS = [P, P, P, P, TOKENS - 4 * P]
RT = len(ROWS)
WCOLS = DB * HIDDEN + HB * D + HB
RING = 4

ATT = [(h * HALF + o, n) for h in range(2) for o, n in ((0, 111), (111, 111), (222, 74))]
UNITS = [(t, b) for t in range(len(ATT)) for b in range(4)]
AW = 111

CONST = {}


def _columns():
    at = 0
    for name, n in (("cos", SEQ), ("sin", SEQ), ("headmask", 2), ("ident", P), ("means", P), ("ones", P),
                    ("tri", P), ("attmask", AW), ("tri16", 2 * EXPERTS), ("iota16", EXPERTS),
                    ("expert_base", EXPERTS), ("valid", RT), ("tile_iota", OVERFLOW * EXPERTS)):
        CONST[name] = (at, n)
        at += n
    return at


NCONST = _columns()

VEC = {}


def _vcolumns():
    at = 0
    for name, n in (("ffn_bias", DB), ("conv_b", IB), ("ln_g", IB), ("ln_b", IB), ("fc_b", DB),
                    ("cproj_b", IB)):
        VEC[name] = (at, n)
        at += n
    return at


NVEC = _vcolumns()

def _jobs():
    v, a = [], []
    v += [("spec_a", part, j) for part in range(2) for j in range(DB)]
    v += [("spec_m", d) for d in range(DB)]
    a += [("tok", h, m) for h in range(2) for m in range(DB)]

    def norm(n):
        a.extend([("var", n, 0), ("var", n, 1)])
        return [("mean", n, 0), ("mean", n, 1)]
    v += norm(0)
    v += [(x, h, m, r) for h in range(2) for m in range(DB) for x in ("q", "k") for r in range(2)]
    a += [("v", t) for t in range(len(ATT))]
    for u in range(len(UNITS) + 4):
        if u < len(UNITS):
            v.append(("score", u))
        if 0 <= u - 2 < len(UNITS):
            a.append(("pt", u - 2))
        if u >= 4 and (u - 4) % 4 == 3:
            a.append(("ot", (u - 4) // 4))
    v += [("wo", h, m) for h in range(2) for m in range(DB)]
    v += norm(1)
    v += [("ffn", h, m) for h in range(2) for m in range(DB)]
    v += norm(2)
    v += [("inh", h, m) for h in range(2) for m in range(IB)]
    a += [("gate", h, m) for h in range(2) for m in range(IB)]
    v += [("conv", h, m) for h in range(2) for m in range(IB)]
    v += norm(3)
    a += [("fc", h, m) for h in range(2) for m in range(DB)]
    v += [("cproj", h, m) for h in range(2) for m in range(IB)]
    v += [("out", h, m) for h in range(2) for m in range(DB)]
    v += norm(4)
    v += [("logits",), ("pos",), ("offset",), ("gt", 0), ("gt", 1)]
    v += [("b2", t) for t in range(RT)]
    a += [("xrow", t) for t in range(RT)] + [("hrow", t) for t in range(RT)]
    return v, a


VJOBS, AJOBS = _jobs()
VNUM = {k: n for n, k in enumerate(VJOBS)}
ANUM = {k: n for n, k in enumerate(AJOBS)}
VBANKS = ABANKS = 3


def vit_tower_kernel(nc, patches, spec_w, spec_c, tok_w, tok_add, tok_sel, attn_w, consts, vecs,
                     inproj_w, conv_w, fc_w, cproj_w, out_w, router_w, router_b, experts, b2,
                     out):
    ctx = ExitStack()
    with ctx:
        def sb(name, shape, dt=F32):
            return ctx.enter_context(nc.sbuf_tensor(name, shape, dt))

        def sem(name):
            return ctx.enter_context(nc.semaphore(name))

        slot_x = nc.dram_tensor("slot_x", [SLOTS, D], F32).ap()
        slot_y = nc.dram_tensor("slot_y", [SLOTS, D], F32).ap()

        cst = sb("cst", [P, NCONST])
        vec = sb("vec", [P, NVEC])
        spec = sb("spec", [P, 5 * DB * D])
        specw = spec[:, 0:2 * DB * D].rearrange("p (x k n) -> p x k n", x=2, k=DB)
        specc = spec[:, 2 * DB * D:].rearrange("p (x k n) -> p x k n", x=3, k=DB)
        tokw = sb("tokw", [P, PB, D])
        tokadd = sb("tokadd", [SEQ + 2, D])
        toksel = sb("toksel", [SEQ + 2, HALF])
        attnm = sb("attnm", [P, 6 * DB * D])
        attnw = attnm[:, :].rearrange("p (x k n) -> p x k n", x=6, k=DB)
        inw = sb("inw", [P, DB, 2 * INNER])
        convw = sb("convw", [P, IB, TAPS, P])
        fcw = sb("fcw", [P, IB, D])
        cprojw = sb("cprojw", [P, DB, INNER])
        outw = sb("outw", [P, IB, D])
        routerw = sb("routerw", [P, DB, EXPERTS])
        routerb = sb("routerb", [1, EXPERTS])
        b2s = sb("b2s", [EXPERTS, D])
        wexp = sb("wexp", [P, RING, WCOLS])

        patchm = sb("patchm", [P, PB * TOKENS])
        xpatch = patchm[:, :].rearrange("p (k n) -> p k n", k=PB)
        sc = patchm[0:AW, 0:3 * 4 * AW].rearrange("p (x n) -> p x n", x=3)
        pr = patchm[0:AW, 12 * AW:20 * AW].rearrange("p (x n) -> p x n", x=2)
        prT = patchm[0:AW, 20 * AW:28 * AW].rearrange("p (x n) -> p x n", x=2)
        res = patchm[:, 0:IB * TOKENS].rearrange("p (k n) -> p k n", k=IB)
        base = patchm[:, 0:RT * D].rearrange("p (t c) -> p t c", t=RT)
        xrow = patchm[:, RT * D:2 * RT * D].rearrange("p (t c) -> p t c", t=RT)
        vaug = spec[0:AW, 0:len(ATT) * HEADS * (HD + 1)].rearrange("p (t a d) -> p t a d", t=len(ATT), a=HEADS)
        gate = spec[:, 0:IB * TOKENS].rearrange("p (k n) -> p k n", k=IB)
        hn = gate
        got = spec[:, 0:RT * D].rearrange("p (t c) -> p t c", t=RT)
        got2 = spec[:, RT * D:2 * RT * D].rearrange("p (t c) -> p t c", t=RT)
        keym = sb("keym", [P, 2 * IB * HALF])
        sq = keym[:, :].rearrange("p (h k n) -> p h k n", h=2, k=IB)
        kT = keym[:, :].rearrange("p (k e n) -> p k e n", k=DB, e=2)
        hid = keym[:, 0:2 * HB * P].rearrange("p (x m n) -> p x m n", x=2, m=HB)
        hpad = attnm[:, 0:IB * IMAGES * PADSEQ].rearrange("p (k i s) -> p k i s", k=IB, i=IMAGES)
        hT = sb("hT", [P, DB, TOKENS])
        xn = sb("xn", [P, DB, TOKENS])
        fcs = xn
        cen = sb("cen", [P, IB, TOKENS])
        qT = cen[:, 0:2, :]
        oT = cen[:, 2:4, :]
        std = sb("std", [P, 2, HALF])
        rstd = sb("rstd", [P, 2, HALF])
        eps = sb("eps", [P, 1])
        spa = sb("spa", [P, 2, DB, D])
        specm = sb("specm", [P, DB, D])
        kr = sb("kr", [P, HALF])
        rot1 = sb("rot1", [P, HALF])
        rot2 = sb("rot2", [P, HALF])
        identb = sb("identb", [P, P], BF16)
        maskb = sb("maskb", [AW, 4, AW], BF16)
        smax = sb("smax", [AW, 3, 4])
        rden = sb("rden", [AW, 2, HEADS])
        onorm = sb("onorm", [AW, 2, D])
        prob = sb("prob", [P, RT, EXPERTS])
        rtmp = sb("rtmp", [P, RT, EXPERTS])
        pick = sb("pick", [P, 2, RT, EXPERTS])
        both = sb("both", [P, RT, EXPERTS])
        gates = sb("gates", [P, RT, EXPERTS])
        slotv = sb("slotv", [P, RT, EXPERTS])
        obase = sb("obase", [P, EXPERTS])
        red = sb("red", [P, 6, RT])
        gsel = sb("gsel", [P, 2, RT])
        slot = sb("slot", [P, 2, RT], I32)
        extra = sb("extra", [EXPERTS, 2])
        count = sb("count", [EXPERTS, 1])
        extrab = sb("extrab", [EXPERTS, P])
        gT = sb("gT", [EXPERTS, TOKENS])
        past = sb("past", [1, OVERFLOW, EXPERTS])
        oexpf = sb("oexpf", [1, OVERFLOW])
        oexp = sb("oexp", [1, OVERFLOW], I32)
        xs = sb("xs", [P, 2, D])
        xsT = sb("xsT", [P, 2, DB, P])
        ysb = sb("ysb", [P, 2, D])
        zeros = ysb[:, 0, :]

        def c(name, rows=P):
            at, n = CONST[name]
            return cst[0:rows, at:at + n]

        def vcol(name, m):
            at, _ = VEC[name]
            return vec[:, at + m:at + m + 1]

        bank = [ctx.enter_context(nc.psum_tensor(f"bank{i}", [P, 512], F32)) for i in range(8)]
        vbank, abank, obank = bank[0:3], bank[3:6], bank[6:8]

        xs_bank, y_banks = [bank[2], bank[5]], obank
        up_banks_a, up_banks_b = [bank[3], bank[4]], [bank[0], bank[1]]

        def vb(key):
            return vbank[VNUM[key] % VBANKS]

        def ab(key):
            return abank[ANUM[key] % ABANKS]

        const_in, spec_in, tok_in, attn_in, rest_in = (
            sem(n) for n in ("const_in", "spec_in", "tok_in", "attn_in", "rest_in"))
        v_full, v_read = sem("v_full"), sem("v_read")
        a_full, a_read = sem("a_full"), sem("a_read")
        squared = sem("squared")
        xn_ready = sem("xn_ready")
        k_rotated = sem("k_rotated")
        k_split = sem("k_split")
        eps_ready = sem("eps_ready")
        vaug_ones = sem("vaug_ones")
        hpad_zero = sem("hpad_zero")
        zeros_ready = sem("zeros_ready")
        bf16_consts = sem("bf16_consts")
        q_ready = sem("q_ready")
        probs_ready = sem("probs_ready")
        pv_done = sem("pv_done")
        o_ready = sem("o_ready")
        dve_step = sem("dve_step")
        zeroed = sem("zeroed")
        shifted = sem("shifted")
        exped = sem("exped")
        picked = sem("picked")
        slots_ready = sem("slots_ready")
        scattered = sem("scattered")
        w_in = [sem(f"w_in{i}") for i in range(RING)]
        xs_in = [sem(f"xs_in{i}") for i in range(2)]
        xs_turned = sem("xs_turned")
        xs_copied = sem("xs_copied")
        up_a, up_b = sem("up_a"), sem("up_b")
        relu_a, relu_b = sem("relu_a"), sem("relu_b")
        down = sem("down")
        y_ready = sem("y_ready")
        y_out = [sem(f"y_out{i}") for i in range(2)]
        gathered = sem("gathered")
        final = sem("final")
        stored = sem("stored")

        block = ctx.enter_context(nc.Block())

        @block.sync
        def _(sp):
            sp.dma_start(cst[:, :], consts).then_inc(const_in, 16)
            sp.dma_start(specw[:, :, :, :], spec_w).then_inc(spec_in, 16)
            sp.dma_start(specc[:, :, :, :], spec_c).then_inc(spec_in, 16)
            sp.dma_start(tokw[:, :, :], tok_w).then_inc(tok_in, 16)
            sp.dma_start(tokadd[:, :], tok_add).then_inc(tok_in, 16)
            sp.dma_start(toksel[:, :], tok_sel).then_inc(tok_in, 16)
            sp.dma_start(xpatch, patches).then_inc(tok_in, 16)
            sp.dma_start(attnw[:, :, :, :], attn_w).then_inc(attn_in, 16)
            sp.dma_start(vec[:, :], vecs).then_inc(rest_in, 16)
            sp.dma_start(inw[:, :, :], inproj_w).then_inc(rest_in, 16)
            sp.dma_start(convw[:, :, :, :], conv_w).then_inc(rest_in, 16)
            sp.dma_start(fcw[:, :, :], fc_w).then_inc(rest_in, 16)
            sp.dma_start(cprojw[:, :, :], cproj_w).then_inc(rest_in, 16)
            sp.dma_start(outw[:, :, :], out_w).then_inc(rest_in, 16)
            sp.dma_start(routerw[:, :, :], router_w).then_inc(rest_in, 16)
            sp.dma_start(routerb[:, :], router_b).then_inc(rest_in, 16)
            sp.dma_start(b2s[:, :], b2).then_inc(rest_in, 16)
            for e in range(RING):
                sp.dma_start(wexp[:, e, :], experts[e]).then_inc(w_in[e], 16)
            sp.wait_ge(zeros_ready, 1)
            sp.dma_start(slot_x.rearrange("(t p) c -> p t c", p=P),
                         zeros.unsqueeze(1).to_broadcast([P, TILES, D])).then_inc(zeroed, 16)
            sp.wait_ge(scattered, 2 * RT * 16)
            for j in range(2):
                sp.dma_start(xs[:, j, :], slot_x[j * P:(j + 1) * P, :]).then_inc(xs_in[j], 16)

            def step(j, u, expert):
                sp.wait_ge(down, j + 1)
                if expert is not None:
                    sp.dma_start(wexp[:, u % RING, :],
                                 experts[bass.ds(expert, 1)].rearrange("o p c -> (o p) c")
                                 ).then_inc(w_in[u % RING], 16)

            def rows(j, u):
                sp.dma_start(xs[:, u % 2, :], slot_x[bass.ds((j + 2) * P, P), :]).then_inc(xs_in[u % 2], 16)

            def store(j, u):
                sp.wait_ge(y_ready, j + 1)
                sp.dma_start(slot_y[bass.ds(j * P, P), :], ysb[:, u % 2, :]).then_inc(y_out[u % 2], 16)

            with sp.Fori(0, EXPERTS // RING - 1) as i:
                for u in range(RING):
                    step(i * RING + u, u, i * RING + (u + RING))
                    rows(i * RING + u, u)
                    store(i * RING + u, u)
            sp.wait_ge(slots_ready, 2)
            for j in range(EXPERTS - RING, TILES):
                over = j + RING - EXPERTS
                step(j, j, sp.value_load(oexp[0:1, over:over + 1], min_val=0, max_val=EXPERTS - 1)
                     if over < OVERFLOW else None)
                if j + 2 < TILES:
                    rows(j, j)
                store(j, j)
            for t in range(RT):
                sp.wait_ge(final, t + 1)
                sp.dma_start(out[t * P:t * P + ROWS[t], :], base[0:ROWS[t], t, :]).then_inc(stored, 16)
            sp.wait_ge(stored, 16 * RT)

        @block.gpsimd
        def _(pool):
            nc.gpsimd.memset(eps[:, :], EPS).then_inc(eps_ready, 1)
            pool.wait_ge(v_full, VNUM["spec_m", 1] + 1)
            nc.gpsimd.memset(vaug, 1.0).then_inc(vaug_ones, 1)
            pool.wait_ge(v_full, VNUM["wo", 1, 1] + 1)
            nc.gpsimd.memset(hpad, 0.0).then_inc(hpad_zero, 1)
            pool.wait_ge(slots_ready, 1)
            pool.wait_ge(zeroed, 16)
            for t in range(RT):
                pool.wait_ge(a_read, ANUM["xrow", t] + 1)
                for k in range(2):
                    nc.gpsimd.indirect_dma_start(
                        out=slot_x, out_offset=bass.IndirectOffsetOnAxis(slot[0:ROWS[t], k, t:t + 1], 0),
                        in_=xrow[0:ROWS[t], t, :], in_offset=None).then_inc(scattered, 16)
            for u in range(2):
                pool.wait_ge(y_out[u], 16 * ((TILES + 1 - u) // 2))
            for t in range(RT):
                for k, g in enumerate((got, got2)):
                    nc.gpsimd.indirect_dma_start(
                        out=g[0:ROWS[t], t, :], out_offset=None, in_=slot_y,
                        in_offset=bass.IndirectOffsetOnAxis(slot[0:ROWS[t], k, t:t + 1], 0)
                    ).then_inc(gathered, 16)
            pool.wait_ge(gathered, 32 * RT)
            pool.wait_ge(stored, 16 * RT)

        @block.tensor
        def _(pe):
            order = {"v": 0, "a": 0}

            def fill(key):
                if key in VNUM:
                    n = VNUM[key]
                    assert n == order["v"], (key, n, order)
                    order["v"] += 1
                    if n >= VBANKS:
                        pe.wait_ge(v_read, n - VBANKS + 1)
                    return vb(key)
                n = ANUM[key]
                assert n == order["a"], (key, n, order)
                order["a"] += 1
                if n >= ABANKS:
                    pe.wait_ge(a_read, n - ABANKS + 1)
                return ab(key)

            def linear(key, dst, lhs, rhs, more=None):
                pairs = list(zip(lhs, rhs)) + (more or [])
                for k, (l, r) in enumerate(pairs):
                    mm = nc.tensor.matmul(dst, l, r, start=k == 0, stop=k == len(pairs) - 1)
                mm.then_inc(v_full if key in VNUM else a_full, 1)

            def cols(h):
                return slice(h * HALF, (h + 1) * HALF)

            ident, means = c("ident"), c("means")

            def norm_sums(n, src, blocks, ready):
                for h in range(2):
                    ready(h)
                    b = fill(("mean", n, h))
                    linear(("mean", n, h), b[:, 0:HALF], [means] * blocks,
                           [src[:, k, cols(h)] for k in range(blocks)])
                for h in range(2):
                    b = fill(("var", n, h))
                    pe.wait_ge(squared, 2 * n + h + 1)
                    linear(("var", n, h), b[:, 0:HALF], [means] * blocks,
                           [sq[:, h, k, :] for k in range(blocks)])

            pe.wait_ge(spec_in, 32)
            wr, wi = specw[:, 0], specw[:, 1]
            co, si, ns = specc[:, 0], specc[:, 1], specc[:, 2]
            for part in range(2):
                for j in range(DB):
                    b = fill(("spec_a", part, j))
                    js = slice(j * P, (j + 1) * P)
                    first, second = ((wr, co), (wi, si)) if part == 0 else ((wi, co), (wr, ns))
                    linear(("spec_a", part, j), b[:, 0:D],
                           [w[:, k, js] for w, _ in (first, second) for k in range(DB)],
                           [f[:, k, :] for _, f in (first, second) for k in range(DB)])
            pe.wait_ge(v_read, VNUM["spec_a", 1, 1] + 1)
            for d in range(DB):
                b = fill(("spec_m", d))
                ds = slice(d * P, (d + 1) * P)
                linear(("spec_m", d), b[:, 0:D],
                       [spa[:, part, k, ds] for part in range(2) for k in range(DB)],
                       [f[:, k, :] for f in (co, ns) for k in range(DB)])

            pe.wait_ge(tok_in, 64)
            for h in range(2):
                for m in range(DB):
                    b = fill(("tok", h, m))
                    ms = slice(m * P, (m + 1) * P)
                    linear(("tok", h, m), b[:, 0:HALF], [tokw[:, k, ms] for k in range(PB)],
                           [xpatch[:, k, cols(h)] for k in range(PB)],
                           [(tokadd[:, ms], toksel[:, :])])

            pe.wait_ge(const_in, 16)
            norm_sums(0, hT, DB, lambda h: pe.wait_ge(a_read, ANUM["tok", h, 1] + 1))

            pe.wait_ge(attn_in, 16)
            for h in range(2):
                pe.wait_ge(xn_ready, h + 1)
                for m in range(DB):
                    ms = slice(m * P, (m + 1) * P)
                    for x in ("q", "k"):
                        for r in range(2):
                            w = attnw[:, 2 * (x == "k") + r]
                            b = fill((x, h, m, r))
                            linear((x, h, m, r), b[:, 0:HALF], [w[:, k, ms] for k in range(DB)],
                                   [xn[:, k, cols(h)] for k in range(DB)])
            for t, (c0, n) in enumerate(ATT):
                b = fill(("v", t))
                linear(("v", t), b[0:n, 0:D], [xn[:, k, c0:c0 + n] for k in range(DB)],
                       [attnw[:, 4, k, :] for k in range(DB)])

            pe.wait_ge(bf16_consts, 2)
            pe.wait_ge(k_split, 4)
            pe.wait_ge(q_ready, 4)
            for u in range(len(UNITS) + 4):
                if u < len(UNITS):
                    t, pair = UNITS[u]
                    c0, n = ATT[t]
                    b = fill(("score", u))
                    nc.tensor.matmul(b[0:n, 0:4 * n].rearrange("p (a q) -> p a q", a=4), identb[0:n, 0:n],
                                     maskb[0:n, :, 0:n], start=True, stop=False)
                    ps = slice(32 * pair, 32 * pair + 32)
                    for half in range(2):
                        mm = nc.tensor.matmul(
                            b[0:n, 2 * n * half:2 * n * (half + 1)].rearrange("p (a q) -> p a q", a=2),
                            qT[ps, half, c0:c0 + n], kT[ps, half, :, c0:c0 + n],
                            start=False, stop=half == 1)
                    mm.then_inc(v_full, 1)
                if 0 <= u - 2 < len(UNITS):
                    w = u - 2
                    n = ATT[UNITS[w][0]][1]
                    b = fill(("pt", w))
                    pe.wait_ge(probs_ready, w + 1)
                    for a in range(4):
                        mm = nc.tensor.transpose(b[0:n, a * n:(a + 1) * n], pr[0:n, w % 2, a * n:(a + 1) * n],
                                                 ident[0:n, 0:n])
                    mm.then_inc(a_full, 1)
                if 0 <= u - 3 < len(UNITS):
                    w = u - 3
                    t, pair = UNITS[w]
                    n = ATT[t][1]
                    pe.wait_ge(a_read, ANUM["pt", w] + 1)
                    if pair == 0 and t >= 2:
                        pe.wait_ge(o_ready, t - 1)
                    for a in range(4):
                        head = 8 * (a // 2) + 2 * pair + a % 2
                        mm = nc.tensor.matmul(obank[t % 2][0:n, head * (HD + 1):(head + 1) * (HD + 1)],
                                              prT[0:n, w % 2, a * n:(a + 1) * n], vaug[0:n, t, head, :],
                                              start=True, stop=True)
                    mm.then_inc(pv_done, 1)
                if u >= 4 and (u - 4) % 4 == 3:
                    t = (u - 4) // 4
                    n = ATT[t][1]
                    b = fill(("ot", t))
                    pe.wait_ge(o_ready, t + 1)
                    for m in range(DB):
                        mm = nc.tensor.transpose(b[:, m * n:(m + 1) * n], onorm[0:n, t % 2, m * P:(m + 1) * P],
                                                 ident[0:n, 0:n])
                    mm.then_inc(a_full, 1)

            def halves(name, blocks, w, src, depth, ready):
                for h in range(2):
                    ready(h)
                    for m in range(blocks):
                        b = fill((name, h, m))
                        linear((name, h, m), b[:, 0:HALF], [w[:, k, m * P:(m + 1) * P] for k in range(depth)],
                               [src[:, k, cols(h)] for k in range(depth)])

            halves("wo", DB, attnw[:, 5], oT, DB, lambda h: pe.wait_ge(a_read, ANUM["ot", 3 * h + 2] + 1))
            norm_sums(1, hT, DB, lambda h: pe.wait_ge(v_read, VNUM["wo", h, 1] + 1))
            halves("ffn", DB, specm[:, :, :], xn, DB, lambda h: pe.wait_ge(xn_ready, 2 + h + 1))
            norm_sums(2, hT, DB, lambda h: pe.wait_ge(v_read, VNUM["ffn", h, 1] + 1))

            pe.wait_ge(rest_in, 9 * 16)
            for h in range(2):
                pe.wait_ge(xn_ready, 4 + h + 1)
                for part, name in enumerate(("inh", "gate")):
                    for m in range(IB):
                        b = fill((name, h, m))
                        linear((name, h, m), b[:, 0:HALF],
                               [inw[:, k, part * INNER + m * P:part * INNER + (m + 1) * P] for k in range(DB)],
                               [xn[:, k, cols(h)] for k in range(DB)])
            for h in range(2):
                for m in range(IB):
                    b = fill(("conv", h, m))
                    pe.wait_ge(v_read, VNUM["inh", h, m] + 1)
                    linear(("conv", h, m), b[:, 0:HALF].rearrange("p (i s) -> p i s", s=SEQ),
                           [convw[:, m, tap, :] for tap in range(TAPS)],
                           [hpad[:, m, 8 * h:8 * h + 8, tap:tap + SEQ] for tap in range(TAPS)])
            norm_sums(3, res, IB, lambda h: pe.wait_ge(v_read, VNUM["conv", h, 3] + 1))
            halves("fc", DB, fcw, hn, IB, lambda h: pe.wait_ge(xn_ready, 6 + h + 1))
            halves("cproj", IB, cprojw, fcs, DB, lambda h: pe.wait_ge(a_read, ANUM["fc", h, 1] + 1))
            halves("out", DB, outw, cen, IB, lambda h: pe.wait_ge(v_read, VNUM["cproj", h, 3] + 1))
            norm_sums(4, hT, DB, lambda h: pe.wait_ge(v_read, VNUM["out", h, 1] + 1))

            pe.wait_ge(xn_ready, 10)
            b = fill(("logits",))
            for t in range(RT):
                ts = slice(t * P, t * P + ROWS[t])
                for k in range(DB):
                    nc.tensor.matmul(b[0:ROWS[t], t * EXPERTS:(t + 1) * EXPERTS], xn[:, k, ts],
                                     routerw[:, k, :], start=k == 0, stop=False)
                mm = nc.tensor.matmul(b[0:ROWS[t], t * EXPERTS:(t + 1) * EXPERTS], c("ones", 1)[:, 0:ROWS[t]], routerb[:, :], start=False, stop=True)
            mm.then_inc(v_full, 1)
            for name, src in (("xrow", xn), ("hrow", hT)):
                for t in range(RT):
                    b = fill((name, t))
                    for m in range(DB):
                        mm = nc.tensor.transpose(b[0:ROWS[t], m * P:(m + 1) * P],
                                                 src[:, m, t * P:t * P + ROWS[t]], ident)
                    mm.then_inc(a_full, 1)
            pe.wait_ge(picked, 1)
            b = fill(("pos",))
            for t in range(RT):
                for s in range(t + 1):
                    nc.tensor.matmul(b[:, t * EXPERTS:(t + 1) * EXPERTS],
                                     c("tri") if s == t else c("ones"),
                                     both[:, s, :], start=s == 0, stop=s == t)
            for t in range(RT):
                mm = nc.tensor.matmul(b[0:EXPERTS, RT * EXPERTS:RT * EXPERTS + 1], both[:, t, :],
                                      c("ones")[:, 0:1], start=t == 0, stop=t == RT - 1)
            mm.then_inc(v_full, 1)
            pe.wait_ge(picked, 2)
            b = fill(("offset",))
            linear(("offset",), b[:, 0:2 * EXPERTS], [extrab[:, :]], [c("tri16", EXPERTS)])
            for g in range(2):
                b = fill(("gt", g))
                for t in ((0, 1, 2, 3), (4,))[g]:
                    mm = nc.tensor.transpose(b[0:EXPERTS, (t % 4) * P:(t % 4 + 1) * P], gates[:, t, :], ident)
                mm.then_inc(v_full, 1)
            for t in range(RT):
                b = fill(("b2", t))
                pe.wait_ge(v_read, VNUM["gt", t // 4] + 1)
                linear(("b2", t), b[0:ROWS[t], 0:D], [gT[:, t * P:t * P + ROWS[t]]], [b2s[:, :]])

            pe.wait_ge(v_read, len(VJOBS))
            pe.wait_ge(a_read, len(AJOBS))

            def turn(w_xs, w_read, u):
                pe.wait_ge(xs_in[u % 2], w_xs)
                if w_read is not None:
                    pe.wait_ge(xs_copied, w_read)
                for k in range(DB):
                    mm = nc.tensor.transpose(xs_bank[u % 2][:, k * P:(k + 1) * P], xs[:, u % 2, k * P:(k + 1) * P],
                                             ident)
                mm.then_inc(xs_turned, 1)

            def up(j, w_w, w_a, w_b, u):
                pe.wait_ge(xs_copied, j + 1)
                pe.wait_ge(w_in[u % RING], w_w)
                w1 = wexp[:, u % RING, 0:DB * HIDDEN].rearrange("p (k n) -> p k n", k=DB)
                for g, (banks, free, w_free, full) in enumerate(((up_banks_a, relu_a, w_a, up_a),
                                                                 (up_banks_b, relu_b, w_b, up_b))):
                    if w_free is not None:
                        pe.wait_ge(free, w_free)
                    for i in range(4):
                        m = 4 * g + i
                        for k in range(DB):
                            mm = nc.tensor.matmul(banks[u % 2][:, i * P:(i + 1) * P], w1[:, k, m * P:(m + 1) * P],
                                                  xsT[:, u % 2, k, :], start=k == 0, stop=k == DB - 1)
                    mm.then_inc(full, 1)

            def downs(j, w_y, u):
                w2 = wexp[:, u % RING, DB * HIDDEN:DB * HIDDEN + HB * D].rearrange("p (m n) -> p m n", m=HB)
                if w_y is not None:
                    pe.wait_ge(y_ready, w_y)
                for m in range(HB):
                    if m == 0:
                        pe.wait_ge(relu_a, j + 1)
                    if m == HB // 2:
                        pe.wait_ge(relu_b, j + 1)
                    mm = nc.tensor.matmul(y_banks[u % 2][:, 0:D], hid[:, u % 2, m, :], w2[:, m, :],
                                          start=m == 0, stop=m == HB - 1)
                mm.then_inc(down, 1)

            turn(16, None, 0)
            up(0, 16, None, None, 0)
            for j in range(1, RING + 1):
                turn(16 * (j // 2 + 1), j - 1 if j >= 2 else None, j)
                downs(j - 1, j - 2 if j >= 3 else None, j - 1)
                up(j, 16 * (j // RING + 1), j - 1 if j >= 2 else None, j - 1 if j >= 2 else None, j)
            with pe.Fori(1, (TILES - 1) // RING) as i:
                for u in range(1, RING + 1):
                    j = i * RING + u
                    turn(i * (RING // 2 * 16) + 16 * (u // 2 + 1), j - 1, u)
                    downs(j - 1, j - 2, u - 1)
                    up(j, i * 16 + 16 * (u // RING + 1), j - 1, j - 1, u)
            downs(TILES - 1, TILES - 2, TILES - 1)

        @block.scalar
        def _(act):
            def take(key):
                act.wait_ge(a_full, ANUM[key] + 1)
                return ab(key)

            def cols(h):
                return slice(h * HALF, (h + 1) * HALF)

            def squares(n, blocks):
                for h in range(2):
                    act.wait_ge(v_read, VNUM["mean", n, h] + 1)
                    nc.scalar.activation(sq[:, h, 0:blocks, :], cen[:, 0:blocks, cols(h)], ACT.Square
                                         ).then_inc(squared, 1)
                for h in range(2):
                    b = take(("var", n, h))
                    if n:
                        act.wait_ge(xn_ready, 2 * n - 1 + h)
                    nc.scalar.activation(std[:, h, :], b[:, 0:HALF], ACT.Sqrt, bias=eps[:, :],
                                         scale=D / (blocks * P)).then_inc(a_read, 1)

            for h in range(2):
                for m in range(DB):
                    b = take(("tok", h, m))
                    nc.scalar.activation(hT[:, m, cols(h)], b[:, 0:HALF], ACT.Copy).then_inc(a_read, 1)
            act.wait_ge(eps_ready, 1)
            squares(0, DB)
            act.wait_ge(const_in, 16)
            for h in range(2):
                for m in range(DB):
                    act.wait_ge(k_rotated, 2 * h + m + 1)
                    for e in range(2):
                        kk = nc.scalar.activation(kT[:, m, e, cols(h)], kr[:, :], ACT.Copy,
                                                  scale=c("headmask")[:, e:e + 1])
                    kk.then_inc(k_split, 1)
            act.wait_ge(vaug_ones, 1)
            for t, (c0, n) in enumerate(ATT):
                b = take(("v", t))
                nc.scalar.activation(vaug[0:n, t, :, 0:HD], b[0:n, 0:D].rearrange("p (a d) -> p a d", a=HEADS),
                                     ACT.Copy).then_inc(a_read, 1)
            for u in range(len(UNITS) + 4):
                if 0 <= u - 2 < len(UNITS):
                    w = u - 2
                    n = ATT[UNITS[w][0]][1]
                    b = take(("pt", w))
                    if w >= 2:
                        act.wait_ge(pv_done, w - 1)
                    nc.scalar.activation(prT[0:n, w % 2, 0:4 * n], b[0:n, 0:4 * n], ACT.Copy).then_inc(a_read, 1)
                if u < len(UNITS):
                    n = ATT[UNITS[u][0]][1]
                    act.wait_ge(v_read, VNUM["score", u] + 1)
                    nc.scalar.activation(pr[0:n, u % 2, 0:4 * n], sc[0:n, u % 3, 0:4 * n], ACT.Exp,
                                         scale=HD ** -0.5).then_inc(probs_ready, 1)
                if u >= 4 and (u - 4) % 4 == 3:
                    t = (u - 4) // 4
                    c0, n = ATT[t]
                    b = take(("ot", t))
                    nc.scalar.activation(oT[:, :, c0:c0 + n], b[:, 0:2 * n].rearrange("p (m n) -> p m n", m=2),
                                         ACT.Copy).then_inc(a_read, 1)
            squares(1, DB)
            squares(2, DB)
            for h in range(2):
                for m in range(IB):
                    b = take(("gate", h, m))
                    nc.scalar.activation(gate[:, m, cols(h)], b[:, 0:HALF], ACT.Silu).then_inc(a_read, 1)
            squares(3, IB)
            for h in range(2):
                for m in range(DB):
                    b = take(("fc", h, m))
                    nc.scalar.activation(fcs[:, m, cols(h)], b[:, 0:HALF], ACT.Silu, bias=vcol("fc_b", m)
                                         ).then_inc(a_read, 1)
            squares(4, DB)
            act.wait_ge(shifted, 1)
            nc.scalar.activation(rtmp[:, :, :], prob[:, :, :], ACT.Exp).then_inc(exped, 1)
            for name, dst in (("xrow", xrow), ("hrow", base)):
                for t in range(RT):
                    b = take((name, t))
                    nc.scalar.activation(dst[0:ROWS[t], t, :], b[0:ROWS[t], 0:D], ACT.Copy).then_inc(a_read, 1)

            def relu(j, u):
                act.wait_ge(up_a, j + 1)
                for i in range(4):
                    r = nc.scalar.activation(hid[:, u % 2, i, :], up_banks_a[u % 2][:, i * P:(i + 1) * P], ACT.Relu,
                                             bias=wexp[:, u % RING, WCOLS - HB + i:WCOLS - HB + i + 1])
                r.then_inc(relu_a, 1)

            def rows_out(j, w_out, u):
                act.wait_ge(down, j + 1)
                if w_out is not None:
                    act.wait_ge(y_out[u % 2], w_out)
                nc.scalar.activation(ysb[:, u % 2, :], y_banks[u % 2][:, 0:D], ACT.Copy).then_inc(y_ready, 1)

            act.wait_ge(zeroed, 16)
            relu(0, 0)
            for j in range(1, RING + 1):
                rows_out(j - 1, 16 * ((j - 1) // 2) if j >= 3 else None, j - 1)
                relu(j, j)
            with act.Fori(1, (TILES - 1) // RING) as i:
                for u in range(1, RING + 1):
                    j = i * RING + u
                    rows_out(j - 1, i * (RING // 2 * 16) + 16 * ((u - 1) // 2), u - 1)
                    relu(j, u)
            rows_out(TILES - 1, 16 * ((TILES - 1) // 2), TILES - 1)

        @block.vector
        def _(dve):
            steps = [0]

            def then(ins):
                steps[0] += 1
                ins.then_inc(dve_step, 1)
                dve.wait_ge(dve_step, steps[0])

            def take(key):
                dve.wait_ge(v_full, VNUM[key] + 1)
                return vb(key)

            def cols(h):
                return slice(h * HALF, (h + 1) * HALF)

            def norm(n, x, blocks, dst):
                share = D / (blocks * P)
                for h in range(2):
                    b = take(("mean", n, h))
                    nc.vector.scalar_tensor_tensor(
                        out=cen[:, 0:blocks, cols(h)], in0=b[:, 0:HALF].unsqueeze(1).to_broadcast([P, blocks, HALF]),
                        scalar=-share, in1=x[:, :, cols(h)], op0=ALU.mult, op1=ALU.add).then_inc(v_read, 1)
                for h in range(2):
                    dve.wait_ge(a_read, ANUM["var", n, h] + 1)
                    then(nc.vector.reciprocal(rstd[:, h, :], std[:, h, :]))
                    r = nc.vector.tensor_tensor(dst[:, :, cols(h)], cen[:, 0:blocks, cols(h)],
                                                rstd[:, h, :].unsqueeze(1).to_broadcast([P, blocks, HALF]), ALU.mult)
                    if blocks == IB:
                        then(r)
                        for m in range(blocks):
                            r = nc.vector.tensor_scalar(dst[:, m, cols(h)], dst[:, m, cols(h)], vcol("ln_g", m),
                                                        vcol("ln_b", m), ALU.mult, ALU.add)
                    r.then_inc(xn_ready, 1)

            nc.vector.memset(zeros, 0.0).then_inc(zeros_ready, 1)
            then(nc.vector.memset(prob[:, :, :], 0.0))
            dve.wait_ge(const_in, 16)
            nc.vector.tensor_copy(identb[:, :], c("ident")).then_inc(bf16_consts, 1)
            nc.vector.tensor_copy(maskb[:, :, :], c("attmask", AW).unsqueeze(1).to_broadcast([AW, 4, AW])
                                  ).then_inc(bf16_consts, 1)
            for part in range(2):
                for j in range(DB):
                    b = take(("spec_a", part, j))
                    nc.vector.tensor_copy(spa[:, part, j, :], b[:, 0:D]).then_inc(v_read, 1)
            for d in range(DB):
                b = take(("spec_m", d))
                nc.vector.tensor_scalar(specm[:, d, :], b[:, 0:D], 1.0 / D, None, ALU.mult).then_inc(v_read, 1)
            norm(0, hT, DB, xn)
            for h in range(2):
                for m in range(DB):
                    for x in ("q", "k"):
                        if x == "k":
                            dve.wait_ge(q_ready, 2 * h + m + 1)
                        elif 2 * h + m:
                            dve.wait_ge(k_rotated, 2 * h + m)
                        for r, (tmp, table) in enumerate(((rot1, "cos"), (rot2, "sin"))):
                            b = take((x, h, m, r))
                            nc.vector.tensor_tensor(
                                tmp[:, :].rearrange("p (i s) -> p i s", s=SEQ),
                                b[:, 0:HALF].rearrange("p (i s) -> p i s", s=SEQ),
                                c(table).unsqueeze(1).to_broadcast([P, 8, SEQ]), ALU.mult).then_inc(v_read, 1)
                        dve.wait_ge(v_read, VNUM[x, h, m, 1] + 1)
                        if x == "q":
                            nc.vector.tensor_tensor(qT[:, m, cols(h)], rot1[:, :], rot2[:, :], ALU.add
                                                    ).then_inc(q_ready, 1)
                        else:
                            if 2 * h + m:
                                dve.wait_ge(k_split, 2 * h + m)
                            nc.vector.tensor_tensor(kr[:, :], rot1[:, :], rot2[:, :], ALU.add
                                                    ).then_inc(k_rotated, 1)
            for u in range(len(UNITS) + 4):
                if u < len(UNITS):
                    n = ATT[UNITS[u][0]][1]
                    b = take(("score", u))
                    s4 = b[0:n, 0:4 * n].rearrange("p (a q) -> p a q", a=4)
                    then(nc.vector.tensor_reduce(smax[0:n, u % 3, :], s4, AX.X, ALU.max))
                    if u >= 3:
                        dve.wait_ge(probs_ready, u - 2)
                    nc.vector.tensor_tensor(sc[0:n, u % 3, 0:4 * n].rearrange("p (a q) -> p a q", a=4), s4,
                                            smax[0:n, u % 3, :].unsqueeze(2).to_broadcast([n, 4, n]), ALU.subtract
                                            ).then_inc(v_read, 1)
                if 0 <= u - 3 < len(UNITS) and UNITS[u - 3][1] == 3:
                    t = UNITS[u - 3][0]
                    n = ATT[t][1]
                    dve.wait_ge(pv_done, u - 2)
                    o = obank[t % 2][0:n, 0:HEADS * (HD + 1)].rearrange("p (a d) -> p a d", a=HEADS)
                    then(nc.vector.reciprocal(rden[0:n, t % 2, :].unsqueeze(2), o[:, :, HD:HD + 1]))
                    if t >= 2:
                        dve.wait_ge(a_full, ANUM["ot", t - 2] + 1)
                    nc.vector.tensor_tensor(onorm[0:n, t % 2, :].rearrange("p (a d) -> p a d", a=HEADS),
                                            o[:, :, 0:HD],
                                            rden[0:n, t % 2, :].unsqueeze(2).to_broadcast([n, HEADS, HD]), ALU.mult
                                            ).then_inc(o_ready, 1)

            def add_to_stream(name, bias):
                for h in range(2):
                    for m in range(DB):
                        b = take((name, h, m))
                        if bias is None:
                            r = nc.vector.tensor_tensor(hT[:, m, cols(h)], b[:, 0:HALF], hT[:, m, cols(h)], ALU.add)
                        else:
                            r = nc.vector.scalar_tensor_tensor(
                                out=hT[:, m, cols(h)], in0=b[:, 0:HALF], scalar=vcol(bias, m),
                                in1=hT[:, m, cols(h)], op0=ALU.add, op1=ALU.add)
                        r.then_inc(v_read, 1)

            add_to_stream("wo", None)
            norm(1, hT, DB, xn)
            dve.wait_ge(rest_in, 9 * 16)
            add_to_stream("ffn", "ffn_bias")
            norm(2, hT, DB, xn)
            dve.wait_ge(hpad_zero, 1)
            for h in range(2):
                for m in range(IB):
                    b = take(("inh", h, m))
                    nc.vector.tensor_copy(hpad[:, m, 8 * h:8 * h + 8, TAPS - 1:PADSEQ],
                                          b[:, 0:HALF].rearrange("p (i s) -> p i s", s=SEQ)).then_inc(v_read, 1)
            for h in range(2):
                for m in range(IB):
                    b = take(("conv", h, m))
                    dve.wait_ge(a_read, ANUM["gate", h, m] + 1)
                    nc.vector.scalar_tensor_tensor(out=res[:, m, cols(h)], in0=b[:, 0:HALF], scalar=vcol("conv_b", m),
                                                   in1=gate[:, m, cols(h)], op0=ALU.add, op1=ALU.mult
                                                   ).then_inc(v_read, 1)
            norm(3, res, IB, hn)
            for h in range(2):
                for m in range(IB):
                    b = take(("cproj", h, m))
                    nc.vector.scalar_tensor_tensor(out=cen[:, m, cols(h)], in0=b[:, 0:HALF], scalar=vcol("cproj_b", m),
                                                   in1=res[:, m, cols(h)], op0=ALU.add, op1=ALU.add
                                                   ).then_inc(v_read, 1)
            add_to_stream("out", None)
            norm(4, hT, DB, xn)

            wide = [P, RT, EXPERTS]

            def each(x):
                return x.unsqueeze(2).to_broadcast(wide)

            def over_tiles(x):
                return x.unsqueeze(1).to_broadcast(wide)

            pb, tmp, iota = prob[:, :, :], rtmp[:, :, :], over_tiles(c("iota16"))
            b = take(("logits",))
            nc.vector.tensor_copy(prob[:, 0:4, :], b[:, 0:4 * EXPERTS].rearrange("p (t e) -> p t e", t=4))
            nc.vector.tensor_copy(prob[0:ROWS[4], 4, :], b[0:ROWS[4], 4 * EXPERTS:5 * EXPERTS]).then_inc(v_read, 1)
            dve.wait_ge(v_read, VNUM["logits",] + 1)
            then(nc.vector.tensor_reduce(red[:, 0, :], pb, AX.X, ALU.max))
            nc.vector.tensor_tensor(pb, pb, each(red[:, 0, :]), ALU.subtract).then_inc(shifted, 1)
            dve.wait_ge(exped, 1)
            then(nc.vector.tensor_reduce(red[:, 1, :], tmp, AX.X, ALU.add))
            then(nc.vector.reciprocal(red[:, 2, :], red[:, 1, :]))
            then(nc.vector.tensor_tensor(pb, tmp, each(red[:, 2, :]), ALU.mult))
            src = pb
            for k in range(2):
                then(nc.vector.tensor_reduce(gsel[:, k, :], src, AX.X, ALU.max))
                then(nc.vector.tensor_tensor(slotv[:, :, :], src, each(gsel[:, k, :]), ALU.is_equal))
                then(nc.vector.tensor_tensor(slotv[:, :, :], slotv[:, :, :], iota, ALU.mult))
                then(nc.vector.tensor_reduce(red[:, 3, :], slotv[:, :, :], AX.X, ALU.min))
                then(nc.vector.tensor_tensor(pick[:, k, :, :], iota, each(red[:, 3, :]), ALU.is_equal))
                if k == 0:
                    then(nc.vector.scalar_tensor_tensor(out=tmp, in0=pick[:, 0, :, :], scalar=-4.0, in1=pb,
                                                        op0=ALU.mult, op1=ALU.add))
                    src = tmp
            then(nc.vector.tensor_tensor(both[:, :, :], pick[:, 0, :, :], pick[:, 1, :, :], ALU.add))
            nc.vector.tensor_tensor(both[:, :, :], both[:, :, :], each(c("valid")), ALU.mult).then_inc(picked, 1)
            then(nc.vector.tensor_tensor(gates[:, :, :], pick[:, 0, :, :], each(gsel[:, 0, :]), ALU.mult))
            then(nc.vector.tensor_tensor(tmp, pick[:, 1, :, :], each(gsel[:, 1, :]), ALU.mult))
            then(nc.vector.tensor_tensor(gates[:, :, :], gates[:, :, :], tmp, ALU.add))
            b = take(("pos",))
            nc.vector.tensor_copy(slotv[:, :, :], b[:, 0:RT * EXPERTS].rearrange("p (t e) -> p t e", t=RT))
            nc.vector.tensor_copy(count[:, :], b[0:EXPERTS, RT * EXPERTS:RT * EXPERTS + 1]).then_inc(v_read, 1)
            dve.wait_ge(v_read, VNUM["pos",] + 1)
            then(nc.vector.tensor_scalar(extra[:, 0:1], count[:, :], float(P), None, ALU.is_gt))
            last = (TOKENS - 1) // P
            for k in range(2, last + 1):
                then(nc.vector.scalar_tensor_tensor(
                    out=extra[:, (k - 1) % 2:(k - 1) % 2 + 1], in0=count[:, :], scalar=float(k * P),
                    in1=extra[:, k % 2:k % 2 + 1], op0=ALU.is_gt, op1=ALU.add))
            nc.vector.tensor_copy(extrab[:, :], extra[:, (last - 1) % 2:(last - 1) % 2 + 1].to_broadcast([EXPERTS, P])
                                  ).then_inc(picked, 1)
            b = take(("offset",))
            then(nc.vector.tensor_scalar(obase[:, :], b[:, 0:EXPERTS], float(P), float((EXPERTS - 1) * P),
                                         ALU.mult, ALU.add))
            nc.vector.tensor_tensor(past[:, :, :], b[0:1, EXPERTS:2 * EXPERTS].unsqueeze(1)
                                    .to_broadcast([1, OVERFLOW, EXPERTS]),
                                    c("tile_iota", 1).rearrange("p (j e) -> p j e", j=OVERFLOW), ALU.is_le
                                    ).then_inc(v_read, 1)
            then(nc.vector.tensor_tensor(obase[:, :], obase[:, :], c("expert_base"), ALU.subtract))
            then(nc.vector.tensor_scalar(tmp, slotv[:, :, :], float(P), None, ALU.is_ge))
            then(nc.vector.tensor_tensor(tmp, tmp, over_tiles(obase[:, :]), ALU.mult))
            then(nc.vector.tensor_tensor(slotv[:, :, :], slotv[:, :, :], tmp, ALU.add))
            then(nc.vector.tensor_tensor(slotv[:, :, :], slotv[:, :, :], over_tiles(c("expert_base")), ALU.add))
            for k in range(2):
                then(nc.vector.tensor_tensor(tmp, slotv[:, :, :], pick[:, k, :, :], ALU.mult))
                then(nc.vector.tensor_reduce(red[:, 4 + k, :], tmp, AX.X, ALU.add))
            nc.vector.tensor_copy(slot[:, :, :], red[:, 4:6, :]).then_inc(slots_ready, 1)
            dve.wait_ge(v_read, VNUM["offset",] + 1)
            then(nc.vector.tensor_reduce(oexpf[:, :], past[:, :, :], AX.X, ALU.add))
            then(nc.vector.tensor_scalar(oexpf[:, :], oexpf[:, :], float(EXPERTS - 1), None, ALU.min))
            nc.vector.tensor_copy(oexp[:, :], oexpf[:, :]).then_inc(slots_ready, 1)
            for g, n in ((0, 4 * P), (1, ROWS[4])):
                b = take(("gt", g))
                nc.vector.tensor_copy(gT[:, 4 * P * g:4 * P * g + n], b[0:EXPERTS, 0:n]).then_inc(v_read, 1)
            for t in range(RT):
                b = take(("b2", t))
                dve.wait_ge(a_read, ANUM["hrow", t] + 1)
                rows = base[0:ROWS[t], t, :]
                nc.vector.tensor_tensor(rows, b[0:ROWS[t], 0:D], rows, ALU.add).then_inc(v_read, 1)

            def copy_rows(j, u):
                dve.wait_ge(xs_turned, j + 1)
                nc.vector.tensor_copy(xsT[:, u % 2, :, :], xs_bank[u % 2][:, 0:D].rearrange("p (k n) -> p k n", k=DB)
                                      ).then_inc(xs_copied, 1)

            def relu(j, u):
                dve.wait_ge(up_b, j + 1)
                for i in range(4):
                    m = 4 + i
                    r = nc.vector.tensor_scalar(hid[:, u % 2, m, :], up_banks_b[u % 2][:, i * P:(i + 1) * P],
                                                wexp[:, u % RING, WCOLS - HB + m:WCOLS - HB + m + 1], 0.0,
                                                ALU.add, ALU.max)
                r.then_inc(relu_b, 1)

            copy_rows(0, 0)
            relu(0, 0)
            with dve.Fori(0, (TILES - 1) // RING) as i:
                for u in range(1, RING + 1):
                    copy_rows(i * RING + u, u)
                    relu(i * RING + u, u)
            dve.wait_ge(gathered, 32 * RT)
            for t in range(RT):
                rows = base[0:ROWS[t], t, :]
                then(nc.vector.scalar_tensor_tensor(out=rows, in0=got[0:ROWS[t], t, :],
                                                    scalar=gsel[0:ROWS[t], 0, t:t + 1], in1=rows,
                                                    op0=ALU.mult, op1=ALU.add))
                nc.vector.scalar_tensor_tensor(out=rows, in0=got2[0:ROWS[t], t, :],
                                               scalar=gsel[0:ROWS[t], 1, t:t + 1], in1=rows,
                                               op0=ALU.mult, op1=ALU.add).then_inc(final, 1)


def _constants():
    k = np.arange(D)
    angle = 2 * np.pi * ((k[:, None] * k[None, :]) % D) / D
    dft = np.stack([np.cos(angle), np.sin(angle), -np.sin(angle)]).astype(np.float32)
    inv = (1.0 / 10000.0 ** (np.arange(0, HD, 2, dtype=np.float32) / HD)).astype(np.float32)
    freq = np.arange(SEQ, dtype=np.float32)[:, None] * inv[None, :]
    feature = np.arange(P) % HD
    block = {}
    block["cos"] = np.cos(freq)[:, feature % (HD // 2)].T
    block["sin"] = (np.sin(freq)[:, feature % (HD // 2)] * np.where(feature < HD // 2, -1.0, 1.0)[None, :]).T
    p = np.arange(P)
    block["headmask"] = np.stack([(p // HD) % 2 == 0, (p // HD) % 2 == 1], 1)
    block["ident"] = np.eye(P)
    block["means"] = np.full((P, P), 1.0 / D)
    block["ones"] = np.ones((P, P))
    block["tri"] = p[:, None] < p[None, :]
    q = np.arange(AW)
    seen = (q[:, None] // SEQ == q[None, :] // SEQ) & (q[None, :] <= q[:, None])
    mask = np.zeros((P, AW))
    mask[:AW] = np.where(seen, 0.0, -1e30)
    block["attmask"] = mask
    e = np.arange(EXPERTS)
    tri16 = np.zeros((P, 2 * EXPERTS))
    tri16[:EXPERTS] = np.concatenate([e[:, None] < e[None, :], e[:, None] <= e[None, :]], 1)
    block["tri16"] = tri16
    block["iota16"] = np.tile(e - EXPERTS, (P, 1))
    block["expert_base"] = np.tile(e * P, (P, 1))
    block["valid"] = np.stack([p < r for r in ROWS], 1)
    block["tile_iota"] = np.tile(np.repeat(np.arange(OVERFLOW), EXPERTS), (P, 1))
    consts = np.zeros((P, NCONST), np.float32)
    for name, (at, n) in CONST.items():
        consts[:, at:at + n] = block[name]
    sel = np.zeros((SEQ + 2, HALF), np.float32)
    s = np.arange(HALF) % SEQ
    sel[s, np.arange(HALF)] = 1.0
    sel[SEQ] = s > 0
    sel[SEQ + 1] = s == 0
    return dft, consts, sel


def _blocks(w):
    return w.reshape(-1, P, w.shape[1]).transpose(1, 0, 2)


def kernel(**inputs):
    import numpy as _np
    import concourse.bacc as _bacc
    from concourse import mybir as _mybir
    from concourse.bass_utils import run_bass_kernel_spmd as _run

    g = {k: _np.asarray(v) for k, v in inputs.items()}
    dft, consts, sel = _constants()

    x = g["x"].reshape(IMAGES, 3, 6, 16, 6, 16).transpose(1, 3, 5, 0, 2, 4).reshape(PATCH, IMAGES, SEQ - 1)
    patches = _np.zeros((PATCH, IMAGES, SEQ), _np.float32)
    patches[:, :, 1:] = x
    tok_add = _np.concatenate([g["L0_tok_position_embeddings"][0], g["L0_tok_b_lin"][None],
                               g["L0_tok_class_token"][0]], 0)
    swap = (_np.arange(D) // HD) * HD + (_np.arange(D) + HD // 2) % HD
    wq, wk = g["L0_attn_Wq"], g["L0_attn_Wk"]
    attn_w = _np.stack([_blocks(w.T) for w in (wq, wq[swap], wk, wk[swap], g["L0_attn_Wv"], g["L0_attn_Wo"])], 1)
    cw = g["L1_attn_conv_w"].reshape(IB, 2, 64, 64, TAPS)
    conv_w = _np.zeros((2, 64, IB, TAPS, 2, 64), _np.float32)
    for i in range(2):
        conv_w[i, :, :, :, i, :] = cw[:, i].transpose(2, 0, 3, 1)
    vecs = _np.concatenate([g[n].reshape(-1, P).T for n in ("L0_ffn_bias", "L1_attn_conv_b", "L1_attn_ln_g",
                                                            "L1_attn_ln_b", "L1_attn_fc_b", "L1_attn_cproj_b")], 1)
    experts = _np.concatenate([
        g["L1_ffn_W1"].reshape(EXPERTS, DB, P, HIDDEN).transpose(0, 2, 1, 3).reshape(EXPERTS, P, -1),
        g["L1_ffn_W2"].reshape(EXPERTS, HB, P, D).transpose(0, 2, 1, 3).reshape(EXPERTS, P, -1),
        g["L1_ffn_b1"].reshape(EXPERTS, HB, P).transpose(0, 2, 1)], 2)
    args = {
        "patches": _blocks(patches.reshape(PATCH, TOKENS)),
        "spec_w": _np.stack([_blocks(g["L0_ffn_w_freq_real"]), _blocks(g["L0_ffn_w_freq_imag"])], 1),
        "spec_c": _np.stack([_blocks(f) for f in dft], 1),
        "tok_w": _blocks(g["L0_tok_W_lin"].T),
        "tok_add": tok_add, "tok_sel": sel, "attn_w": attn_w, "consts": consts, "vecs": vecs,
        "inproj_w": _blocks(g["L1_attn_in_proj_w"].T),
        "conv_w": conv_w.reshape(P, IB, TAPS, P),
        "fc_w": _blocks(g["L1_attn_fc_w"].T),
        "cproj_w": _blocks(g["L1_attn_cproj_w"].T),
        "out_w": _blocks(g["L1_attn_out_w"].T),
        "router_w": _blocks(g["L1_ffn_Wr"]),
        "router_b": g["L1_ffn_br"][None],
        "experts": experts, "b2": g["L1_ffn_b2"],
    }
    nc = _bacc.Bacc("TRN2", target_bir_lowering=False, num_devices=1)
    arrays, aps = {}, []
    for name, a in args.items():
        a = _np.ascontiguousarray(a)
        arrays[f"in_{name}"] = a
        aps.append(nc.dram_tensor(f"in_{name}", a.shape, _mybir.dt.from_np(a.dtype), kind="ExternalInput").ap())
    out = nc.dram_tensor("out_0", (TOKENS, D), _mybir.dt.float32, kind="ExternalOutput").ap()
    vit_tower_kernel(nc, *aps, out)
    r = _run(nc, [arrays], core_ids=[0])
    return r.results[0]["out_0"].reshape(IMAGES, SEQ, D)
```

```python
import numpy as np
import concourse.bass as bass
from concourse import mybir
from contextlib import ExitStack

F32 = mybir.dt.float32
BF16 = mybir.dt.bfloat16
I32 = mybir.dt.int32
ALU = mybir.AluOpType
ACT = mybir.ActivationFunctionType
AX = mybir.AxisListType

P = 128
IMAGES = 16
SEQ = 37
TOKENS = IMAGES * SEQ
HALF = TOKENS // 2
D = 256
DB = D // P
PATCH = 768
PB = PATCH // P
HEADS = 16
HD = D // HEADS
INNER = 512
IB = INNER // P
TAPS = 4
PADSEQ = SEQ + TAPS - 1
EPS = 1e-5

EXPERTS = 16
HIDDEN = 1024
HB = HIDDEN // P
PAIRS = 2 * TOKENS
TILES = EXPERTS + (PAIRS - EXPERTS) // P
AHEAD = 2
SLOTS = (TILES + AHEAD + 1) * P
ROWS = [P, P, P, P, TOKENS - 4 * P]
RT = len(ROWS)
WCOLS = DB * HIDDEN + HB * D + HB
RING = 4

ATT = [(h * HALF + o, n) for h in range(2) for o, n in ((0, 111), (111, 111), (222, 74))]
UNITS = [(t, b) for t in range(len(ATT)) for b in range(4)]
AW = 111

CONST = {}


def _columns():
    at = 0
    for name, n in (("cos", SEQ), ("sin", SEQ), ("headmask", 2), ("ident", P), ("means", P), ("ones", P),
                    ("tri", P), ("attmask", AW), ("tri16", EXPERTS + 1), ("iota16", EXPERTS),
                    ("valid", RT)):
        CONST[name] = (at, n)
        at += n
    return at


NCONST = _columns()

VEC = {}


def _vcolumns():
    at = 0
    for name, n in (("ffn_bias", DB), ("conv_b", IB), ("ln_g", IB), ("ln_b", IB), ("fc_b", DB),
                    ("cproj_b", IB)):
        VEC[name] = (at, n)
        at += n
    return at


NVEC = _vcolumns()

def _jobs():
    v, a = [], []
    v += [("spec_a", part, j) for part in range(2) for j in range(DB)]
    v += [("spec_m", d) for d in range(DB)]
    a += [("tok", h, m) for h in range(2) for m in range(DB)]

    def norm(n):
        a.extend([("var", n, 0), ("var", n, 1)])
        return [("mean", n, 0), ("mean", n, 1)]
    v += norm(0)
    v += [(x, h, m, r) for h in range(2) for m in range(DB) for x in ("q", "k") for r in range(2)]
    a += [("v", t) for t in range(len(ATT))]
    for u in range(len(UNITS) + 4):
        if u < len(UNITS):
            v.append(("score", u))
        if 0 <= u - 2 < len(UNITS):
            a.append(("pt", u - 2))
        if u >= 4 and (u - 4) % 4 == 3:
            a.append(("ot", (u - 4) // 4))
    v += [("wo", h, m) for h in range(2) for m in range(DB)]
    v += norm(1)
    v += [("ffn", h, m) for h in range(2) for m in range(DB)]
    v += norm(2)
    v += [("inh", h, m) for h in range(2) for m in range(IB)]
    a += [("gate", h, m) for h in range(2) for m in range(IB)]
    v += [("conv", h, m) for h in range(2) for m in range(IB)]
    v += norm(3)
    a += [("fc", h, m) for h in range(2) for m in range(DB)]
    v += [("cproj", h, m) for h in range(2) for m in range(IB)]
    v += [("out", h, m) for h in range(2) for m in range(DB)]
    v += norm(4)
    v += [("logits",), ("pos",), ("offset",), ("gt", 0), ("gt", 1)]
    v += [("b2", t) for t in range(RT)]
    a += [("xrow", t) for t in range(RT)] + [("hrow", t) for t in range(RT)]
    return v, a


VJOBS, AJOBS = _jobs()
VNUM = {k: n for n, k in enumerate(VJOBS)}
ANUM = {k: n for n, k in enumerate(AJOBS)}
VBANKS = ABANKS = 3


def vit_tower_kernel(nc, patches, spec_w, spec_c, tok_w, tok_add, tok_sel, attn_w, consts, vecs,
                     inproj_w, conv_w, fc_w, cproj_w, out_w, router_w, router_b, experts, b2,
                     out):
    ctx = ExitStack()
    with ctx:
        def sb(name, shape, dt=F32):
            return ctx.enter_context(nc.sbuf_tensor(name, shape, dt))

        def sem(name):
            return ctx.enter_context(nc.semaphore(name))

        slot_rows = nc.dram_tensor("slot_rows", [SLOTS, D], F32).ap()

        cst = sb("cst", [P, NCONST])
        vec = sb("vec", [P, NVEC])
        spec = sb("spec", [P, 5 * DB * D])
        specw = spec[:, 0:2 * DB * D].rearrange("p (x k n) -> p x k n", x=2, k=DB)
        specc = spec[:, 2 * DB * D:].rearrange("p (x k n) -> p x k n", x=3, k=DB)
        late = sb("late", [P, PB * D + DB * 2 * INNER + IB * TAPS * P + IB * D + DB * INNER])
        parts, at = [], 0
        for k, n in ((PB, D), (DB, 2 * INNER), (IB * TAPS, P), (IB, D), (DB, INNER)):
            parts.append(late[:, at:at + k * n].rearrange("p (k n) -> p k n", k=k))
            at += k * n
        tokw, inw, convw, fcw, cprojw = parts
        convw = convw.rearrange("p (m t) n -> p m t n", t=TAPS)
        xsT = late[:, 0:(TILES + AHEAD) * D].rearrange("p (j k n) -> p j k n", k=DB, n=P)
        tokadd = sb("tokadd", [SEQ + 2, D])
        toksel = sb("toksel", [SEQ + 2, HALF])
        attnm = sb("attnm", [P, 6 * DB * D])
        attnw = attnm[:, :].rearrange("p (x k n) -> p x k n", x=6, k=DB)
        outw = sb("outw", [P, IB, D])
        routerw = sb("routerw", [P, DB, EXPERTS])
        routerb = sb("routerb", [1, EXPERTS])
        b2s = sb("b2s", [EXPERTS, D])
        wexp = sb("wexp", [P, RING, WCOLS])

        patchm = sb("patchm", [P, PB * TOKENS])
        xpatch = patchm[:, :].rearrange("p (k n) -> p k n", k=PB)
        sc = patchm[0:AW, 0:3 * 4 * AW].rearrange("p (x n) -> p x n", x=3)
        pr = patchm[0:AW, 12 * AW:20 * AW].rearrange("p (x n) -> p x n", x=2)
        prT = patchm[0:AW, 20 * AW:28 * AW].rearrange("p (x n) -> p x n", x=2)
        res = patchm[:, 0:IB * TOKENS].rearrange("p (k n) -> p k n", k=IB)
        base = patchm[:, 0:RT * D].rearrange("p (t c) -> p t c", t=RT)
        xrow = patchm[:, RT * D:2 * RT * D].rearrange("p (t c) -> p t c", t=RT)
        vaug = spec[0:AW, 0:len(ATT) * HEADS * (HD + 1)].rearrange("p (t a d) -> p t a d", t=len(ATT), a=HEADS)
        gate = spec[:, 0:IB * TOKENS].rearrange("p (k n) -> p k n", k=IB)
        hn = gate
        got = spec[:, 0:RT * D].rearrange("p (t c) -> p t c", t=RT)
        got2 = spec[:, RT * D:2 * RT * D].rearrange("p (t c) -> p t c", t=RT)
        keym = sb("keym", [P, 2 * IB * HALF])
        sq = keym[:, :].rearrange("p (h k n) -> p h k n", h=2, k=IB)
        kT = keym[:, :].rearrange("p (k e n) -> p k e n", k=DB, e=2)
        hid = keym[:, 0:HB * P].rearrange("p (m n) -> p m n", m=HB)
        hpad = attnm[:, 0:IB * IMAGES * PADSEQ].rearrange("p (k i s) -> p k i s", k=IB, i=IMAGES)
        hT = sb("hT", [P, DB, TOKENS])
        xn = sb("xn", [P, DB, TOKENS])
        fcs = xn
        cen = sb("cen", [P, IB, TOKENS])
        qT = cen[:, 0:2, :]
        oT = cen[:, 2:4, :]
        std = sb("std", [P, 2, HALF])
        rstd = sb("rstd", [P, 2, HALF])
        eps = sb("eps", [P, 1])
        spa = sb("spa", [P, 2, DB, D])
        specm = sb("specm", [P, DB, D])
        kr = sb("kr", [P, HALF])
        rot1 = sb("rot1", [P, HALF])
        rot2 = sb("rot2", [P, HALF])
        identb = sb("identb", [P, P], BF16)
        maskb = sb("maskb", [AW, 4, AW], BF16)
        smax = sb("smax", [AW, 3, 4])
        rden = sb("rden", [AW, 2, HEADS])
        onorm = sb("onorm", [AW, 2, D])
        prob = sb("prob", [P, RT, EXPERTS])
        rtmp = sb("rtmp", [P, RT, EXPERTS])
        pick = sb("pick", [P, 2, RT, EXPERTS])
        both = sb("both", [P, RT, EXPERTS])
        gates = sb("gates", [P, RT, EXPERTS])
        slotv = sb("slotv", [P, RT, EXPERTS])
        obase = sb("obase", [P, EXPERTS])
        red = sb("red", [P, 6, RT])
        gsel = sb("gsel", [P, 2, RT])
        slot = sb("slot", [P, 2, RT], I32)
        extra = sb("extra", [EXPERTS, 2])
        count = sb("count", [EXPERTS, 1])
        extrab = sb("extrab", [EXPERTS, P])
        gT = sb("gT", [EXPERTS, TOKENS])
        starts = sb("starts", [1, EXPERTS + 1], I32)
        xs = sb("xs", [P, AHEAD + 1, D])
        ysb = sb("ysb", [P, D])
        zeros = ysb[:, :]

        def c(name, rows=P):
            at, n = CONST[name]
            return cst[0:rows, at:at + n]

        def vcol(name, m):
            at, _ = VEC[name]
            return vec[:, at + m:at + m + 1]

        bank = [ctx.enter_context(nc.psum_tensor(f"bank{i}", [P, 512], F32)) for i in range(8)]
        vbank, abank, obank = bank[0:3], bank[3:6], bank[6:8]

        xs_bank, up_bank_a, up_bank_b, y_bank = bank[2], bank[3], bank[0], bank[6]

        def vb(key):
            return vbank[VNUM[key] % VBANKS]

        def ab(key):
            return abank[ANUM[key] % ABANKS]

        const_in, spec_in, tok_in, attn_in, rest_in = (
            sem(n) for n in ("const_in", "spec_in", "tok_in", "attn_in", "rest_in"))
        v_full, v_read = sem("v_full"), sem("v_read")
        a_full, a_read = sem("a_full"), sem("a_read")
        squared = sem("squared")
        xn_ready = sem("xn_ready")
        k_rotated = sem("k_rotated")
        k_split = sem("k_split")
        eps_ready = sem("eps_ready")
        vaug_ones = sem("vaug_ones")
        hpad_zero = sem("hpad_zero")
        zeros_ready = sem("zeros_ready")
        bf16_consts = sem("bf16_consts")
        q_ready = sem("q_ready")
        probs_ready = sem("probs_ready")
        pv_done = sem("pv_done")
        o_ready = sem("o_ready")
        dve_step = sem("dve_step")
        shifted = sem("shifted")
        exped = sem("exped")
        picked = sem("picked")
        slots_ready = sem("slots_ready")
        scattered = sem("scattered")
        w_in = [sem(f"w_in{i}") for i in range(RING)]
        xs_first = [sem(f"xs_first{i}") for i in range(AHEAD)]
        xs_in = sem("xs_in")
        xs_turned = sem("xs_turned")
        xs_copied = sem("xs_copied")
        up_a, up_b = sem("up_a"), sem("up_b")
        relu_a, relu_b = sem("relu_a"), sem("relu_b")
        down = sem("down")
        y_ready = sem("y_ready")
        y_out = sem("y_out")
        rows_stored = sem("rows_stored")
        gathered = sem("gathered")
        final = sem("final")
        stored = sem("stored")

        block = ctx.enter_context(nc.Block())

        def tiles_of(eng, e):
            return (eng.value_load(starts[0:1, bass.ds(e, 1)], min_val=0, max_val=TILES - 1),
                    eng.value_load(starts[0:1, bass.ds(e + 1, 1)], min_val=1, max_val=TILES))

        @block.sync
        def _(sp):
            sp.dma_start(cst[:, :], consts).then_inc(const_in, 16)
            sp.dma_start(specw[:, :, :, :], spec_w).then_inc(spec_in, 16)
            sp.dma_start(specc[:, :, :, :], spec_c).then_inc(spec_in, 16)
            sp.dma_start(tokw, tok_w).then_inc(tok_in, 16)
            sp.dma_start(tokadd[:, :], tok_add).then_inc(tok_in, 16)
            sp.dma_start(toksel[:, :], tok_sel).then_inc(tok_in, 16)
            sp.dma_start(xpatch, patches).then_inc(tok_in, 16)
            sp.dma_start(attnw[:, :, :, :], attn_w).then_inc(attn_in, 16)
            sp.dma_start(vec[:, :], vecs).then_inc(rest_in, 16)
            sp.dma_start(inw, inproj_w).then_inc(rest_in, 16)
            sp.dma_start(convw, conv_w).then_inc(rest_in, 16)
            sp.dma_start(fcw, fc_w).then_inc(rest_in, 16)
            sp.dma_start(cprojw, cproj_w).then_inc(rest_in, 16)
            sp.dma_start(outw[:, :, :], out_w).then_inc(rest_in, 16)
            sp.dma_start(routerw[:, :, :], router_w).then_inc(rest_in, 16)
            sp.dma_start(routerb[:, :], router_b).then_inc(rest_in, 16)
            sp.dma_start(b2s[:, :], b2).then_inc(rest_in, 16)
            for e in range(RING):
                sp.dma_start(wexp[:, e, :], experts[e]).then_inc(w_in[e], 16)
            sp.wait_ge(zeros_ready, 1)
            sp.dma_start(slot_rows.rearrange("(t p) c -> p t c", p=P),
                         zeros.unsqueeze(1).to_broadcast([P, SLOTS // P, D])).then_inc(y_out, 16)
            sp.wait_ge(scattered, 2 * RT * 16)
            for j in range(AHEAD):
                sp.dma_start(xs[:, j, :], slot_rows[j * P:(j + 1) * P, :]).then_inc(xs_first[j], 16)
            sp.dma_start(xs[:, AHEAD, :], slot_rows[AHEAD * P:(AHEAD + 1) * P, :]).then_inc(xs_in, 16)
            sp.wait_ge(slots_ready, 1)

            def expert(e, u, following):
                first, end = tiles_of(sp, e)
                with sp.Fori(first, end) as j:
                    sp.wait_ge(xs_turned, j + (AHEAD + 1))
                    sp.dma_start(xs[:, AHEAD, :], slot_rows[bass.ds((j + (AHEAD + 1)) * P, P), :]).then_inc(xs_in, 16)
                    sp.wait_ge(y_ready, j + 1)
                    sp.dma_start(slot_rows[bass.ds(j * P, P), :], ysb[:, :]).then_inc(y_out, 16)
                if following is not None:
                    sp.dma_start(wexp[:, u, :], experts[bass.ds(following, 1)].rearrange("o p c -> (o p) c")
                                 ).then_inc(w_in[u], 16)
                return end

            with sp.Fori(0, EXPERTS // RING - 1) as g:
                for u in range(RING):
                    expert(g * RING + u, u, g * RING + (RING + u))
            for u in range(RING):
                end = expert(EXPERTS - RING + u, u, None)
            sp.wait_ge(xs_in, end * 16 + 16)
            for t in range(RT):
                sp.wait_ge(final, t + 1)
                sp.dma_start(out[t * P:t * P + ROWS[t], :], base[0:ROWS[t], t, :]).then_inc(stored, 16)
            sp.wait_ge(stored, 16 * RT)

        @block.gpsimd
        def _(pool):
            nc.gpsimd.memset(eps[:, :], EPS).then_inc(eps_ready, 1)
            pool.wait_ge(v_full, VNUM["spec_m", 1] + 1)
            nc.gpsimd.memset(vaug, 1.0).then_inc(vaug_ones, 1)
            pool.wait_ge(v_full, VNUM["wo", 1, 1] + 1)
            nc.gpsimd.memset(hpad, 0.0).then_inc(hpad_zero, 1)
            pool.wait_ge(slots_ready, 1)
            pool.wait_ge(y_out, 16)
            for t in range(RT):
                pool.wait_ge(a_read, ANUM["xrow", t] + 1)
                for k in range(2):
                    nc.gpsimd.indirect_dma_start(
                        out=slot_rows, out_offset=bass.IndirectOffsetOnAxis(slot[0:ROWS[t], k, t:t + 1], 0),
                        in_=xrow[0:ROWS[t], t, :], in_offset=None).then_inc(scattered, 16)
            pool.wait_ge(slots_ready, 1)
            _, end = tiles_of(pool, EXPERTS - 1)
            pool.wait_ge(y_out, end * 16 + 16)
            pool.sem_inc(rows_stored, 1)
            pool.wait_ge(rows_stored, 1)
            for t in range(RT):
                for k, g in enumerate((got, got2)):
                    nc.gpsimd.indirect_dma_start(
                        out=g[0:ROWS[t], t, :], out_offset=None, in_=slot_rows,
                        in_offset=bass.IndirectOffsetOnAxis(slot[0:ROWS[t], k, t:t + 1], 0)
                    ).then_inc(gathered, 16)
            pool.wait_ge(gathered, 32 * RT)
            pool.wait_ge(stored, 16 * RT)

        @block.tensor
        def _(pe):
            order = {"v": 0, "a": 0}

            def fill(key):
                if key in VNUM:
                    n = VNUM[key]
                    assert n == order["v"], (key, n, order)
                    order["v"] += 1
                    if n >= VBANKS:
                        pe.wait_ge(v_read, n - VBANKS + 1)
                    return vb(key)
                n = ANUM[key]
                assert n == order["a"], (key, n, order)
                order["a"] += 1
                if n >= ABANKS:
                    pe.wait_ge(a_read, n - ABANKS + 1)
                return ab(key)

            def linear(key, dst, lhs, rhs, more=None):
                pairs = list(zip(lhs, rhs)) + (more or [])
                for k, (l, r) in enumerate(pairs):
                    mm = nc.tensor.matmul(dst, l, r, start=k == 0, stop=k == len(pairs) - 1)
                mm.then_inc(v_full if key in VNUM else a_full, 1)

            def cols(h):
                return slice(h * HALF, (h + 1) * HALF)

            ident, means = c("ident"), c("means")

            def norm_sums(n, src, blocks, ready):
                for h in range(2):
                    ready(h)
                    b = fill(("mean", n, h))
                    linear(("mean", n, h), b[:, 0:HALF], [means] * blocks,
                           [src[:, k, cols(h)] for k in range(blocks)])
                for h in range(2):
                    b = fill(("var", n, h))
                    pe.wait_ge(squared, 2 * n + h + 1)
                    linear(("var", n, h), b[:, 0:HALF], [means] * blocks,
                           [sq[:, h, k, :] for k in range(blocks)])

            pe.wait_ge(spec_in, 32)
            wr, wi = specw[:, 0], specw[:, 1]
            co, si, ns = specc[:, 0], specc[:, 1], specc[:, 2]
            for part in range(2):
                for j in range(DB):
                    b = fill(("spec_a", part, j))
                    js = slice(j * P, (j + 1) * P)
                    first, second = ((wr, co), (wi, si)) if part == 0 else ((wi, co), (wr, ns))
                    linear(("spec_a", part, j), b[:, 0:D],
                           [w[:, k, js] for w, _ in (first, second) for k in range(DB)],
                           [f[:, k, :] for _, f in (first, second) for k in range(DB)])
            pe.wait_ge(v_read, VNUM["spec_a", 1, 1] + 1)
            for d in range(DB):
                b = fill(("spec_m", d))
                ds = slice(d * P, (d + 1) * P)
                linear(("spec_m", d), b[:, 0:D],
                       [spa[:, part, k, ds] for part in range(2) for k in range(DB)],
                       [f[:, k, :] for f in (co, ns) for k in range(DB)])

            pe.wait_ge(tok_in, 64)
            for h in range(2):
                for m in range(DB):
                    b = fill(("tok", h, m))
                    ms = slice(m * P, (m + 1) * P)
                    linear(("tok", h, m), b[:, 0:HALF], [tokw[:, k, ms] for k in range(PB)],
                           [xpatch[:, k, cols(h)] for k in range(PB)],
                           [(tokadd[:, ms], toksel[:, :])])

            pe.wait_ge(const_in, 16)
            norm_sums(0, hT, DB, lambda h: pe.wait_ge(a_read, ANUM["tok", h, 1] + 1))

            pe.wait_ge(attn_in, 16)
            for h in range(2):
                pe.wait_ge(xn_ready, h + 1)
                for m in range(DB):
                    ms = slice(m * P, (m + 1) * P)
                    for x in ("q", "k"):
                        for r in range(2):
                            w = attnw[:, 2 * (x == "k") + r]
                            b = fill((x, h, m, r))
                            linear((x, h, m, r), b[:, 0:HALF], [w[:, k, ms] for k in range(DB)],
                                   [xn[:, k, cols(h)] for k in range(DB)])
            for t, (c0, n) in enumerate(ATT):
                b = fill(("v", t))
                linear(("v", t), b[0:n, 0:D], [xn[:, k, c0:c0 + n] for k in range(DB)],
                       [attnw[:, 4, k, :] for k in range(DB)])

            pe.wait_ge(bf16_consts, 2)
            pe.wait_ge(k_split, 4)
            pe.wait_ge(q_ready, 4)
            for u in range(len(UNITS) + 4):
                if u < len(UNITS):
                    t, pair = UNITS[u]
                    c0, n = ATT[t]
                    b = fill(("score", u))
                    nc.tensor.matmul(b[0:n, 0:4 * n].rearrange("p (a q) -> p a q", a=4), identb[0:n, 0:n],
                                     maskb[0:n, :, 0:n], start=True, stop=False)
                    ps = slice(32 * pair, 32 * pair + 32)
                    for half in range(2):
                        mm = nc.tensor.matmul(
                            b[0:n, 2 * n * half:2 * n * (half + 1)].rearrange("p (a q) -> p a q", a=2),
                            qT[ps, half, c0:c0 + n], kT[ps, half, :, c0:c0 + n],
                            start=False, stop=half == 1)
                    mm.then_inc(v_full, 1)
                if 0 <= u - 2 < len(UNITS):
                    w = u - 2
                    n = ATT[UNITS[w][0]][1]
                    b = fill(("pt", w))
                    pe.wait_ge(probs_ready, w + 1)
                    for a in range(4):
                        mm = nc.tensor.transpose(b[0:n, a * n:(a + 1) * n], pr[0:n, w % 2, a * n:(a + 1) * n],
                                                 ident[0:n, 0:n])
                    mm.then_inc(a_full, 1)
                if 0 <= u - 3 < len(UNITS):
                    w = u - 3
                    t, pair = UNITS[w]
                    n = ATT[t][1]
                    pe.wait_ge(a_read, ANUM["pt", w] + 1)
                    if pair == 0 and t >= 2:
                        pe.wait_ge(o_ready, t - 1)
                    for a in range(4):
                        head = 8 * (a // 2) + 2 * pair + a % 2
                        mm = nc.tensor.matmul(obank[t % 2][0:n, head * (HD + 1):(head + 1) * (HD + 1)],
                                              prT[0:n, w % 2, a * n:(a + 1) * n], vaug[0:n, t, head, :],
                                              start=True, stop=True)
                    mm.then_inc(pv_done, 1)
                if u >= 4 and (u - 4) % 4 == 3:
                    t = (u - 4) // 4
                    n = ATT[t][1]
                    b = fill(("ot", t))
                    pe.wait_ge(o_ready, t + 1)
                    for m in range(DB):
                        mm = nc.tensor.transpose(b[:, m * n:(m + 1) * n], onorm[0:n, t % 2, m * P:(m + 1) * P],
                                                 ident[0:n, 0:n])
                    mm.then_inc(a_full, 1)

            def halves(name, blocks, w, src, depth, ready):
                for h in range(2):
                    ready(h)
                    for m in range(blocks):
                        b = fill((name, h, m))
                        linear((name, h, m), b[:, 0:HALF], [w[:, k, m * P:(m + 1) * P] for k in range(depth)],
                               [src[:, k, cols(h)] for k in range(depth)])

            halves("wo", DB, attnw[:, 5], oT, DB, lambda h: pe.wait_ge(a_read, ANUM["ot", 3 * h + 2] + 1))
            norm_sums(1, hT, DB, lambda h: pe.wait_ge(v_read, VNUM["wo", h, 1] + 1))
            halves("ffn", DB, specm[:, :, :], xn, DB, lambda h: pe.wait_ge(xn_ready, 2 + h + 1))
            norm_sums(2, hT, DB, lambda h: pe.wait_ge(v_read, VNUM["ffn", h, 1] + 1))

            pe.wait_ge(rest_in, 9 * 16)
            for h in range(2):
                pe.wait_ge(xn_ready, 4 + h + 1)
                for part, name in enumerate(("inh", "gate")):
                    for m in range(IB):
                        b = fill((name, h, m))
                        linear((name, h, m), b[:, 0:HALF],
                               [inw[:, k, part * INNER + m * P:part * INNER + (m + 1) * P] for k in range(DB)],
                               [xn[:, k, cols(h)] for k in range(DB)])
            for h in range(2):
                for m in range(IB):
                    b = fill(("conv", h, m))
                    pe.wait_ge(v_read, VNUM["inh", h, m] + 1)
                    linear(("conv", h, m), b[:, 0:HALF].rearrange("p (i s) -> p i s", s=SEQ),
                           [convw[:, m, tap, :] for tap in range(TAPS)],
                           [hpad[:, m, 8 * h:8 * h + 8, tap:tap + SEQ] for tap in range(TAPS)])
            norm_sums(3, res, IB, lambda h: pe.wait_ge(v_read, VNUM["conv", h, 3] + 1))
            halves("fc", DB, fcw, hn, IB, lambda h: pe.wait_ge(xn_ready, 6 + h + 1))
            halves("cproj", IB, cprojw, fcs, DB, lambda h: pe.wait_ge(a_read, ANUM["fc", h, 1] + 1))
            halves("out", DB, outw, cen, IB, lambda h: pe.wait_ge(v_read, VNUM["cproj", h, 3] + 1))
            norm_sums(4, hT, DB, lambda h: pe.wait_ge(v_read, VNUM["out", h, 1] + 1))

            pe.wait_ge(xn_ready, 10)
            b = fill(("logits",))
            for t in range(RT):
                ts = slice(t * P, t * P + ROWS[t])
                for k in range(DB):
                    nc.tensor.matmul(b[0:ROWS[t], t * EXPERTS:(t + 1) * EXPERTS], xn[:, k, ts],
                                     routerw[:, k, :], start=k == 0, stop=False)
                mm = nc.tensor.matmul(b[0:ROWS[t], t * EXPERTS:(t + 1) * EXPERTS], c("ones", 1)[:, 0:ROWS[t]], routerb[:, :], start=False, stop=True)
            mm.then_inc(v_full, 1)
            for name, src in (("xrow", xn), ("hrow", hT)):
                for t in range(RT):
                    b = fill((name, t))
                    for m in range(DB):
                        mm = nc.tensor.transpose(b[0:ROWS[t], m * P:(m + 1) * P],
                                                 src[:, m, t * P:t * P + ROWS[t]], ident)
                    mm.then_inc(a_full, 1)
            pe.wait_ge(picked, 1)
            b = fill(("pos",))
            for t in range(RT):
                for s in range(t + 1):
                    nc.tensor.matmul(b[:, t * EXPERTS:(t + 1) * EXPERTS],
                                     c("tri") if s == t else c("ones"),
                                     both[:, s, :], start=s == 0, stop=s == t)
            for t in range(RT):
                mm = nc.tensor.matmul(b[0:EXPERTS, RT * EXPERTS:RT * EXPERTS + 1], both[:, t, :],
                                      c("ones")[:, 0:1], start=t == 0, stop=t == RT - 1)
            mm.then_inc(v_full, 1)
            pe.wait_ge(picked, 2)
            b = fill(("offset",))
            linear(("offset",), b[:, 0:EXPERTS + 1], [extrab[:, :]], [c("tri16", EXPERTS)])
            for g in range(2):
                b = fill(("gt", g))
                for t in ((0, 1, 2, 3), (4,))[g]:
                    mm = nc.tensor.transpose(b[0:EXPERTS, (t % 4) * P:(t % 4 + 1) * P], gates[:, t, :], ident)
                mm.then_inc(v_full, 1)
            for t in range(RT):
                b = fill(("b2", t))
                pe.wait_ge(v_read, VNUM["gt", t // 4] + 1)
                linear(("b2", t), b[0:ROWS[t], 0:D], [gT[:, t * P:t * P + ROWS[t]]], [b2s[:, :]])

            pe.wait_ge(v_read, len(VJOBS))
            pe.wait_ge(a_read, len(AJOBS))

            def turn(rows, j):
                for k in range(DB):
                    mm = nc.tensor.transpose(xs_bank[:, k * P:(k + 1) * P], rows[:, k * P:(k + 1) * P], ident)
                mm.then_inc(xs_turned, 1)

            for j in range(AHEAD):
                pe.wait_ge(xs_first[j], 16)
                if j:
                    pe.wait_ge(xs_copied, j)
                turn(xs[:, j, :], j)
            pe.wait_ge(slots_ready, 1)
            with pe.Fori(0, EXPERTS // RING) as g:
                for u in range(RING):
                    w1 = wexp[:, u, 0:DB * HIDDEN].rearrange("p (k n) -> p k n", k=DB)
                    w2 = wexp[:, u, DB * HIDDEN:DB * HIDDEN + HB * D].rearrange("p (m n) -> p m n", m=HB)
                    first, end = tiles_of(pe, g * RING + u)
                    with pe.Fori(first, end) as j:
                        pe.wait_ge(w_in[u], g * 16 + 16)
                        pe.wait_ge(xs_copied, j + 1)
                        for up_bank, full, m0 in ((up_bank_a, up_a, 0), (up_bank_b, up_b, 4)):
                            for i in range(4):
                                m = m0 + i
                                for k in range(DB):
                                    mm = nc.tensor.matmul(
                                        up_bank[:, i * P:(i + 1) * P], w1[:, k, m * P:(m + 1) * P],
                                        xsT[:, bass.ds(j, 1), k, :].rearrange("p j n -> p (j n)"),
                                        start=k == 0, stop=k == DB - 1)
                            mm.then_inc(full, 1)
                        pe.wait_ge(xs_in, j * 16 + 16)
                        pe.wait_ge(xs_copied, j + AHEAD)
                        turn(xs[:, AHEAD, :], j)
                        pe.wait_ge(relu_a, j + 1)
                        for m in range(HB):
                            if m == HB // 2:
                                pe.wait_ge(relu_b, j + 1)
                            mm = nc.tensor.matmul(y_bank[:, 0:D], hid[:, m, :], w2[:, m, :],
                                                  start=m == 0, stop=m == HB - 1)
                        mm.then_inc(down, 1)

        @block.scalar
        def _(act):
            def take(key):
                act.wait_ge(a_full, ANUM[key] + 1)
                return ab(key)

            def cols(h):
                return slice(h * HALF, (h + 1) * HALF)

            def squares(n, blocks):
                for h in range(2):
                    act.wait_ge(v_read, VNUM["mean", n, h] + 1)
                    nc.scalar.activation(sq[:, h, 0:blocks, :], cen[:, 0:blocks, cols(h)], ACT.Square
                                         ).then_inc(squared, 1)
                for h in range(2):
                    b = take(("var", n, h))
                    if n:
                        act.wait_ge(xn_ready, 2 * n - 1 + h)
                    nc.scalar.activation(std[:, h, :], b[:, 0:HALF], ACT.Sqrt, bias=eps[:, :],
                                         scale=D / (blocks * P)).then_inc(a_read, 1)

            for h in range(2):
                for m in range(DB):
                    b = take(("tok", h, m))
                    nc.scalar.activation(hT[:, m, cols(h)], b[:, 0:HALF], ACT.Copy).then_inc(a_read, 1)
            act.wait_ge(eps_ready, 1)
            squares(0, DB)
            act.wait_ge(const_in, 16)
            for h in range(2):
                for m in range(DB):
                    act.wait_ge(k_rotated, 2 * h + m + 1)
                    for e in range(2):
                        kk = nc.scalar.activation(kT[:, m, e, cols(h)], kr[:, :], ACT.Copy,
                                                  scale=c("headmask")[:, e:e + 1])
                    kk.then_inc(k_split, 1)
            act.wait_ge(vaug_ones, 1)
            for t, (c0, n) in enumerate(ATT):
                b = take(("v", t))
                nc.scalar.activation(vaug[0:n, t, :, 0:HD], b[0:n, 0:D].rearrange("p (a d) -> p a d", a=HEADS),
                                     ACT.Copy).then_inc(a_read, 1)
            for u in range(len(UNITS) + 4):
                if 0 <= u - 2 < len(UNITS):
                    w = u - 2
                    n = ATT[UNITS[w][0]][1]
                    b = take(("pt", w))
                    if w >= 2:
                        act.wait_ge(pv_done, w - 1)
                    nc.scalar.activation(prT[0:n, w % 2, 0:4 * n], b[0:n, 0:4 * n], ACT.Copy).then_inc(a_read, 1)
                if u < len(UNITS):
                    n = ATT[UNITS[u][0]][1]
                    act.wait_ge(v_read, VNUM["score", u] + 1)
                    nc.scalar.activation(pr[0:n, u % 2, 0:4 * n], sc[0:n, u % 3, 0:4 * n], ACT.Exp,
                                         scale=HD ** -0.5).then_inc(probs_ready, 1)
                if u >= 4 and (u - 4) % 4 == 3:
                    t = (u - 4) // 4
                    c0, n = ATT[t]
                    b = take(("ot", t))
                    nc.scalar.activation(oT[:, :, c0:c0 + n], b[:, 0:2 * n].rearrange("p (m n) -> p m n", m=2),
                                         ACT.Copy).then_inc(a_read, 1)
            squares(1, DB)
            squares(2, DB)
            for h in range(2):
                for m in range(IB):
                    b = take(("gate", h, m))
                    nc.scalar.activation(gate[:, m, cols(h)], b[:, 0:HALF], ACT.Silu).then_inc(a_read, 1)
            squares(3, IB)
            for h in range(2):
                for m in range(DB):
                    b = take(("fc", h, m))
                    nc.scalar.activation(fcs[:, m, cols(h)], b[:, 0:HALF], ACT.Silu, bias=vcol("fc_b", m)
                                         ).then_inc(a_read, 1)
            squares(4, DB)
            act.wait_ge(shifted, 1)
            nc.scalar.activation(rtmp[:, :, :], prob[:, :, :], ACT.Exp).then_inc(exped, 1)
            for name, dst in (("xrow", xrow), ("hrow", base)):
                for t in range(RT):
                    b = take((name, t))
                    nc.scalar.activation(dst[0:ROWS[t], t, :], b[0:ROWS[t], 0:D], ACT.Copy).then_inc(a_read, 1)

            act.wait_ge(slots_ready, 1)
            with act.Fori(0, EXPERTS // RING) as g:
                for u in range(RING):
                    b1 = wexp[:, u, WCOLS - HB:WCOLS]
                    first, end = tiles_of(act, g * RING + u)
                    with act.Fori(first, end) as j:
                        act.wait_ge(up_a, j + 1)
                        for i in range(4):
                            r = nc.scalar.activation(hid[:, i, :], up_bank_a[:, i * P:(i + 1) * P], ACT.Relu,
                                                     bias=b1[:, i:i + 1])
                        r.then_inc(relu_a, 1)
                        act.wait_ge(down, j + 1)
                        act.wait_ge(y_out, j * 16 + 16)
                        nc.scalar.activation(ysb[:, :], y_bank[:, 0:D], ACT.Copy).then_inc(y_ready, 1)

        @block.vector
        def _(dve):
            steps = [0]

            def then(ins):
                steps[0] += 1
                ins.then_inc(dve_step, 1)
                dve.wait_ge(dve_step, steps[0])

            def take(key):
                dve.wait_ge(v_full, VNUM[key] + 1)
                return vb(key)

            def cols(h):
                return slice(h * HALF, (h + 1) * HALF)

            def norm(n, x, blocks, dst):
                share = D / (blocks * P)
                for h in range(2):
                    b = take(("mean", n, h))
                    nc.vector.scalar_tensor_tensor(
                        out=cen[:, 0:blocks, cols(h)], in0=b[:, 0:HALF].unsqueeze(1).to_broadcast([P, blocks, HALF]),
                        scalar=-share, in1=x[:, :, cols(h)], op0=ALU.mult, op1=ALU.add).then_inc(v_read, 1)
                for h in range(2):
                    dve.wait_ge(a_read, ANUM["var", n, h] + 1)
                    then(nc.vector.reciprocal(rstd[:, h, :], std[:, h, :]))
                    r = nc.vector.tensor_tensor(dst[:, :, cols(h)], cen[:, 0:blocks, cols(h)],
                                                rstd[:, h, :].unsqueeze(1).to_broadcast([P, blocks, HALF]), ALU.mult)
                    if blocks == IB:
                        then(r)
                        for m in range(blocks):
                            r = nc.vector.tensor_scalar(dst[:, m, cols(h)], dst[:, m, cols(h)], vcol("ln_g", m),
                                                        vcol("ln_b", m), ALU.mult, ALU.add)
                    r.then_inc(xn_ready, 1)

            nc.vector.memset(zeros, 0.0).then_inc(zeros_ready, 1)
            then(nc.vector.memset(prob[:, :, :], 0.0))
            dve.wait_ge(const_in, 16)
            nc.vector.tensor_copy(identb[:, :], c("ident")).then_inc(bf16_consts, 1)
            nc.vector.tensor_copy(maskb[:, :, :], c("attmask", AW).unsqueeze(1).to_broadcast([AW, 4, AW])
                                  ).then_inc(bf16_consts, 1)
            for part in range(2):
                for j in range(DB):
                    b = take(("spec_a", part, j))
                    nc.vector.tensor_copy(spa[:, part, j, :], b[:, 0:D]).then_inc(v_read, 1)
            for d in range(DB):
                b = take(("spec_m", d))
                nc.vector.tensor_scalar(specm[:, d, :], b[:, 0:D], 1.0 / D, None, ALU.mult).then_inc(v_read, 1)
            norm(0, hT, DB, xn)
            for h in range(2):
                for m in range(DB):
                    for x in ("q", "k"):
                        if x == "k":
                            dve.wait_ge(q_ready, 2 * h + m + 1)
                        elif 2 * h + m:
                            dve.wait_ge(k_rotated, 2 * h + m)
                        for r, (tmp, table) in enumerate(((rot1, "cos"), (rot2, "sin"))):
                            b = take((x, h, m, r))
                            nc.vector.tensor_tensor(
                                tmp[:, :].rearrange("p (i s) -> p i s", s=SEQ),
                                b[:, 0:HALF].rearrange("p (i s) -> p i s", s=SEQ),
                                c(table).unsqueeze(1).to_broadcast([P, 8, SEQ]), ALU.mult).then_inc(v_read, 1)
                        dve.wait_ge(v_read, VNUM[x, h, m, 1] + 1)
                        if x == "q":
                            nc.vector.tensor_tensor(qT[:, m, cols(h)], rot1[:, :], rot2[:, :], ALU.add
                                                    ).then_inc(q_ready, 1)
                        else:
                            if 2 * h + m:
                                dve.wait_ge(k_split, 2 * h + m)
                            nc.vector.tensor_tensor(kr[:, :], rot1[:, :], rot2[:, :], ALU.add
                                                    ).then_inc(k_rotated, 1)
            for u in range(len(UNITS) + 4):
                if u < len(UNITS):
                    n = ATT[UNITS[u][0]][1]
                    b = take(("score", u))
                    s4 = b[0:n, 0:4 * n].rearrange("p (a q) -> p a q", a=4)
                    then(nc.vector.tensor_reduce(smax[0:n, u % 3, :], s4, AX.X, ALU.max))
                    if u >= 3:
                        dve.wait_ge(probs_ready, u - 2)
                    nc.vector.tensor_tensor(sc[0:n, u % 3, 0:4 * n].rearrange("p (a q) -> p a q", a=4), s4,
                                            smax[0:n, u % 3, :].unsqueeze(2).to_broadcast([n, 4, n]), ALU.subtract
                                            ).then_inc(v_read, 1)
                if 0 <= u - 3 < len(UNITS) and UNITS[u - 3][1] == 3:
                    t = UNITS[u - 3][0]
                    n = ATT[t][1]
                    dve.wait_ge(pv_done, u - 2)
                    o = obank[t % 2][0:n, 0:HEADS * (HD + 1)].rearrange("p (a d) -> p a d", a=HEADS)
                    then(nc.vector.reciprocal(rden[0:n, t % 2, :].unsqueeze(2), o[:, :, HD:HD + 1]))
                    if t >= 2:
                        dve.wait_ge(a_full, ANUM["ot", t - 2] + 1)
                    nc.vector.tensor_tensor(onorm[0:n, t % 2, :].rearrange("p (a d) -> p a d", a=HEADS),
                                            o[:, :, 0:HD],
                                            rden[0:n, t % 2, :].unsqueeze(2).to_broadcast([n, HEADS, HD]), ALU.mult
                                            ).then_inc(o_ready, 1)

            def add_to_stream(name, bias):
                for h in range(2):
                    for m in range(DB):
                        b = take((name, h, m))
                        if bias is None:
                            r = nc.vector.tensor_tensor(hT[:, m, cols(h)], b[:, 0:HALF], hT[:, m, cols(h)], ALU.add)
                        else:
                            r = nc.vector.scalar_tensor_tensor(
                                out=hT[:, m, cols(h)], in0=b[:, 0:HALF], scalar=vcol(bias, m),
                                in1=hT[:, m, cols(h)], op0=ALU.add, op1=ALU.add)
                        r.then_inc(v_read, 1)

            add_to_stream("wo", None)
            norm(1, hT, DB, xn)
            dve.wait_ge(rest_in, 9 * 16)
            add_to_stream("ffn", "ffn_bias")
            norm(2, hT, DB, xn)
            dve.wait_ge(hpad_zero, 1)
            for h in range(2):
                for m in range(IB):
                    b = take(("inh", h, m))
                    nc.vector.tensor_copy(hpad[:, m, 8 * h:8 * h + 8, TAPS - 1:PADSEQ],
                                          b[:, 0:HALF].rearrange("p (i s) -> p i s", s=SEQ)).then_inc(v_read, 1)
            for h in range(2):
                for m in range(IB):
                    b = take(("conv", h, m))
                    dve.wait_ge(a_read, ANUM["gate", h, m] + 1)
                    nc.vector.scalar_tensor_tensor(out=res[:, m, cols(h)], in0=b[:, 0:HALF], scalar=vcol("conv_b", m),
                                                   in1=gate[:, m, cols(h)], op0=ALU.add, op1=ALU.mult
                                                   ).then_inc(v_read, 1)
            norm(3, res, IB, hn)
            for h in range(2):
                for m in range(IB):
                    b = take(("cproj", h, m))
                    nc.vector.scalar_tensor_tensor(out=cen[:, m, cols(h)], in0=b[:, 0:HALF], scalar=vcol("cproj_b", m),
                                                   in1=res[:, m, cols(h)], op0=ALU.add, op1=ALU.add
                                                   ).then_inc(v_read, 1)
            add_to_stream("out", None)
            norm(4, hT, DB, xn)

            wide = [P, RT, EXPERTS]

            def each(x):
                return x.unsqueeze(2).to_broadcast(wide)

            def over_tiles(x):
                return x.unsqueeze(1).to_broadcast(wide)

            pb, tmp, iota = prob[:, :, :], rtmp[:, :, :], over_tiles(c("iota16"))
            b = take(("logits",))
            nc.vector.tensor_copy(prob[:, 0:4, :], b[:, 0:4 * EXPERTS].rearrange("p (t e) -> p t e", t=4))
            nc.vector.tensor_copy(prob[0:ROWS[4], 4, :], b[0:ROWS[4], 4 * EXPERTS:5 * EXPERTS]).then_inc(v_read, 1)
            dve.wait_ge(v_read, VNUM["logits",] + 1)
            then(nc.vector.tensor_reduce(red[:, 0, :], pb, AX.X, ALU.max))
            nc.vector.tensor_tensor(pb, pb, each(red[:, 0, :]), ALU.subtract).then_inc(shifted, 1)
            dve.wait_ge(exped, 1)
            then(nc.vector.tensor_reduce(red[:, 1, :], tmp, AX.X, ALU.add))
            then(nc.vector.reciprocal(red[:, 2, :], red[:, 1, :]))
            then(nc.vector.tensor_tensor(pb, tmp, each(red[:, 2, :]), ALU.mult))
            src = pb
            for k in range(2):
                then(nc.vector.tensor_reduce(gsel[:, k, :], src, AX.X, ALU.max))
                then(nc.vector.tensor_tensor(slotv[:, :, :], src, each(gsel[:, k, :]), ALU.is_equal))
                then(nc.vector.tensor_tensor(slotv[:, :, :], slotv[:, :, :], iota, ALU.mult))
                then(nc.vector.tensor_reduce(red[:, 3, :], slotv[:, :, :], AX.X, ALU.min))
                then(nc.vector.tensor_tensor(pick[:, k, :, :], iota, each(red[:, 3, :]), ALU.is_equal))
                if k == 0:
                    then(nc.vector.scalar_tensor_tensor(out=tmp, in0=pick[:, 0, :, :], scalar=-4.0, in1=pb,
                                                        op0=ALU.mult, op1=ALU.add))
                    src = tmp
            then(nc.vector.tensor_tensor(both[:, :, :], pick[:, 0, :, :], pick[:, 1, :, :], ALU.add))
            nc.vector.tensor_tensor(both[:, :, :], both[:, :, :], each(c("valid")), ALU.mult).then_inc(picked, 1)
            then(nc.vector.tensor_tensor(gates[:, :, :], pick[:, 0, :, :], each(gsel[:, 0, :]), ALU.mult))
            then(nc.vector.tensor_tensor(tmp, pick[:, 1, :, :], each(gsel[:, 1, :]), ALU.mult))
            then(nc.vector.tensor_tensor(gates[:, :, :], gates[:, :, :], tmp, ALU.add))
            b = take(("pos",))
            nc.vector.tensor_copy(slotv[:, :, :], b[:, 0:RT * EXPERTS].rearrange("p (t e) -> p t e", t=RT))
            nc.vector.tensor_copy(count[:, :], b[0:EXPERTS, RT * EXPERTS:RT * EXPERTS + 1]).then_inc(v_read, 1)
            dve.wait_ge(v_read, VNUM["pos",] + 1)
            then(nc.vector.tensor_scalar(extra[:, 0:1], count[:, :], float(P), 1.0, ALU.is_gt, ALU.add))
            last = (TOKENS - 1) // P
            for k in range(2, last + 1):
                then(nc.vector.scalar_tensor_tensor(
                    out=extra[:, (k - 1) % 2:(k - 1) % 2 + 1], in0=count[:, :], scalar=float(k * P),
                    in1=extra[:, k % 2:k % 2 + 1], op0=ALU.is_gt, op1=ALU.add))
            nc.vector.tensor_copy(extrab[:, :], extra[:, (last - 1) % 2:(last - 1) % 2 + 1].to_broadcast([EXPERTS, P])
                                  ).then_inc(picked, 1)
            b = take(("offset",))
            nc.vector.tensor_copy(starts[:, :], b[0:1, 0:EXPERTS + 1])
            nc.vector.tensor_scalar(obase[:, :], b[:, 0:EXPERTS], float(P), None, ALU.mult).then_inc(v_read, 1)
            dve.wait_ge(v_read, VNUM["offset",] + 1)
            then(nc.vector.tensor_tensor(slotv[:, :, :], slotv[:, :, :], over_tiles(obase[:, :]), ALU.add))
            for k in range(2):
                then(nc.vector.tensor_tensor(tmp, slotv[:, :, :], pick[:, k, :, :], ALU.mult))
                then(nc.vector.tensor_reduce(red[:, 4 + k, :], tmp, AX.X, ALU.add))
            nc.vector.tensor_copy(slot[:, :, :], red[:, 4:6, :]).then_inc(slots_ready, 1)
            for g, n in ((0, 4 * P), (1, ROWS[4])):
                b = take(("gt", g))
                nc.vector.tensor_copy(gT[:, 4 * P * g:4 * P * g + n], b[0:EXPERTS, 0:n]).then_inc(v_read, 1)
            for t in range(RT):
                b = take(("b2", t))
                dve.wait_ge(a_read, ANUM["hrow", t] + 1)
                rows = base[0:ROWS[t], t, :]
                nc.vector.tensor_tensor(rows, b[0:ROWS[t], 0:D], rows, ALU.add).then_inc(v_read, 1)

            def copy_rows(tile):
                nc.vector.tensor_copy(xsT[:, bass.ds(tile, 1), :, :].rearrange("p j k n -> p (j k) n"),
                                      xs_bank[:, 0:D].rearrange("p (k n) -> p k n", k=DB)).then_inc(xs_copied, 1)

            for j in range(AHEAD):
                dve.wait_ge(xs_turned, j + 1)
                copy_rows(j)
            dve.wait_ge(slots_ready, 1)
            with dve.Fori(0, EXPERTS // RING) as g:
                for u in range(RING):
                    b1 = wexp[:, u, WCOLS - HB:WCOLS]
                    first, end = tiles_of(dve, g * RING + u)
                    with dve.Fori(first, end) as j:
                        dve.wait_ge(up_b, j + 1)
                        for i in range(4):
                            r = nc.vector.tensor_scalar(hid[:, 4 + i, :], up_bank_b[:, i * P:(i + 1) * P],
                                                        b1[:, 4 + i:5 + i], 0.0, ALU.add, ALU.max)
                        r.then_inc(relu_b, 1)
                        dve.wait_ge(xs_turned, j + (AHEAD + 1))
                        copy_rows(j + AHEAD)
            dve.wait_ge(gathered, 32 * RT)
            for t in range(RT):
                rows = base[0:ROWS[t], t, :]
                then(nc.vector.scalar_tensor_tensor(out=rows, in0=got[0:ROWS[t], t, :],
                                                    scalar=gsel[0:ROWS[t], 0, t:t + 1], in1=rows,
                                                    op0=ALU.mult, op1=ALU.add))
                nc.vector.scalar_tensor_tensor(out=rows, in0=got2[0:ROWS[t], t, :],
                                               scalar=gsel[0:ROWS[t], 1, t:t + 1], in1=rows,
                                               op0=ALU.mult, op1=ALU.add).then_inc(final, 1)


def _constants():
    k = np.arange(D)
    angle = 2 * np.pi * ((k[:, None] * k[None, :]) % D) / D
    dft = np.stack([np.cos(angle), np.sin(angle), -np.sin(angle)]).astype(np.float32)
    inv = (1.0 / 10000.0 ** (np.arange(0, HD, 2, dtype=np.float32) / HD)).astype(np.float32)
    freq = np.arange(SEQ, dtype=np.float32)[:, None] * inv[None, :]
    feature = np.arange(P) % HD
    block = {}
    block["cos"] = np.cos(freq)[:, feature % (HD // 2)].T
    block["sin"] = (np.sin(freq)[:, feature % (HD // 2)] * np.where(feature < HD // 2, -1.0, 1.0)[None, :]).T
    p = np.arange(P)
    block["headmask"] = np.stack([(p // HD) % 2 == 0, (p // HD) % 2 == 1], 1)
    block["ident"] = np.eye(P)
    block["means"] = np.full((P, P), 1.0 / D)
    block["ones"] = np.ones((P, P))
    block["tri"] = p[:, None] < p[None, :]
    q = np.arange(AW)
    seen = (q[:, None] // SEQ == q[None, :] // SEQ) & (q[None, :] <= q[:, None])
    mask = np.zeros((P, AW))
    mask[:AW] = np.where(seen, 0.0, -1e30)
    block["attmask"] = mask
    e = np.arange(EXPERTS)
    tri16 = np.zeros((P, EXPERTS + 1))
    tri16[:EXPERTS] = e[:, None] < np.arange(EXPERTS + 1)[None, :]
    block["tri16"] = tri16
    block["iota16"] = np.tile(e - EXPERTS, (P, 1))
    block["valid"] = np.stack([p < r for r in ROWS], 1)
    consts = np.zeros((P, NCONST), np.float32)
    for name, (at, n) in CONST.items():
        consts[:, at:at + n] = block[name]
    sel = np.zeros((SEQ + 2, HALF), np.float32)
    s = np.arange(HALF) % SEQ
    sel[s, np.arange(HALF)] = 1.0
    sel[SEQ] = s > 0
    sel[SEQ + 1] = s == 0
    return dft, consts, sel


def _blocks(w):
    return w.reshape(-1, P, w.shape[1]).transpose(1, 0, 2)


def kernel(**inputs):
    import numpy as _np
    import concourse.bacc as _bacc
    from concourse import mybir as _mybir
    from concourse.bass_utils import run_bass_kernel_spmd as _run

    g = {k: _np.asarray(v) for k, v in inputs.items()}
    dft, consts, sel = _constants()

    x = g["x"].reshape(IMAGES, 3, 6, 16, 6, 16).transpose(1, 3, 5, 0, 2, 4).reshape(PATCH, IMAGES, SEQ - 1)
    patches = _np.zeros((PATCH, IMAGES, SEQ), _np.float32)
    patches[:, :, 1:] = x
    tok_add = _np.concatenate([g["L0_tok_position_embeddings"][0], g["L0_tok_b_lin"][None],
                               g["L0_tok_class_token"][0]], 0)
    swap = (_np.arange(D) // HD) * HD + (_np.arange(D) + HD // 2) % HD
    wq, wk = g["L0_attn_Wq"], g["L0_attn_Wk"]
    attn_w = _np.stack([_blocks(w.T) for w in (wq, wq[swap], wk, wk[swap], g["L0_attn_Wv"], g["L0_attn_Wo"])], 1)
    cw = g["L1_attn_conv_w"].reshape(IB, 2, 64, 64, TAPS)
    conv_w = _np.zeros((2, 64, IB, TAPS, 2, 64), _np.float32)
    for i in range(2):
        conv_w[i, :, :, :, i, :] = cw[:, i].transpose(2, 0, 3, 1)
    vecs = _np.concatenate([g[n].reshape(-1, P).T for n in ("L0_ffn_bias", "L1_attn_conv_b", "L1_attn_ln_g",
                                                            "L1_attn_ln_b", "L1_attn_fc_b", "L1_attn_cproj_b")], 1)
    experts = _np.concatenate([
        g["L1_ffn_W1"].reshape(EXPERTS, DB, P, HIDDEN).transpose(0, 2, 1, 3).reshape(EXPERTS, P, -1),
        g["L1_ffn_W2"].reshape(EXPERTS, HB, P, D).transpose(0, 2, 1, 3).reshape(EXPERTS, P, -1),
        g["L1_ffn_b1"].reshape(EXPERTS, HB, P).transpose(0, 2, 1)], 2)
    args = {
        "patches": _blocks(patches.reshape(PATCH, TOKENS)),
        "spec_w": _np.stack([_blocks(g["L0_ffn_w_freq_real"]), _blocks(g["L0_ffn_w_freq_imag"])], 1),
        "spec_c": _np.stack([_blocks(f) for f in dft], 1),
        "tok_w": _blocks(g["L0_tok_W_lin"].T),
        "tok_add": tok_add, "tok_sel": sel, "attn_w": attn_w, "consts": consts, "vecs": vecs,
        "inproj_w": _blocks(g["L1_attn_in_proj_w"].T),
        "conv_w": conv_w.reshape(P, IB, TAPS, P),
        "fc_w": _blocks(g["L1_attn_fc_w"].T),
        "cproj_w": _blocks(g["L1_attn_cproj_w"].T),
        "out_w": _blocks(g["L1_attn_out_w"].T),
        "router_w": _blocks(g["L1_ffn_Wr"]),
        "router_b": g["L1_ffn_br"][None],
        "experts": experts, "b2": g["L1_ffn_b2"],
    }
    nc = _bacc.Bacc("TRN2", target_bir_lowering=False, num_devices=1)
    arrays, aps = {}, []
    for name, a in args.items():
        a = _np.ascontiguousarray(a)
        arrays[f"in_{name}"] = a
        aps.append(nc.dram_tensor(f"in_{name}", a.shape, _mybir.dt.from_np(a.dtype), kind="ExternalInput").ap())
    out = nc.dram_tensor("out_0", (TOKENS, D), _mybir.dt.float32, kind="ExternalOutput").ap()
    vit_tower_kernel(nc, *aps, out)
    r = _run(nc, [arrays], core_ids=[0])
    return r.results[0]["out_0"].reshape(IMAGES, SEQ, D)
```

```python
import numpy as np
import concourse.bass as bass
from concourse import mybir
from contextlib import ExitStack

F32 = mybir.dt.float32
BF16 = mybir.dt.bfloat16
I32 = mybir.dt.int32
ALU = mybir.AluOpType
ACT = mybir.ActivationFunctionType
AX = mybir.AxisListType

P = 128
IMAGES = 16
SEQ = 37
TOKENS = IMAGES * SEQ
HALF = TOKENS // 2
D = 256
DB = D // P
PATCH = 768
PB = PATCH // P
HEADS = 16
HD = D // HEADS
HPB = HEADS // DB
INNER = 512
IB = INNER // P
TAPS = 4
PADSEQ = SEQ + TAPS - 1
EPS = 1e-5

EXPERTS = 16
HIDDEN = 1024
HB = HIDDEN // P
PAIRS = 2 * TOKENS
TILES = EXPERTS + (PAIRS - EXPERTS) // P
AHEAD = 1
SLOTS = (TILES + AHEAD + 1) * P
ROWS = [P, P, P, P, TOKENS - 4 * P]
RT = len(ROWS)
LIMITS = (TOKENS - 1) // P + 1
WCOLS = DB * HIDDEN + HB * D + HB
RING = 4

ATT = [(h * HALF + o, n) for h in range(2) for o, n in ((0, 111), (111, 111), (222, 74))]
UNITS = [(t, b) for t in range(len(ATT)) for b in range(4)]
AW = 111
PAIRW = 3 * HD

CONST = {}


def _columns():
    at = 0
    for name, n in (("cos", SEQ), ("sin", SEQ), ("headmask", HPB), ("ident", P), ("means", P), ("ones", P),
                    ("tri", P), ("attmask", AW), ("tri16", EXPERTS + 1), ("slots16", RT * EXPERTS),
                    ("limits", LIMITS), ("iota16", EXPERTS)):
        CONST[name] = (at, n)
        at += n
    return at


NCONST = _columns()

VEC = {}


def _vcolumns():
    at = 0
    for name, n in (("ffn_bias", DB), ("conv_b", IB), ("ln_g", IB), ("ln_b", IB), ("fc_b", DB),
                    ("cproj_b", IB)):
        VEC[name] = (at, n)
        at += n
    return at


NVEC = _vcolumns()

def _jobs():
    def each(name, h, blocks):
        return [(name, h, m) for m in range(blocks)]

    v = [("spec_a", part, j) for part in range(2) for j in range(DB)]
    v += [("mean", 0, 0), ("mean", 0, 1)] + [("spec_m", d) for d in range(DB)]
    for h in range(2):
        v += [(x, h, m) for m in range(DB) for x in ("q", "k")]
        if h == 0:
            v += [("fold", m) for m in range(DB)]
    v += [("score", u) for u in range(3)] + [("biases",)] + [("score", u) for u in range(3, len(UNITS))]
    v += each("wo", 0, DB) + [("mean", 1, 0)] + each("ffn", 0, DB)
    v += each("wo", 1, DB) + [("mean", 2, 0), ("mean", 1, 1)] + each("inh", 0, IB)
    v += each("ffn", 1, DB) + [("mean", 2, 1)] + each("conv", 0, IB)[:3] + each("inh", 1, IB)
    v += [("conv", 0, 3), ("conv", 1, 0), ("mean", 3, 0)] + each("conv", 1, IB)[1:]
    v += each("fc", 0, DB) + [("mean", 3, 1)] + each("out", 0, DB)
    v += each("fc", 1, DB) + [("mean", 4, 0)]
    v += each("out", 1, DB) + [("mean", 4, 1)]
    v += [("logits",), ("count",), ("slots",), ("starts",), ("gt", 0), ("gt", 1)]
    v += [("b2", t) for t in range(RT)]

    a = each("tok", 0, DB) + each("tok", 1, DB) + [("var", 0, 0), ("var", 0, 1)]
    a += [("v", t) for t in range(len(ATT))]
    a += [("pt", u) for u in range(len(UNITS))]
    a += [("var", 1, 0), ("var", 2, 0), ("var", 1, 1)] + each("gate", 0, IB)
    a += [("var", 2, 1)] + each("gate", 1, IB) + [("var", 3, 0), ("var", 3, 1)]
    a += [("hrow", 0), ("hrow", 1), ("rowvar",)] + [("xrow", t) for t in range(RT)]
    a += [("hrow", t) for t in range(2, RT)]
    return v, a


NORMS = [(0, 0), (0, 1), (1, 0), (2, 0), (1, 1), (2, 1), (3, 0), (3, 1), (4, 0), (4, 1)]
NORMALISED = [(0, 0), (0, 1), (2, 0), (2, 1)]
VJOBS, AJOBS = _jobs()
VNUM = {k: n for n, k in enumerate(VJOBS)}
ANUM = {k: n for n, k in enumerate(AJOBS)}
VBANKS = ABANKS = 3


def sums_by_act(u):
    return u >= 8 and u % 2 == 1


def vit_tower_kernel(nc, patches, spec_w, spec_c, tok_w, tok_add, tok_sel, attn_w, wo_w, consts, vecs,
                     inproj_w, conv_w, fc_w, cproj_w, out_w, router_w, router_b, experts, b2,
                     out):
    ctx = ExitStack()
    with ctx:
        def sb(name, shape, dt=F32):
            return ctx.enter_context(nc.sbuf_tensor(name, shape, dt))

        def sem(name):
            return ctx.enter_context(nc.semaphore(name))

        slot_rows = nc.dram_tensor("slot_rows", [SLOTS, D], F32).ap()

        cst = sb("cst", [P, NCONST])
        vec = sb("vec", [P, NVEC])
        spec = sb("spec", [P, 5 * DB * D])
        specw = spec[:, 0:2 * DB * D].rearrange("p (x k n) -> p x k n", x=2, k=DB)
        specc = spec[:, 2 * DB * D:].rearrange("p (x k n) -> p x k n", x=3, k=DB)
        late = sb("late", [P, PB * D + DB * 2 * INNER + IB * TAPS * P + IB * D + DB * INNER])
        parts, at = [], 0
        for k, n in ((PB, D), (DB, 2 * INNER), (IB * TAPS, P), (IB, D), (IB, D)):
            parts.append(late[:, at:at + k * n].rearrange("p (k n) -> p k n", k=k))
            at += k * n
        tokw, inw, convw, fcw, cprojw = parts
        convw = convw.rearrange("p (m t) n -> p m t n", t=TAPS)
        xsT = late[:, 0:(TILES + AHEAD) * D].rearrange("p (j k n) -> p j k n", k=DB, n=P)
        tokadd = sb("tokadd", [SEQ + 2, D])
        toksel = sb("toksel", [SEQ + 2, HALF])
        attnm = sb("attnm", [P, 6 * DB * D])
        attnw = attnm[:, 0:3 * DB * D].rearrange("p (x k n) -> p x k n", x=3, k=DB)
        wo = attnm[:, 5 * DB * D:].rearrange("p (k n) -> p k n", k=DB)
        outw = sb("outw", [P, IB, D])
        routerw = sb("routerw", [P, DB, EXPERTS])
        routerb = sb("routerb", [1, EXPERTS])
        b2s = sb("b2s", [EXPERTS, D])
        wexp = sb("wexp", [P, RING, WCOLS])

        patchm = sb("patchm", [P, PB * TOKENS])
        xpatch = patchm[:, :].rearrange("p (k n) -> p k n", k=PB)
        sc = patchm[0:AW, 0:8 * AW].rearrange("p (x n) -> p x n", x=2)
        pr = patchm[0:AW, 8 * AW:24 * AW].rearrange("p (x n) -> p x n", x=4)
        prT = patchm[0:AW, 24 * AW:32 * AW].rearrange("p (x n) -> p x n", x=2)
        res = patchm[:, 0:IB * TOKENS].rearrange("p (k n) -> p k n", k=IB)
        base = patchm[:, 0:RT * D].rearrange("p (t c) -> p t c", t=RT)
        xrow = patchm[:, RT * D:2 * RT * D].rearrange("p (t c) -> p t c", t=RT)
        vals = spec[0:AW, 0:len(ATT) * HEADS // 2 * PAIRW].rearrange("p (t a n) -> p t a n", t=len(ATT), n=PAIRW)
        gate = spec[:, 0:IB * TOKENS].rearrange("p (k n) -> p k n", k=IB)
        got = spec[:, 0:RT * D].rearrange("p (t c) -> p t c", t=RT)
        got2 = spec[:, RT * D:2 * RT * D].rearrange("p (t c) -> p t c", t=RT)
        keym = sb("keym", [P, 2 * IB * HALF])
        sqlast = keym[:, 0:DB * TOKENS].rearrange("p (k n) -> p k n", k=DB)
        sq = keym[:, :].rearrange("p (h k n) -> p h k n", h=2, k=IB)
        kheads = wexp[:, 1:4, :].rearrange("p u c -> p (u c)")[:, 0:HEADS * TOKENS].rearrange(
            "p (m e n) -> p m e n", m=DB, e=HPB)
        hid = keym[:, 0:HB * P].rearrange("p (m n) -> p m n", m=HB)
        hpad = attnm[:, 0:IB * IMAGES * PADSEQ].rearrange("p (k i s) -> p k i s", k=IB, i=IMAGES)
        hT = sb("hT", [P, DB, TOKENS])
        xn = sb("xn", [P, DB, TOKENS])
        fcs = xn
        cen = sb("cen", [P, IB, TOKENS])
        qT = cen[:, 0:2, :]
        oT = cen[:, 2:4, :]
        std = sb("std", [P, 2, HALF])
        rstd = sb("rstd", [P, 2, HALF])
        rowrstd = sb("rowrstd", [P, 2, RT])
        outb = sb("outb", [P, DB])
        rbias = sb("rbias", [P, EXPERTS])
        fcb = sb("fcb", [P, DB])
        eps = sb("eps", [P, 1])
        spa = sb("spa", [P, 2, DB, D])
        folded = spa[:, 0]
        specm = sb("specm", [P, DB, D])
        kr = sb("kr", [P, DB, HALF])
        rot1 = sb("rot1", [P, HALF])
        rot2 = sb("rot2", [P, HALF])
        krot1 = sb("krot1", [P, HALF])
        krot2 = sb("krot2", [P, HALF])
        identb = sb("identb", [P, P], BF16)
        maskb = sb("maskb", [AW, 4, AW], BF16)
        trib = sb("trib", [P, P], BF16)
        onesb = sb("onesb", [P, P], BF16)
        tri16b = sb("tri16b", [EXPERTS, EXPERTS + 1], BF16)
        slots16b = sb("slots16b", [EXPERTS, RT * EXPERTS], BF16)
        smax = sb("smax", [AW, 3, 4])
        psums = sb("psums", [AW, 2, 4])
        rden = sb("rden", [AW, 2, 4])
        prob = sb("prob", [P, RT, EXPERTS])
        rtmp = sb("rtmp", [P, RT, EXPERTS])
        pick = sb("pick", [P, 2, RT, EXPERTS])
        both = sb("both", [P, RT, EXPERTS], BF16)
        ptmp = sb("ptmp", [P, 2, RT, EXPERTS])
        gates = sb("gates", [P, RT, EXPERTS])
        slotv = sb("slotv", [P, RT, EXPERTS])
        red = sb("red", [P, 5, RT])
        gsel = sb("gsel", [P, 2, RT])
        slot = sb("slot", [P, 2, RT], I32)
        over = sb("over", [EXPERTS, LIMITS], BF16)
        gT = sb("gT", [EXPERTS, TOKENS])
        starts = sb("starts", [1, EXPERTS + 1], I32)
        xs = sb("xs", [P, AHEAD + 1, D])
        ysb = sb("ysb", [P, D])
        zeros = ysb[:, :]

        def c(name, rows=P):
            at, n = CONST[name]
            return cst[0:rows, at:at + n]

        def vcol(name, m):
            at, _ = VEC[name]
            return vec[:, at + m:at + m + 1]

        bank = [ctx.enter_context(nc.psum_tensor(f"bank{i}", [P, 512], F32)) for i in range(8)]
        vbank, abank, obank = bank[0:3], bank[3:6], bank[6:8]

        xs_bank, up_bank_a, up_bank_b, y_bank = bank[2], bank[3], bank[0], bank[6]

        def vb(key):
            return vbank[VNUM[key] % VBANKS]

        def ab(key):
            return abank[ANUM[key] % ABANKS]

        const_in, tok_in, attn_in, wo_in, rest_in = (
            sem(n) for n in ("const_in", "tok_in", "attn_in", "wo_in", "rest_in"))
        spec_in = [sem(f"spec_in{i}") for i in range(3)]
        patches_in = [sem(f"patches_in{i}") for i in range(2)]
        v_full, v_read = sem("v_full"), sem("v_read")
        a_full, a_read = sem("a_full"), sem("a_read")
        squared = sem("squared")
        xn_ready = sem("xn_ready")
        k_products = sem("k_products")
        k_rotated = sem("k_rotated")
        k_split = sem("k_split")
        eps_ready = sem("eps_ready")
        vals_zero = sem("vals_zero")
        hpad_zero = sem("hpad_zero")
        zeros_ready = sem("zeros_ready")
        bf16_consts = sem("bf16_consts")
        q_ready = sem("q_ready")
        probs_ready = sem("probs_ready")
        sums_ready = sem("sums_ready")
        probs_normal = sem("probs_normal")
        pv_done = sem("pv_done")
        o_ready = sem("o_ready")
        dve_step = sem("dve_step")
        rows_divide = sem("rows_divide")
        res_summed = sem("res_summed")
        squares_summed = sem("squares_summed")
        fc_folded = sem("fc_folded")
        fc_divided = sem("fc_divided")
        fc_ready = sem("fc_ready")
        shifted = sem("shifted")
        exped = sem("exped")
        picked = sem("picked")
        slots_ready = sem("slots_ready")
        scattered = sem("scattered")
        w_in = [sem(f"w_in{i}") for i in range(RING)]
        xs_first = [sem(f"xs_first{i}") for i in range(AHEAD)]
        xs_in = sem("xs_in")
        xs_turned = sem("xs_turned")
        xs_copied = sem("xs_copied")
        up_a, up_b = sem("up_a"), sem("up_b")
        relu_a, relu_b = sem("relu_a"), sem("relu_b")
        down = sem("down")
        y_ready = sem("y_ready")
        y_out = sem("y_out")
        rows_stored = sem("rows_stored")
        gathered = [[sem(f"gathered{t}_{k}") for k in range(2)] for t in range(RT)]
        final = sem("final")
        stored = sem("stored")

        block = ctx.enter_context(nc.Block())

        def tiles_of(eng, e):
            return (eng.value_load(starts[0:1, bass.ds(e, 1)], min_val=0, max_val=TILES - 1),
                    eng.value_load(starts[0:1, bass.ds(e + 1, 1)], min_val=1, max_val=TILES))

        @block.sync
        def _(sp):
            for x in range(2):
                sp.dma_start(specw[:, x, :, :], spec_w[:, x]).then_inc(spec_in[x], 16)
                sp.dma_start(specc[:, x, :, :], spec_c[:, x]).then_inc(spec_in[x], 16)
            sp.dma_start(specc[:, 2, :, :], spec_c[:, 2]).then_inc(spec_in[2], 16)
            sp.dma_start(tokw, tok_w).then_inc(tok_in, 16)
            sp.dma_start(tokadd[:, :], tok_add).then_inc(tok_in, 16)
            sp.dma_start(toksel[:, :], tok_sel).then_inc(tok_in, 16)
            for h in range(2):
                sp.dma_start(xpatch[:, :, h * HALF:(h + 1) * HALF], patches[:, :, h * HALF:(h + 1) * HALF]
                             ).then_inc(patches_in[h], 16)
            sp.dma_start(cst[:, :], consts).then_inc(const_in, 16)
            sp.dma_start(attnw[:, :, :, :], attn_w).then_inc(attn_in, 16)
            sp.dma_start(wo, wo_w).then_inc(wo_in, 16)
            sp.dma_start(vec[:, :], vecs).then_inc(rest_in, 16)
            sp.dma_start(inw, inproj_w).then_inc(rest_in, 16)
            sp.dma_start(convw, conv_w).then_inc(rest_in, 16)
            sp.dma_start(fcw, fc_w).then_inc(rest_in, 16)
            sp.dma_start(cprojw, cproj_w).then_inc(rest_in, 16)
            sp.dma_start(outw[:, :, :], out_w).then_inc(rest_in, 16)
            sp.dma_start(routerw[:, :, :], router_w).then_inc(rest_in, 16)
            sp.dma_start(routerb[:, :], router_b).then_inc(rest_in, 16)
            sp.dma_start(b2s[:, :], b2).then_inc(rest_in, 16)
            for e in range(RING):
                if e == 1:
                    sp.wait_ge(v_full, VNUM["score", len(UNITS) - 1] + 1)
                sp.dma_start(wexp[:, e, :], experts[e]).then_inc(w_in[e], 16)
            sp.wait_ge(zeros_ready, 1)
            sp.dma_start(slot_rows.rearrange("(t p) c -> p t c", p=P),
                         zeros.unsqueeze(1).to_broadcast([P, SLOTS // P, D])).then_inc(y_out, 16)
            sp.wait_ge(scattered, 2 * RT * 16)
            for j in range(AHEAD):
                sp.dma_start(xs[:, j, :], slot_rows[j * P:(j + 1) * P, :]).then_inc(xs_first[j], 16)
            sp.dma_start(xs[:, AHEAD, :], slot_rows[AHEAD * P:(AHEAD + 1) * P, :]).then_inc(xs_in, 16)
            sp.wait_ge(slots_ready, 2)

            def expert(e, u, following):
                first, end = tiles_of(sp, e)
                with sp.Fori(first, end) as j:
                    sp.wait_ge(xs_turned, j + (AHEAD + 1))
                    sp.dma_start(xs[:, AHEAD, :], slot_rows[bass.ds((j + (AHEAD + 1)) * P, P), :]).then_inc(xs_in, 16)
                    sp.wait_ge(y_ready, j + 1)
                    sp.dma_start(slot_rows[bass.ds(j * P, P), :], ysb[:, :]).then_inc(y_out, 16)
                if following is not None:
                    sp.dma_start(wexp[:, u, :], experts[bass.ds(following, 1)].rearrange("o p c -> (o p) c")
                                 ).then_inc(w_in[u], 16)
                return end

            with sp.Fori(0, EXPERTS // RING - 1) as g:
                for u in range(RING):
                    expert(g * RING + u, u, g * RING + (RING + u))
            for u in range(RING):
                end = expert(EXPERTS - RING + u, u, None)
            sp.wait_ge(xs_in, end * 16 + 16)
            for t in range(RT):
                sp.wait_ge(final, t + 1)
                sp.dma_start(out[t * P:t * P + ROWS[t], :], base[0:ROWS[t], t, :]).then_inc(stored, 16)
            sp.wait_ge(stored, 16 * RT)

        @block.gpsimd
        def _(pool):
            nc.gpsimd.memset(eps[:, :], EPS).then_inc(eps_ready, 1)
            pool.wait_ge(v_full, VNUM["spec_m", 1] + 1)
            nc.gpsimd.memset(vals, 0.0).then_inc(vals_zero, 1)
            for h in range(2):
                for m in range(DB):
                    pool.wait_ge(k_products, 2 * h + m + 1)
                    if h:
                        pool.wait_ge(k_split, m + 1)
                    nc.gpsimd.tensor_tensor(kr[:, m, :], krot1[:, :], krot2[:, :], ALU.add).then_inc(k_rotated, 1)
            pool.wait_ge(a_full, ANUM["v", len(ATT) - 1] + 1)
            nc.gpsimd.memset(hpad, 0.0).then_inc(hpad_zero, 1)
            for u in range(len(UNITS)):
                n = ATT[UNITS[u][0]][1]
                pool.wait_ge(sums_ready, u + 1)
                p4 = pr[0:n, u % 4, 0:4 * n].rearrange("p (a q) -> p a q", a=4)
                nc.gpsimd.tensor_tensor(p4, p4, rden[0:n, u % 2, :].unsqueeze(2).to_broadcast([n, 4, n]), ALU.mult
                                        ).then_inc(probs_normal, 1)
            pool.wait_ge(v_full, VNUM["biases",] + 1)
            for k in range(IB):
                nc.gpsimd.tensor_scalar(fcw[:, k, :], fcw[:, k, :], vcol("ln_g", k), None, ALU.mult
                                        ).then_inc(fc_folded, 1)
            for h in range(2):
                for m in range(1, IB):
                    pool.wait_ge(v_read, VNUM["conv", h, m] + 1)
                    if m > 1:
                        pool.wait_ge(res_summed, (IB - 1) * h + m - 1)
                    before = res[:, 0, h * HALF:(h + 1) * HALF] if m == 1 else kr[:, h, :]
                    nc.gpsimd.tensor_tensor(kr[:, h, :], before, res[:, m, h * HALF:(h + 1) * HALF], ALU.add
                                            ).then_inc(res_summed, 1)
                pool.wait_ge(squared, NORMS.index((3, h)) + 1)
                nc.gpsimd.tensor_tensor(sq[:, h, 0:2, :], sq[:, h, 0:2, :], sq[:, h, 2:4, :], ALU.add
                                        ).then_inc(squares_summed, 1)
            pool.wait_ge(slots_ready, 1)
            pool.wait_ge(y_out, 16)
            for t in range(RT):
                pool.wait_ge(a_read, ANUM["xrow", t] + 1)
                for k in range(2):
                    nc.gpsimd.indirect_dma_start(
                        out=slot_rows, out_offset=bass.IndirectOffsetOnAxis(slot[0:ROWS[t], k, t:t + 1], 0),
                        in_=xrow[0:ROWS[t], t, :], in_offset=None).then_inc(scattered, 16)
            pool.wait_ge(slots_ready, 2)
            _, end = tiles_of(pool, EXPERTS - 1)
            pool.wait_ge(y_out, end * 16 + 16)
            pool.sem_inc(rows_stored, 1)
            pool.wait_ge(rows_stored, 1)
            for t in range(RT):
                for k, g in enumerate((got, got2)):
                    nc.gpsimd.indirect_dma_start(
                        out=g[0:ROWS[t], t, :], out_offset=None, in_=slot_rows,
                        in_offset=bass.IndirectOffsetOnAxis(slot[0:ROWS[t], k, t:t + 1], 0)
                    ).then_inc(gathered[t][k], 16)
            for t in range(RT):
                for k in range(2):
                    pool.wait_ge(gathered[t][k], 16)
            pool.wait_ge(stored, 16 * RT)

        @block.tensor
        def _(pe):
            order = {"v": 0, "a": 0}

            def fill(key):
                if key in VNUM:
                    n = VNUM[key]
                    assert n == order["v"], (key, n, order)
                    order["v"] += 1
                    if n >= VBANKS:
                        pe.wait_ge(v_read, n - VBANKS + 1)
                    return vb(key)
                n = ANUM[key]
                assert n == order["a"], (key, n, order)
                order["a"] += 1
                if n >= ABANKS:
                    pe.wait_ge(a_read, n - ABANKS + 1)
                return ab(key)

            def linear(key, dst, lhs, rhs, more=None):
                pairs = list(zip(lhs, rhs)) + (more or [])
                for k, (l, r) in enumerate(pairs):
                    mm = nc.tensor.matmul(dst, l, r, start=k == 0, stop=k == len(pairs) - 1)
                mm.then_inc(v_full if key in VNUM else a_full, 1)

            def cols(h):
                return slice(h * HALF, (h + 1) * HALF)

            ident, means = c("ident"), c("means")

            def mean(n, h, src, blocks):
                linear(("mean", n, h), fill(("mean", n, h))[:, 0:HALF], [means] * blocks,
                       [src[:, k, cols(h)] for k in range(blocks)])

            def var(n, h, blocks):
                b = fill(("var", n, h))
                pe.wait_ge(squared, NORMS.index((n, h)) + 1)
                linear(("var", n, h), b[:, 0:HALF], [means] * blocks, [sq[:, h, k, :] for k in range(blocks)])

            def read_out(*key):
                if key in VNUM:
                    pe.wait_ge(v_read, VNUM[key] + 1)
                else:
                    pe.wait_ge(a_read, ANUM[key] + 1)

            def dense(name, h, blocks, w, src, depth, first=0):
                for m in blocks:
                    linear((name, h, m), fill((name, h, m))[:, 0:HALF],
                           [w[:, k, first + m * P:first + (m + 1) * P] for k in range(depth)],
                           [src[:, k, cols(h)] for k in range(depth)])

            wr, wi = specw[:, 0], specw[:, 1]
            co, si, ns = specc[:, 0], specc[:, 1], specc[:, 2]
            for part in range(2):
                for j in range(DB):
                    b = fill(("spec_a", part, j))
                    js = slice(j * P, (j + 1) * P)
                    for x, (w, f) in enumerate(((wr, co), (wi, si)) if part == 0 else ((wi, co), (wr, ns))):
                        pe.wait_ge(spec_in[2 if part and x else x], 16 if part and x else 32)
                        for k in range(DB):
                            mm = nc.tensor.matmul(b[:, 0:D], w[:, k, js], f[:, k, :],
                                                  start=x == 0 and k == 0, stop=x == 1 and k == DB - 1)
                    mm.then_inc(v_full, 1)

            def spec_m(d):
                b = fill(("spec_m", d))
                ds = slice(d * P, (d + 1) * P)
                linear(("spec_m", d), b[:, 0:D],
                       [spa[:, part, k, ds] for part in range(2) for k in range(DB)],
                       [f[:, k, :] for f in (co, ns) for k in range(DB)])

            pe.wait_ge(tok_in, 48)

            def tok(h, m):
                b = fill(("tok", h, m))
                ms = slice(m * P, (m + 1) * P)
                linear(("tok", h, m), b[:, 0:HALF], [tokw[:, k, ms] for k in range(PB)],
                       [xpatch[:, k, cols(h)] for k in range(PB)],
                       [(tokadd[:, ms], toksel[:, :])])

            pe.wait_ge(patches_in[0], 16)
            tok(0, 0)
            tok(0, 1)
            pe.wait_ge(patches_in[1], 16)
            tok(1, 0)
            pe.wait_ge(const_in, 16)
            read_out("tok", 0, 1)
            mean(0, 0, hT, DB)
            tok(1, 1)
            var(0, 0, DB)
            read_out("tok", 1, 1)
            mean(0, 1, hT, DB)
            read_out("spec_a", 1, 1)
            spec_m(0)
            var(0, 1, DB)
            spec_m(1)

            pe.wait_ge(attn_in, 16)
            for h in range(2):
                pe.wait_ge(xn_ready, h + 1)
                for m in range(DB):
                    ms = slice(m * P, (m + 1) * P)
                    for x, name in enumerate(("q", "k")):
                        linear((name, h, m), fill((name, h, m))[:, 0:HALF],
                               [attnw[:, x, k, ms] for k in range(DB)], [xn[:, k, cols(h)] for k in range(DB)])
                if h == 0:
                    pe.wait_ge(rest_in, 9 * 16)
                    for m in range(DB):
                        linear(("fold", m), fill(("fold", m))[:, 0:D],
                               [cprojw[:, k, m * P:(m + 1) * P] for k in range(IB)], [outw[:, k, :] for k in range(IB)])
                for t in range(3 * h, 3 * h + 3):
                    c0, n = ATT[t]
                    linear(("v", t), fill(("v", t))[0:n, 0:D], [xn[:, k, c0:c0 + n] for k in range(DB)],
                           [attnw[:, 2, k, :] for k in range(DB)])

            pe.wait_ge(bf16_consts, 2)
            for u in range(len(UNITS) + 4):
                if u < len(UNITS):
                    t, four = UNITS[u]
                    c0, n = ATT[t]
                    if four % 2 == 0 and t in (0, 3):
                        pe.wait_ge(k_split, 2 * (t // 3) + four // 2 + 1)
                        pe.wait_ge(q_ready, 2 * (t // 3) + four // 2 + 1)
                    b = fill(("score", u))
                    nc.tensor.matmul(b[0:n, 0:4 * n].rearrange("p (a q) -> p a q", a=4), identb[0:n, 0:n],
                                     maskb[0:n, :, 0:n], start=True, stop=False)
                    m, e = four // 2, 4 * (four % 2)
                    nc.tensor.matmul(b[0:n, 0:4 * n].rearrange("p (a q) -> p a q", a=4), qT[:, m, c0:c0 + n],
                                     kheads[:, m, e:e + 4, c0:c0 + n],
                                     start=False, stop=True).then_inc(v_full, 1)
                if u == 2:
                    pe.wait_ge(rest_in, 9 * 16)
                    b = fill(("biases",))
                    for m in range(DB):
                        for k in range(IB):
                            mm = nc.tensor.matmul(b[:, m:m + 1], fcw[:, k, m * P:(m + 1) * P], vcol("ln_b", k),
                                                  start=k == 0, stop=k == IB - 1)
                    for m in range(DB):
                        for k in range(IB):
                            nc.tensor.matmul(b[:, DB + EXPERTS + m:DB + EXPERTS + m + 1], outw[:, k, m * P:(m + 1) * P],
                                             vcol("cproj_b", k), start=k == 0, stop=k == IB - 1)
                    nc.tensor.matmul(b[:, DB:DB + EXPERTS], c("ones", 1), routerb[:, :], start=True, stop=True
                                     ).then_inc(v_full, 1)
                if 0 <= u - 3 < len(UNITS):
                    w = u - 3
                    n = ATT[UNITS[w][0]][1]
                    b = fill(("pt", w))
                    pe.wait_ge(probs_normal, w + 1)
                    for a in range(4):
                        mm = nc.tensor.transpose(b[0:n, a * n:(a + 1) * n], pr[0:n, w % 4, a * n:(a + 1) * n],
                                                 ident[0:n, 0:n])
                    mm.then_inc(a_full, 1)
                if 0 <= u - 4 < len(UNITS):
                    w = u - 4
                    t, four = UNITS[w]
                    n = ATT[t][1]
                    pe.wait_ge(a_read, ANUM["pt", w] + 1)
                    if four == 0 and t >= 2:
                        pe.wait_ge(o_ready, t - 1)
                    for a in range(4):
                        pair, odd = 2 * four + a // 2, a % 2
                        m, at = pair // 4, 32 * (pair % 4)
                        mm = nc.tensor.matmul(obank[t % 2][at:at + 32, m * n:(m + 1) * n],
                                              vals[0:n, t, pair, odd * HD:odd * HD + 2 * HD],
                                              prT[0:n, w % 2, a * n:(a + 1) * n],
                                              start=not odd, stop=bool(odd))
                    mm.then_inc(pv_done, 1)

                if u == len(UNITS):
                    pe.wait_ge(wo_in, 16)
                    dense("wo", 0, range(DB), wo, oT, DB)
                elif u == len(UNITS) + 1:
                    read_out("wo", 0, 1)
                    mean(1, 0, hT, DB)
                elif u == len(UNITS) + 3:
                    var(1, 0, DB)
                    dense("ffn", 0, range(DB), specm[:, :, :], cen, DB)

            pe.wait_ge(o_ready, 6)
            dense("wo", 1, range(DB), wo, oT, DB)
            read_out("ffn", 0, 1)
            mean(2, 0, hT, DB)
            read_out("wo", 1, 1)
            mean(1, 1, hT, DB)
            read_out("mean", 2, 0)
            dense("inh", 0, [0], inw, cen, DB)
            var(2, 0, DB)
            dense("inh", 0, [1, 2], inw, cen, DB)
            var(1, 1, DB)
            dense("inh", 0, [3], inw, cen, DB)
            dense("ffn", 1, range(DB), specm[:, :, :], cen, DB)

            def conv(h, m):
                read_out("inh", h, m)
                linear(("conv", h, m), fill(("conv", h, m))[:, 0:HALF].rearrange("p (i s) -> p i s", s=SEQ),
                       [convw[:, m, tap, :] for tap in range(TAPS)],
                       [hpad[:, m, 8 * h:8 * h + 8, tap:tap + SEQ] for tap in range(TAPS)])

            pe.wait_ge(xn_ready, NORMALISED.index((2, 0)) + 1)
            dense("gate", 0, [0, 1, 2], inw, xn, DB, INNER)
            read_out("ffn", 1, 1)
            mean(2, 1, hT, DB)
            dense("gate", 0, [3], inw, xn, DB, INNER)
            conv(0, 0)
            var(2, 1, DB)
            conv(0, 1)
            conv(0, 2)
            dense("inh", 1, range(IB), inw, cen, DB)
            pe.wait_ge(xn_ready, NORMALISED.index((2, 1)) + 1)
            dense("gate", 1, [0, 1], inw, xn, DB, INNER)
            conv(0, 3)
            dense("gate", 1, [2, 3], inw, xn, DB, INNER)

            def mean_of_res(h):
                pe.wait_ge(res_summed, (IB - 1) * (h + 1))
                linear(("mean", 3, h), fill(("mean", 3, h))[:, 0:HALF], [means], [kr[:, h, :]])

            def var_of_res(h):
                pe.wait_ge(squares_summed, h + 1)
                var(3, h, 2)

            conv(1, 0)
            mean_of_res(0)
            conv(1, 1)
            conv(1, 2)
            var_of_res(0)
            conv(1, 3)
            pe.wait_ge(fc_folded, IB)
            dense("fc", 0, range(DB), fcw, cen, IB)
            mean_of_res(1)

            def output(h, m):
                b = fill(("out", h, m))[:, 0:HALF]
                ms = slice(m * P, (m + 1) * P)
                for k in range(IB):
                    nc.tensor.matmul(b, outw[:, k, ms], res[:, k, cols(h)], start=k == 0, stop=False)
                pe.wait_ge(fc_ready, DB * (h + 1))
                for k in range(DB):
                    mm = nc.tensor.matmul(b, folded[:, k, ms], fcs[:, k, cols(h)], start=False, stop=k == DB - 1)
                mm.then_inc(v_full, 1)

            output(0, 0)
            output(0, 1)
            var_of_res(1)
            dense("fc", 1, range(DB), fcw, cen, IB)
            read_out("out", 0, 1)
            mean(4, 0, hT, DB)

            def rows(name, src, t):
                b = fill((name, t))
                for m in range(DB):
                    mm = nc.tensor.transpose(b[0:ROWS[t], m * P:(m + 1) * P],
                                             src[:, m, t * P:t * P + ROWS[t]], ident)
                mm.then_inc(a_full, 1)

            rows("hrow", hT, 0)
            output(1, 0)
            output(1, 1)
            rows("hrow", hT, 1)

            last_mean = fill(("mean", 4, 1))
            logits, rowvar = fill(("logits",)), fill(("rowvar",))

            def router(t):
                es = slice(t * EXPERTS, (t + 1) * EXPERTS)
                for k in range(DB):
                    mm = nc.tensor.matmul(logits[0:ROWS[t], es], cen[:, k, t * P:t * P + ROWS[t]], routerw[:, k, :],
                                          start=k == 0, stop=k == DB - 1)
                return mm

            def variance(t):
                for k in range(DB):
                    mm = nc.tensor.matmul(rowvar[0:ROWS[t], t:t + 1], sqlast[:, k, t * P:t * P + ROWS[t]],
                                          means[:, 0:1], start=k == 0, stop=k == DB - 1)
                return mm

            nc.tensor.matmul(logits[:, (RT - 1) * EXPERTS:RT * EXPERTS], c("ones", 1), routerb[:, :],
                             start=True, stop=True)
            nc.tensor.matmul(rowvar[:, RT - 1:RT], means, means[:, 0:1], start=True, stop=True)
            ahead = HALF // P
            pe.wait_ge(squared, NORMS.index((4, 0)) + 1)
            for t in range(ahead):
                router(t)
                variance(t)
            read_out("out", 1, 1)
            linear(("mean", 4, 1), last_mean[:, 0:HALF], [means] * DB, [hT[:, k, cols(1)] for k in range(DB)])
            read_out("mean", 4, 1)
            for t in range(ahead, RT):
                mm = router(t)
            mm.then_inc(v_full, 1)
            pe.wait_ge(squared, NORMS.index((4, 1)) + 1)
            for t in range(ahead, RT):
                mm = variance(t)
            mm.then_inc(a_full, 1)
            for t in range(RT):
                rows("xrow", cen, t)
            for t in range(2, RT):
                rows("hrow", hT, t)

            pe.wait_ge(picked, 1)
            b = fill(("count",))
            for t in range(RT):
                mm = nc.tensor.matmul(b[0:EXPERTS, 0:1], both[0:ROWS[t], t, :], onesb[0:ROWS[t], 0:1],
                                      start=t == 0, stop=t == RT - 1)
            mm.then_inc(v_full, 1)
            b = fill(("slots",))[:, 0:RT * EXPERTS]
            nc.tensor.matmul(b, trib[:, :], both[:, :, :].rearrange("p t e -> p (t e)"), start=True, stop=False)
            for t in range(RT - 1):
                later = RT - 1 - t
                nc.tensor.matmul(b[:, (t + 1) * EXPERTS:].rearrange("p (t e) -> p t e", e=EXPERTS), onesb[:, :],
                                 both[:, t:t + 1, :].to_broadcast([P, later, EXPERTS]), start=False, stop=False)
            pe.wait_ge(picked, 2)

            def every(k):
                return over[:, k:k + 1].to_broadcast([EXPERTS, P])

            for k in range(LIMITS):
                mm = nc.tensor.matmul(b, every(k), slots16b[:, :], start=False, stop=k == LIMITS - 1)
            mm.then_inc(v_full, 1)
            linear(("starts",), fill(("starts",))[:, 0:EXPERTS + 1], [every(k) for k in range(LIMITS)],
                   [tri16b[:, :]] * LIMITS)
            pe.wait_ge(picked, 3)
            for g in range(2):
                b = fill(("gt", g))
                for t in ((0, 1, 2, 3), (4,))[g]:
                    mm = nc.tensor.transpose(b[0:EXPERTS, (t % 4) * P:(t % 4 + 1) * P], gates[:, t, :], ident)
                mm.then_inc(v_full, 1)
            for t in range(RT):
                b = fill(("b2", t))
                pe.wait_ge(v_read, VNUM["gt", t // 4] + 1)
                linear(("b2", t), b[0:ROWS[t], 0:D], [gT[:, t * P:t * P + ROWS[t]]], [b2s[:, :]])

            pe.wait_ge(v_read, len(VJOBS))
            pe.wait_ge(a_read, len(AJOBS))

            def turn(rows, j):
                for k in range(DB):
                    mm = nc.tensor.transpose(xs_bank[:, k * P:(k + 1) * P], rows[:, k * P:(k + 1) * P], ident)
                mm.then_inc(xs_turned, 1)

            for j in range(AHEAD):
                pe.wait_ge(xs_first[j], 16)
                if j:
                    pe.wait_ge(xs_copied, j)
                turn(xs[:, j, :], j)
            pe.wait_ge(slots_ready, 2)
            with pe.Fori(0, EXPERTS // RING) as g:
                for u in range(RING):
                    w1 = wexp[:, u, 0:DB * HIDDEN].rearrange("p (k n) -> p k n", k=DB)
                    w2 = wexp[:, u, DB * HIDDEN:DB * HIDDEN + HB * D].rearrange("p (m n) -> p m n", m=HB)
                    first, end = tiles_of(pe, g * RING + u)
                    with pe.Fori(first, end) as j:
                        pe.wait_ge(w_in[u], g * 16 + 16)
                        pe.wait_ge(xs_copied, j + 1)
                        for up_bank, full, m0 in ((up_bank_a, up_a, 0), (up_bank_b, up_b, 4)):
                            for i in range(4):
                                m = m0 + i
                                for k in range(DB):
                                    mm = nc.tensor.matmul(
                                        up_bank[:, i * P:(i + 1) * P], w1[:, k, m * P:(m + 1) * P],
                                        xsT[:, bass.ds(j, 1), k, :].rearrange("p j n -> p (j n)"),
                                        start=k == 0, stop=k == DB - 1)
                            mm.then_inc(full, 1)
                        pe.wait_ge(xs_in, j * 16 + 16)
                        pe.wait_ge(xs_copied, j + AHEAD)
                        turn(xs[:, AHEAD, :], j)
                        pe.wait_ge(relu_a, j + 1)
                        for m in range(HB):
                            if m == HB // 2:
                                pe.wait_ge(relu_b, j + 1)
                            mm = nc.tensor.matmul(y_bank[:, 0:D], hid[:, m, :], w2[:, m, :],
                                                  start=m == 0, stop=m == HB - 1)
                        mm.then_inc(down, 1)

        @block.scalar
        def _(act):
            def take(key):
                act.wait_ge(a_full, ANUM[key] + 1)
                return ab(key)

            def cols(h):
                return slice(h * HALF, (h + 1) * HALF)

            def square(n, h, blocks):
                act.wait_ge(v_read, VNUM["mean", n, h] + 1)
                dst = sqlast[:, :, cols(h)] if n == 4 else sq[:, h, 0:blocks, :]
                nc.scalar.activation(dst, cen[:, 0:blocks, cols(h)], ACT.Square
                                     ).then_inc(squared, 1)

            def deviation(n, h, blocks):
                nc.scalar.activation(std[:, h, :], take(("var", n, h))[:, 0:HALF], ACT.Sqrt, bias=eps[:, :],
                                     scale=D / (blocks * P)).then_inc(a_read, 1)

            def gates_of(h):
                for m in range(IB):
                    nc.scalar.activation(gate[:, m, cols(h)], take(("gate", h, m))[:, 0:HALF], ACT.Silu
                                         ).then_inc(a_read, 1)

            def fc_of(h):
                for m in range(DB):
                    act.wait_ge(fc_divided, DB * h + m + 1)
                    nc.scalar.activation(fcs[:, m, cols(h)], (rot1, rot2)[m][:, :], ACT.Silu,
                                         bias=fcb[:, m:m + 1]).then_inc(fc_ready, 1)

            def rows(name, dst, t):
                scale = rowrstd[0:ROWS[t], 1, t:t + 1] if name == "xrow" else 1.0
                nc.scalar.activation(dst[0:ROWS[t], t, :], take((name, t))[0:ROWS[t], 0:D], ACT.Copy,
                                     scale=scale).then_inc(a_read, 1)

            for h in range(2):
                for m in range(DB):
                    if (h, m) == (1, 1):
                        square(0, 0, DB)
                    b = take(("tok", h, m))
                    nc.scalar.activation(hT[:, m, cols(h)], b[:, 0:HALF], ACT.Copy).then_inc(a_read, 1)
            act.wait_ge(eps_ready, 1)
            deviation(0, 0, DB)
            square(0, 1, DB)
            deviation(0, 1, DB)
            act.wait_ge(const_in, 16)

            def split_keys(h, m, heads):
                act.wait_ge(k_rotated, 2 * h + m + 1)
                for e in heads:
                    kk = nc.scalar.activation(kheads[:, m, e, cols(h)], kr[:, m, :], ACT.Copy,
                                              scale=c("headmask")[:, e:e + 1])
                if e == HPB - 1:
                    kk.then_inc(k_split, 1)

            for m in range(DB):
                split_keys(0, m, range(HPB))
                act.wait_ge(vals_zero, 1)
                for t in range(3 * m, 3 * m + 3):
                    n = ATT[t][1]
                    values = take(("v", t))[0:n, 0:D].rearrange("p (a x d) -> p a x d", x=2, d=HD)
                    nc.scalar.activation(vals[0:n, t, :, 0:HD], values[:, :, 0, :], ACT.Copy)
                    nc.scalar.activation(vals[0:n, t, :, 2 * HD:3 * HD], values[:, :, 1, :], ACT.Copy
                                         ).then_inc(a_read, 1)
            for u in range(len(UNITS) + 4):
                if 0 <= u - 3 < len(UNITS):
                    w = u - 3
                    n = ATT[UNITS[w][0]][1]
                    b = take(("pt", w))
                    if w >= 2:
                        act.wait_ge(pv_done, w - 1)
                    nc.scalar.activation(prT[0:n, w % 2, 0:4 * n], b[0:n, 0:4 * n], ACT.Copy).then_inc(a_read, 1)
                if u < len(UNITS):
                    n = ATT[UNITS[u][0]][1]
                    act.wait_ge(v_read, VNUM["score", u] + 1)
                    if u >= 4:
                        act.wait_ge(a_full, ANUM["pt", u - 4] + 1)
                    if not sums_by_act(u):
                        nc.scalar.activation(pr[0:n, u % 4, 0:4 * n], sc[0:n, u % 2, 0:4 * n], ACT.Exp,
                                             scale=HD ** -0.5).then_inc(probs_ready, 1)
                    for a in range(4 if sums_by_act(u) else 0):
                        if a == 0:
                            act.wait_ge(sums_ready, u - 1)
                        e = nc.scalar.activation(pr[0:n, u % 4, a * n:(a + 1) * n], sc[0:n, u % 2, a * n:(a + 1) * n],
                                                 ACT.Exp, scale=HD ** -0.5, accum_out=psums[0:n, u % 2, a:a + 1])
                        if a == 3:
                            e.then_inc(probs_ready, 1)
                if u < DB * HPB // 2:
                    split_keys(1, 2 * u // HPB, range(2 * u % HPB, 2 * u % HPB + 2))
                if 0 <= u - 4 < len(UNITS) and UNITS[u - 4][1] == 3:
                    t = UNITS[u - 4][0]
                    c0, n = ATT[t]
                    act.wait_ge(pv_done, u - 3)
                    nc.scalar.activation(oT[:, :, c0:c0 + n],
                                         obank[t % 2][:, 0:2 * n].rearrange("p (m n) -> p m n", m=2),
                                         ACT.Copy).then_inc(o_ready, 1)
                if u == len(UNITS) + 2:
                    square(1, 0, DB)
                elif u == len(UNITS) + 3:
                    deviation(1, 0, DB)
            square(2, 0, DB)
            deviation(2, 0, DB)
            square(1, 1, DB)
            deviation(1, 1, DB)
            gates_of(0)
            square(2, 1, DB)
            deviation(2, 1, DB)
            gates_of(1)
            square(3, 0, IB)
            deviation(3, 0, IB)
            fc_of(0)
            square(3, 1, IB)
            deviation(3, 1, IB)
            fc_of(1)
            square(4, 0, DB)
            rows("hrow", base, 0)
            rows("hrow", base, 1)
            square(4, 1, DB)
            nc.scalar.activation(rowrstd[:, 0, :], take(("rowvar",))[:, 0:RT], ACT.Sqrt, bias=eps[:, :]
                                 ).then_inc(a_read, 1)
            act.wait_ge(rows_divide, 1)
            for t in range(RT):
                rows("xrow", xrow, t)
            act.wait_ge(shifted, 1)
            nc.scalar.activation(rtmp[:, :, :], prob[:, :, :], ACT.Exp).then_inc(exped, 1)
            for t in range(2, RT):
                rows("hrow", base, t)

            act.wait_ge(slots_ready, 2)
            with act.Fori(0, EXPERTS // RING) as g:
                for u in range(RING):
                    b1 = wexp[:, u, WCOLS - HB:WCOLS]
                    first, end = tiles_of(act, g * RING + u)
                    with act.Fori(first, end) as j:
                        act.wait_ge(up_a, j + 1)
                        for i in range(4):
                            r = nc.scalar.activation(hid[:, i, :], up_bank_a[:, i * P:(i + 1) * P], ACT.Relu,
                                                     bias=b1[:, i:i + 1])
                        r.then_inc(relu_a, 1)
                        act.wait_ge(down, j + 1)
                        act.wait_ge(y_out, j * 16 + 16)
                        nc.scalar.activation(ysb[:, :], y_bank[:, 0:D], ACT.Copy).then_inc(y_ready, 1)

        @block.vector
        def _(dve):
            steps = [0]

            def then(ins):
                steps[0] += 1
                ins.then_inc(dve_step, 1)
                dve.wait_ge(dve_step, steps[0])

            def take(key):
                dve.wait_ge(v_full, VNUM[key] + 1)
                return vb(key)

            def cols(h):
                return slice(h * HALF, (h + 1) * HALF)

            def centre(n, h, x, blocks):
                b = take(("mean", n, h))
                nc.vector.scalar_tensor_tensor(
                    out=cen[:, 0:blocks, cols(h)], in0=b[:, 0:HALF].unsqueeze(1).to_broadcast([P, blocks, HALF]),
                    scalar=-D / (blocks * P), in1=x[:, :, cols(h)], op0=ALU.mult, op1=ALU.add).then_inc(v_read, 1)

            def inverse(n, h):
                dve.wait_ge(a_read, ANUM["var", n, h] + 1)
                then(nc.vector.reciprocal(rstd[:, h, :], std[:, h, :]))

            def normalise(n, h):
                nc.vector.tensor_tensor(xn[:, :, cols(h)], cen[:, 0:DB, cols(h)],
                                        rstd[:, h, :].unsqueeze(1).to_broadcast([P, DB, HALF]), ALU.mult
                                        ).then_inc(xn_ready, 1)

            nc.vector.memset(zeros, 0.0).then_inc(zeros_ready, 1)
            for part in range(2):
                for j in range(DB):
                    b = take(("spec_a", part, j))
                    nc.vector.tensor_copy(spa[:, part, j, :], b[:, 0:D]).then_inc(v_read, 1)
            dve.wait_ge(const_in, 16)
            nc.vector.tensor_copy(identb[:, :], c("ident")).then_inc(bf16_consts, 1)
            nc.vector.tensor_copy(maskb[:, :, :], c("attmask", AW).unsqueeze(1).to_broadcast([AW, 4, AW])
                                  ).then_inc(bf16_consts, 1)
            for dst, name, n in ((trib, "tri", P), (onesb, "ones", P), (tri16b, "tri16", EXPERTS),
                                 (slots16b, "slots16", EXPERTS)):
                nc.vector.tensor_copy(dst[:, :], c(name, n)).then_inc(bf16_consts, 1)
            centre(0, 0, hT, DB)
            centre(0, 1, hT, DB)
            for d in range(DB):
                b = take(("spec_m", d))
                nc.vector.tensor_scalar(specm[:, d, :], b[:, 0:D], 1.0 / D, None, ALU.mult).then_inc(v_read, 1)
                inverse(0, d)
                normalise(0, d)
            def by_image(x):
                return x.rearrange("p (i s) -> p i s", s=SEQ)

            at_sin, _ = CONST["sin"]
            for h in range(2):
                for m in range(DB):
                    for x in ("q", "k"):
                        if 2 * h + m:
                            dve.wait_ge(q_ready if x == "q" else k_rotated, 2 * h + m)
                        by_cos, by_sin = (rot1, rot2) if x == "q" else (krot1, krot2)
                        b = take((x, h, m))
                        then(nc.vector.tensor_tensor(by_image(by_cos[:, :]), by_image(b[:, 0:HALF]),
                                                     c("cos").unsqueeze(1).to_broadcast([P, 8, SEQ]), ALU.mult))
                        for src, dst in ((slice(P // 2, P), slice(0, P // 2)), (slice(0, P // 2), slice(P // 2, P))):
                            r = nc.vector.tensor_tensor(
                                by_image(by_sin[dst, :]), by_image(b[src, 0:HALF]),
                                cst[src, at_sin:at_sin + SEQ].unsqueeze(1).to_broadcast([P // 2, 8, SEQ]), ALU.mult)
                        r.then_inc(v_read, 1)
                        dve.wait_ge(v_read, VNUM[x, h, m] + 1)
                        if x == "q":
                            nc.vector.tensor_tensor(qT[:, m, cols(h)], rot1[:, :], rot2[:, :], ALU.add
                                                    ).then_inc(q_ready, 1)
                        else:
                            dve.sem_inc(k_products, 1)
                if h == 0:
                    for m in range(DB):
                        nc.vector.tensor_copy(folded[:, m, :], take(("fold", m))[:, 0:D]).then_inc(v_read, 1)
            for u in range(len(UNITS) + 1):
                if u < len(UNITS):
                    n = ATT[UNITS[u][0]][1]
                    b = take(("score", u))
                    s4 = b[0:n, 0:4 * n].rearrange("p (a q) -> p a q", a=4)
                    then(nc.vector.tensor_reduce(smax[0:n, u % 3, :], s4, AX.X, ALU.max))
                    if u >= 2:
                        dve.wait_ge(probs_ready, u - 1)
                    nc.vector.tensor_tensor(sc[0:n, u % 2, 0:4 * n].rearrange("p (a q) -> p a q", a=4), s4,
                                            smax[0:n, u % 3, :].unsqueeze(2).to_broadcast([n, 4, n]), ALU.subtract
                                            ).then_inc(v_read, 1)
                if u == 2:
                    dve.wait_ge(rest_in, 9 * 16)
                    at, _ = VEC["fc_b"]
                    b = take(("biases",))
                    nc.vector.tensor_copy(rbias[:, :], b[:, DB:DB + EXPERTS])
                    nc.vector.tensor_copy(outb[:, :], b[:, DB + EXPERTS:2 * DB + EXPERTS])
                    nc.vector.tensor_tensor(fcb[:, :], b[:, 0:DB], vec[:, at:at + DB], ALU.add).then_inc(v_read, 1)
                if u >= 1:
                    w = u - 1
                    n = ATT[UNITS[w][0]][1]
                    dve.wait_ge(probs_ready, w + 1)
                    if not sums_by_act(w):
                        then(nc.vector.tensor_reduce(
                            psums[0:n, w % 2, :], pr[0:n, w % 4, 0:4 * n].rearrange("p (a q) -> p a q", a=4),
                            AX.X, ALU.add))
                    if w >= 2:
                        dve.wait_ge(probs_normal, w - 1)
                    nc.vector.reciprocal(rden[0:n, w % 2, :], psums[0:n, w % 2, :]).then_inc(sums_ready, 1)

            def add_to_stream(name, h, m):
                b = take((name, h, m))
                nc.vector.tensor_tensor(hT[:, m, cols(h)], b[:, 0:HALF], hT[:, m, cols(h)], ALU.add
                                        ).then_inc(v_read, 1)

            def ffn(h):
                for m in range(DB):
                    b = take(("ffn", h, m))
                    divided = (rot1, rot2)[m]
                    then(nc.vector.tensor_tensor(divided[:, :], b[:, 0:HALF], rstd[:, h, :], ALU.mult))
                    nc.vector.scalar_tensor_tensor(
                        out=hT[:, m, cols(h)], in0=divided[:, :], scalar=vcol("ffn_bias", m),
                        in1=hT[:, m, cols(h)], op0=ALU.add, op1=ALU.add).then_inc(v_read, 1)

            def inh(h):
                for m in range(IB):
                    b = take(("inh", h, m))
                    nc.vector.tensor_tensor(hpad[:, m, 8 * h:8 * h + 8, TAPS - 1:PADSEQ],
                                            b[:, 0:HALF].rearrange("p (i s) -> p i s", s=SEQ),
                                            rstd[:, h, :].rearrange("p (i s) -> p i s", s=SEQ), ALU.mult
                                            ).then_inc(v_read, 1)

            def conv(h, m):
                b = take(("conv", h, m))
                dve.wait_ge(a_read, ANUM["gate", h, m] + 1)
                nc.vector.scalar_tensor_tensor(out=res[:, m, cols(h)], in0=b[:, 0:HALF], scalar=vcol("conv_b", m),
                                               in1=gate[:, m, cols(h)], op0=ALU.add, op1=ALU.mult
                                               ).then_inc(v_read, 1)

            def fc(h, m):
                b = take(("fc", h, m))
                if h:
                    dve.wait_ge(fc_ready, m + 1)
                nc.vector.tensor_tensor((rot1, rot2)[m][:, :], b[:, 0:HALF], rstd[:, h, :], ALU.mult
                                        ).then_inc(fc_divided, 1)
                dve.wait_ge(fc_divided, DB * h + m + 1)
                dve.sem_inc(v_read, 1)

            def out_to_stream(h, m):
                b = take(("out", h, m))
                nc.vector.scalar_tensor_tensor(out=hT[:, m, cols(h)], in0=b[:, 0:HALF], scalar=outb[:, m:m + 1],
                                               in1=hT[:, m, cols(h)], op0=ALU.add, op1=ALU.add).then_inc(v_read, 1)

            add_to_stream("wo", 0, 0)
            add_to_stream("wo", 0, 1)
            centre(1, 0, hT, DB)
            inverse(1, 0)
            ffn(0)
            add_to_stream("wo", 1, 0)
            add_to_stream("wo", 1, 1)
            centre(2, 0, hT, DB)
            centre(1, 1, hT, DB)
            inverse(2, 0)
            dve.wait_ge(hpad_zero, 1)
            inh(0)
            normalise(2, 0)
            inverse(1, 1)
            ffn(1)
            centre(2, 1, hT, DB)
            conv(0, 0)
            inverse(2, 1)
            conv(0, 1)
            normalise(2, 1)
            conv(0, 2)
            inh(1)
            conv(0, 3)
            conv(1, 0)
            centre(3, 0, res, IB)
            conv(1, 1)
            conv(1, 2)
            inverse(3, 0)
            conv(1, 3)
            fc(0, 0)
            fc(0, 1)
            centre(3, 1, res, IB)
            out_to_stream(0, 0)
            out_to_stream(0, 1)
            inverse(3, 1)
            fc(1, 0)
            fc(1, 1)
            centre(4, 0, hT, DB)
            out_to_stream(1, 0)
            out_to_stream(1, 1)
            centre(4, 1, hT, DB)
            dve.wait_ge(a_read, ANUM["rowvar",] + 1)
            nc.vector.reciprocal(rowrstd[:, 1, :], rowrstd[:, 0, :]).then_inc(rows_divide, 1)

            wide = [P, RT, EXPERTS]

            def each(x):
                return x.unsqueeze(2).to_broadcast(wide)

            def over_tiles(x):
                return x.unsqueeze(1).to_broadcast(wide)

            tmp, iota = rtmp[:, :, :], over_tiles(c("iota16"))
            dve.wait_ge(rows_divide, 1)
            logits = slotv[:, :, :]
            then(nc.vector.tensor_tensor(
                logits, take(("logits",))[:, 0:RT * EXPERTS].rearrange("p (t e) -> p t e", e=EXPERTS),
                each(rowrstd[:, 1, :]), ALU.mult))
            dve.sem_inc(v_read, 1)
            then(nc.vector.tensor_tensor(logits, logits, over_tiles(rbias[:, :]), ALU.add))
            first = prob[:, :, :]
            src = logits
            for k in range(2):
                then(nc.vector.tensor_reduce(red[:, k, :], src, AX.X, ALU.max))
                then(nc.vector.tensor_tensor(first, src, each(red[:, k, :]), ALU.is_equal))
                then(nc.vector.tensor_tensor(first, first, iota, ALU.mult))
                then(nc.vector.tensor_reduce(red[:, 2 + k, :], first, AX.X, ALU.min))
                then(nc.vector.tensor_tensor(pick[:, k, :, :], iota, each(red[:, 2 + k, :]), ALU.is_equal))
                if k == 0:
                    then(nc.vector.scalar_tensor_tensor(out=tmp, in0=pick[:, 0, :, :], scalar=-1e30, in1=logits,
                                                        op0=ALU.mult, op1=ALU.add))
                    src = tmp
            nc.vector.tensor_tensor(both[:, :, :], pick[:, 0, :, :], pick[:, 1, :, :], ALU.add).then_inc(picked, 1)
            then(nc.vector.tensor_tensor(prob[:, :, :], logits, each(red[:, 0, :]), ALU.subtract))
            dve.sem_inc(shifted, 1)
            b = take(("count",))
            then(nc.vector.tensor_tensor(
                over[:, :], b[0:EXPERTS, 0:1].to_broadcast([EXPERTS, LIMITS]), c("limits", EXPERTS), ALU.is_gt))
            dve.sem_inc(picked, 1)
            dve.sem_inc(v_read, 1)
            b = take(("slots",))
            both_choices = [P, 2, RT * EXPERTS]
            then(nc.vector.tensor_tensor(ptmp[:, :, :, :].rearrange("p k t e -> p k (t e)"),
                                         pick[:, :, :, :].rearrange("p k t e -> p k (t e)"),
                                         b[:, 0:RT * EXPERTS].unsqueeze(1).to_broadcast(both_choices), ALU.mult))
            dve.sem_inc(v_read, 1)
            with nc.allow_low_precision(reason="one whole number below 4096 and zeros"):
                nc.vector.tensor_reduce(slot[:, :, :], ptmp[:, :, :, :], AX.X, ALU.add).then_inc(slots_ready, 1)
            b = take(("starts",))
            then(nc.vector.tensor_copy(starts[:, :], b[0:1, 0:EXPERTS + 1]))
            dve.sem_inc(slots_ready, 1)
            dve.sem_inc(v_read, 1)
            dve.wait_ge(exped, 1)
            then(nc.vector.tensor_reduce(red[:, 1, :], tmp, AX.X, ALU.add))
            then(nc.vector.reciprocal(red[:, 4, :], red[:, 1, :]))
            then(nc.vector.tensor_tensor(prob[:, :, :], tmp, each(red[:, 4, :]), ALU.mult))
            dve.wait_ge(slots_ready, 1)
            then(nc.vector.tensor_tensor(ptmp[:, :, :, :].rearrange("p k t e -> p k (t e)"),
                                         pick[:, :, :, :].rearrange("p k t e -> p k (t e)"),
                                         prob[:, :, :].rearrange("p t e -> p (t e)").unsqueeze(1)
                                         .to_broadcast(both_choices), ALU.mult))
            nc.vector.tensor_tensor(gates[:, :, :], ptmp[:, 0, :, :], ptmp[:, 1, :, :], ALU.add).then_inc(picked, 1)
            nc.vector.tensor_reduce(gsel[:, :, :], ptmp[:, :, :, :], AX.X, ALU.add)
            for g, n in ((0, 4 * P), (1, ROWS[4])):
                b = take(("gt", g))
                nc.vector.tensor_copy(gT[:, 4 * P * g:4 * P * g + n], b[0:EXPERTS, 0:n]).then_inc(v_read, 1)
            for t in range(RT):
                b = take(("b2", t))
                dve.wait_ge(a_read, ANUM["hrow", t] + 1)
                rows = base[0:ROWS[t], t, :]
                nc.vector.tensor_tensor(rows, b[0:ROWS[t], 0:D], rows, ALU.add).then_inc(v_read, 1)

            def copy_rows(tile):
                nc.vector.tensor_copy(xsT[:, bass.ds(tile, 1), :, :].rearrange("p j k n -> p (j k) n"),
                                      xs_bank[:, 0:D].rearrange("p (k n) -> p k n", k=DB)).then_inc(xs_copied, 1)

            for j in range(AHEAD):
                dve.wait_ge(xs_turned, j + 1)
                copy_rows(j)
            dve.wait_ge(slots_ready, 2)
            with dve.Fori(0, EXPERTS // RING) as g:
                for u in range(RING):
                    b1 = wexp[:, u, WCOLS - HB:WCOLS]
                    first, end = tiles_of(dve, g * RING + u)
                    with dve.Fori(first, end) as j:
                        dve.wait_ge(up_b, j + 1)
                        for i in range(4):
                            r = nc.vector.tensor_scalar(hid[:, 4 + i, :], up_bank_b[:, i * P:(i + 1) * P],
                                                        b1[:, 4 + i:5 + i], 0.0, ALU.add, ALU.max)
                        r.then_inc(relu_b, 1)
                        dve.wait_ge(xs_turned, j + (AHEAD + 1))
                        copy_rows(j + AHEAD)
            for t in range(RT):
                dve.wait_ge(gathered[t][0], 16)
                rows = base[0:ROWS[t], t, :]
                then(nc.vector.scalar_tensor_tensor(out=rows, in0=got[0:ROWS[t], t, :],
                                                    scalar=gsel[0:ROWS[t], 0, t:t + 1], in1=rows,
                                                    op0=ALU.mult, op1=ALU.add))
                dve.wait_ge(gathered[t][1], 16)
                nc.vector.scalar_tensor_tensor(out=rows, in0=got2[0:ROWS[t], t, :],
                                               scalar=gsel[0:ROWS[t], 1, t:t + 1], in1=rows,
                                               op0=ALU.mult, op1=ALU.add).then_inc(final, 1)


def _constants():
    k = np.arange(D)
    angle = 2 * np.pi * ((k[:, None] * k[None, :]) % D) / D
    dft = np.stack([np.cos(angle), np.sin(angle), -np.sin(angle)]).astype(np.float32)
    inv = (1.0 / 10000.0 ** (np.arange(0, HD, 2, dtype=np.float32) / HD)).astype(np.float32)
    freq = np.arange(SEQ, dtype=np.float32)[:, None] * inv[None, :]
    feature = np.arange(P) % (HD // 2)
    second = np.arange(P) >= P // 2
    block = {}
    block["cos"] = np.cos(freq)[:, feature].T
    block["sin"] = (np.sin(freq)[:, feature] * np.where(second, -1.0, 1.0)[None, :]).T
    p = np.arange(P)
    block["headmask"] = np.stack([p % (P // 2) // (HD // 2) == e for e in range(HPB)], 1)
    block["ident"] = np.eye(P)
    block["means"] = np.full((P, P), 1.0 / D)
    block["ones"] = np.ones((P, P))
    block["tri"] = p[:, None] < p[None, :]
    q = np.arange(AW)
    seen = (q[:, None] // SEQ == q[None, :] // SEQ) & (q[None, :] <= q[:, None])
    mask = np.zeros((P, AW))
    mask[:AW] = np.where(seen, 0.0, -1e30)
    block["attmask"] = mask
    e = np.arange(EXPERTS)
    tri16 = np.zeros((P, EXPERTS + 1))
    tri16[:EXPERTS] = e[:, None] < np.arange(EXPERTS + 1)[None, :]
    block["tri16"] = tri16
    block["slots16"] = np.tile(P * tri16[:, 0:EXPERTS], (1, RT))
    block["limits"] = np.tile(np.array([-1] + [P * k for k in range(1, LIMITS)]), (P, 1))
    block["iota16"] = np.tile(e - EXPERTS, (P, 1))
    consts = np.zeros((P, NCONST), np.float32)
    for name, (at, n) in CONST.items():
        consts[:, at:at + n] = block[name]
    sel = np.zeros((SEQ + 2, HALF), np.float32)
    s = np.arange(HALF) % SEQ
    sel[s, np.arange(HALF)] = 1.0
    sel[SEQ] = s > 0
    sel[SEQ + 1] = s == 0
    return dft, consts, sel


def _rotary():
    f = np.arange(D).reshape(DB, HPB, 2, HD // 2)
    return f.transpose(0, 2, 1, 3).reshape(D)


def _blocks(w):
    return w.reshape(-1, P, w.shape[1]).transpose(1, 0, 2)


def kernel(**inputs):
    import numpy as _np
    import concourse.bacc as _bacc
    from concourse import mybir as _mybir
    from concourse.bass_utils import run_bass_kernel_spmd as _run

    g = {k: _np.asarray(v) for k, v in inputs.items()}
    dft, consts, sel = _constants()

    x = g["x"].reshape(IMAGES, 3, 6, 16, 6, 16).transpose(1, 3, 5, 0, 2, 4).reshape(PATCH, IMAGES, SEQ - 1)
    patches = _np.zeros((PATCH, IMAGES, SEQ), _np.float32)
    patches[:, :, 1:] = x
    tok_add = _np.concatenate([g["L0_tok_position_embeddings"][0], g["L0_tok_b_lin"][None],
                               g["L0_tok_class_token"][0]], 0)
    rotary = _rotary()
    wq, wk = g["L0_attn_Wq"], g["L0_attn_Wk"]
    attn_w = _np.stack([_blocks(w.T) for w in (wq[rotary], wk[rotary], g["L0_attn_Wv"])], 1)
    cw = g["L1_attn_conv_w"].reshape(IB, 2, 64, 64, TAPS)
    conv_w = _np.zeros((2, 64, IB, TAPS, 2, 64), _np.float32)
    for i in range(2):
        conv_w[i, :, :, :, i, :] = cw[:, i].transpose(2, 0, 3, 1)
    vecs = _np.concatenate([g[n].reshape(-1, P).T for n in ("L0_ffn_bias", "L1_attn_conv_b", "L1_attn_ln_g",
                                                            "L1_attn_ln_b", "L1_attn_fc_b", "L1_attn_cproj_b")], 1)
    experts = _np.concatenate([
        g["L1_ffn_W1"].reshape(EXPERTS, DB, P, HIDDEN).transpose(0, 2, 1, 3).reshape(EXPERTS, P, -1),
        g["L1_ffn_W2"].reshape(EXPERTS, HB, P, D).transpose(0, 2, 1, 3).reshape(EXPERTS, P, -1),
        g["L1_ffn_b1"].reshape(EXPERTS, HB, P).transpose(0, 2, 1)], 2)
    args = {
        "patches": _blocks(patches.reshape(PATCH, TOKENS)),
        "spec_w": _np.stack([_blocks(g["L0_ffn_w_freq_real"]), _blocks(g["L0_ffn_w_freq_imag"])], 1),
        "spec_c": _np.stack([_blocks(f) for f in dft], 1),
        "tok_w": _blocks(g["L0_tok_W_lin"].T),
        "tok_add": tok_add, "tok_sel": sel, "attn_w": attn_w, "wo_w": _blocks(g["L0_attn_Wo"].T), "consts": consts, "vecs": vecs,
        "inproj_w": _blocks(g["L1_attn_in_proj_w"].T),
        "conv_w": conv_w.reshape(P, IB, TAPS, P),
        "fc_w": _blocks(g["L1_attn_fc_w"].T),
        "cproj_w": _blocks(g["L1_attn_cproj_w"]),
        "out_w": _blocks(g["L1_attn_out_w"].T),
        "router_w": _blocks(g["L1_ffn_Wr"]),
        "router_b": g["L1_ffn_br"][None],
        "experts": experts, "b2": g["L1_ffn_b2"],
    }
    nc = _bacc.Bacc("TRN2", target_bir_lowering=False, num_devices=1)
    arrays, aps = {}, []
    for name, a in args.items():
        a = _np.ascontiguousarray(a)
        arrays[f"in_{name}"] = a
        aps.append(nc.dram_tensor(f"in_{name}", a.shape, _mybir.dt.from_np(a.dtype), kind="ExternalInput").ap())
    out = nc.dram_tensor("out_0", (TOKENS, D), _mybir.dt.float32, kind="ExternalOutput").ap()
    vit_tower_kernel(nc, *aps, out)
    r = _run(nc, [arrays], core_ids=[0])
    return r.results[0]["out_0"].reshape(IMAGES, SEQ, D)
```
